# Optimizing a Trainium2 kernel written in Bass

```python
import numpy as np
import jax
import jax.numpy as jnp

def _softmax(x, axis=-1):
    return jax.nn.softmax(x, axis=axis)

def _gelu(x):
    return jax.nn.gelu(x, approximate=True)

def _silu(x):
    return jax.nn.silu(x)

def _sigmoid(x):
    return jax.nn.sigmoid(x)

def _layernorm(x, axis=-1, eps=1e-05):
    m = jnp.mean(x, axis=axis, keepdims=True)
    v = jnp.var(x, axis=axis, keepdims=True)
    return (x - m) / jnp.sqrt(v + eps)

def _scatter_add(tgt, idx, src, axis=0):
    return tgt.at[idx].add(src)

def _segment_sum(src, seg, n):
    return jax.ops.segment_sum(src, seg, n)
kernel_name = 'mk_seq_preln_d1_jaxref_r4_49629d'

def setup_inputs(seed: int=0):
    np.random.seed(seed)
    _w = jnp.asarray

    def _L0_attn_setup():
        import jax, jax.numpy as jnp
        import numpy as np
        B, S, D, H, DFF = (4, 512, 256, 16, 1024)
        HD = D // H

        def rmsnorm(x, scale, eps=1e-06):
            var = jnp.mean(jnp.square(x), axis=-1, keepdims=True)
            return x * jax.lax.rsqrt(var + eps) * scale

        def gdn_attention(x, wq, bq, wk, bk, wv, bv, wbeta, bbeta, wo, bo):
            b, s, _ = x.shape
            q = (x @ wq + bq).reshape(b, s, H, HD)
            k = (x @ wk + bk).reshape(b, s, H, HD)
            v = (x @ wv + bv).reshape(b, s, H, HD)
            k = k / (jnp.linalg.norm(k, axis=-1, keepdims=True) + 1e-06)
            beta = jax.nn.sigmoid(x @ wbeta + bbeta)[..., None]
            q = jnp.transpose(q, (1, 0, 2, 3))
            k = jnp.transpose(k, (1, 0, 2, 3))
            v = jnp.transpose(v, (1, 0, 2, 3))
            beta = jnp.transpose(beta, (1, 0, 2, 3))

            def _step(Sm, inputs):
                q_t, k_t, v_t, beta_t = inputs
                Sk = jnp.einsum('bhde,bhe->bhd', Sm, k_t)
                delta = v_t - Sk
                Sm = Sm + beta_t[..., None] * jnp.einsum('bhd,bhe->bhde', delta, k_t)
                o_t = jnp.einsum('bhde,bhe->bhd', Sm, q_t)
                return (Sm, o_t)
            S0 = jnp.zeros((b, H, HD, HD), x.dtype)
            _, outputs = jax.lax.scan(_step, S0, (q, k, v, beta))
            outputs = jnp.transpose(outputs, (1, 0, 2, 3)).reshape(b, s, D)
            return outputs @ wo + bo
        key = jax.random.key(seed)
        ks = jax.random.split(key, 16)
        s = 1.0 / np.sqrt(D)
        inp = {'x': jax.random.normal(ks[0], (B, S, D), jnp.float32), 'wq': jax.random.normal(ks[1], (D, D), jnp.float32) * s, 'bq': jnp.zeros((D,), jnp.float32), 'wk': jax.random.normal(ks[2], (D, D), jnp.float32) * s, 'bk': jnp.zeros((D,), jnp.float32), 'wv': jax.random.normal(ks[3], (D, D), jnp.float32) * s, 'bv': jnp.zeros((D,), jnp.float32), 'wbeta': jax.random.normal(ks[4], (D, H), jnp.float32) * s, 'bbeta': jnp.zeros((H,), jnp.float32), 'wo': jax.random.normal(ks[5], (D, D), jnp.float32) * s, 'bo': jnp.zeros((D,), jnp.float32), 'w1': jax.random.normal(ks[6], (D, DFF), jnp.float32) * s, 'b1': jnp.zeros((DFF,), jnp.float32), 'w2': jax.random.normal(ks[7], (DFF, D), jnp.float32) * (1.0 / np.sqrt(DFF)), 'b2': jnp.zeros((D,), jnp.float32), 'ln1_scale': jnp.ones((D,), jnp.float32), 'ln2_scale': jnp.ones((D,), jnp.float32)}
        return inp
    _L0_attn_in = _L0_attn_setup()

    def _L0_ffn_setup():
        import jax, jax.numpy as jnp
        import numpy as np
        R = 64
        key = jax.random.key(seed)
        k1, k2, k3 = jax.random.split(key, 3)
        B, S, D_IN, D_OUT = (8, 1024, 256, 256)
        x = jax.random.normal(k1, (B, S, D_IN), dtype=jnp.float32)
        weight = jax.random.normal(k2, (D_OUT, D_IN), dtype=jnp.float32) * (1.0 / np.sqrt(D_IN))
        disha = jax.random.normal(k3, (R, D_OUT), dtype=jnp.float32) * 0.01
        return {'x': x, 'weight': weight, 'disha': disha}
    _L0_ffn_in = _L0_ffn_setup()
    _d = {'L0_attn_x': _L0_attn_in['x'], 'L0_attn_wq': _L0_attn_in['wq'], 'L0_attn_bq': _L0_attn_in['bq'], 'L0_attn_wk': _L0_attn_in['wk'], 'L0_attn_bk': _L0_attn_in['bk'], 'L0_attn_wv': _L0_attn_in['wv'], 'L0_attn_bv': _L0_attn_in['bv'], 'L0_attn_wbeta': _L0_attn_in['wbeta'], 'L0_attn_bbeta': _L0_attn_in['bbeta'], 'L0_attn_wo': _L0_attn_in['wo'], 'L0_attn_bo': _L0_attn_in['bo'], 'L0_attn_w1': _L0_attn_in['w1'], 'L0_attn_b1': _L0_attn_in['b1'], 'L0_attn_w2': _L0_attn_in['w2'], 'L0_attn_b2': _L0_attn_in['b2'], 'L0_attn_ln1_scale': _L0_attn_in['ln1_scale'], 'L0_attn_ln2_scale': _L0_attn_in['ln2_scale'], 'L0_ffn_weight': _L0_ffn_in['weight'], 'L0_ffn_disha': _L0_ffn_in['disha']}
    _x0 = _d['L0_attn_x']
    _d['L0_attn_x'] = jax.random.normal(jax.random.fold_in(jax.random.key(seed), 1), (16, 512, 256), dtype=_x0.dtype)
    del _x0
    return _d

def reference(L0_attn_x, L0_attn_wq, L0_attn_bq, L0_attn_wk, L0_attn_bk, L0_attn_wv, L0_attn_bv, L0_attn_wbeta, L0_attn_bbeta, L0_attn_wo, L0_attn_bo, L0_attn_w1, L0_attn_b1, L0_attn_w2, L0_attn_b2, L0_attn_ln1_scale, L0_attn_ln2_scale, L0_ffn_weight, L0_ffn_disha):

    def _L0_attn_ref(x, wq, bq, wk, bk, wv, bv, wbeta, bbeta, wo, bo, w1, b1, w2, b2, ln1_scale, ln2_scale):
        import jax, jax.numpy as jnp
        import numpy as np
        B, S, D, H, DFF = (4, 512, 256, 16, 1024)
        HD = D // H

        def rmsnorm(x, scale, eps=1e-06):
            var = jnp.mean(jnp.square(x), axis=-1, keepdims=True)
            return x * jax.lax.rsqrt(var + eps) * scale

        def gdn_attention(x, wq, bq, wk, bk, wv, bv, wbeta, bbeta, wo, bo):
            b, s, _ = x.shape
            q = (x @ wq + bq).reshape(b, s, H, HD)
            k = (x @ wk + bk).reshape(b, s, H, HD)
            v = (x @ wv + bv).reshape(b, s, H, HD)
            k = k / (jnp.linalg.norm(k, axis=-1, keepdims=True) + 1e-06)
            beta = jax.nn.sigmoid(x @ wbeta + bbeta)[..., None]
            q = jnp.transpose(q, (1, 0, 2, 3))
            k = jnp.transpose(k, (1, 0, 2, 3))
            v = jnp.transpose(v, (1, 0, 2, 3))
            beta = jnp.transpose(beta, (1, 0, 2, 3))

            def _step(Sm, inputs):
                q_t, k_t, v_t, beta_t = inputs
                Sk = jnp.einsum('bhde,bhe->bhd', Sm, k_t)
                delta = v_t - Sk
                Sm = Sm + beta_t[..., None] * jnp.einsum('bhd,bhe->bhde', delta, k_t)
                o_t = jnp.einsum('bhde,bhe->bhd', Sm, q_t)
                return (Sm, o_t)
            S0 = jnp.zeros((b, H, HD, HD), x.dtype)
            _, outputs = jax.lax.scan(_step, S0, (q, k, v, beta))
            outputs = jnp.transpose(outputs, (1, 0, 2, 3)).reshape(b, s, D)
            return outputs @ wo + bo
        residual = x
        h = rmsnorm(x, ln1_scale)
        h = gdn_attention(h, wq, bq, wk, bk, wv, bv, wbeta, bbeta, wo, bo)
        x = h + residual
        residual = x
        h = rmsnorm(x, ln2_scale)
        h = jax.nn.gelu(h @ w1 + b1) @ w2 + b2
        return h + residual

    def _L0_ffn_ref(x, weight, disha):
        import jax, jax.numpy as jnp
        import numpy as np
        R = 64
        result = jnp.einsum('bsd,od->bso', x, weight)
        r = disha.shape[0]
        pooled = x.reshape(*x.shape[:-1], x.shape[-1] // r, r).sum(axis=-2)
        return result + pooled @ disha
    x = L0_attn_x
    x = x + _L0_attn_ref(_layernorm(x, axis=-1), L0_attn_wq, L0_attn_bq, L0_attn_wk, L0_attn_bk, L0_attn_wv, L0_attn_bv, L0_attn_wbeta, L0_attn_bbeta, L0_attn_wo, L0_attn_bo, L0_attn_w1, L0_attn_b1, L0_attn_w2, L0_attn_b2, L0_attn_ln1_scale, L0_attn_ln2_scale)
    x = x + _L0_ffn_ref(_layernorm(x, axis=-1), L0_ffn_weight, L0_ffn_disha)
    return x

_drawn_inputs = setup_inputs


def setup_inputs(seed=0):
    import zlib

    import numpy as np

    out = dict(_drawn_inputs(seed))
    spreads = {'L0_attn_bq': (0.0, 0.1),
     'L0_attn_bk': (0.0, 0.1),
     'L0_attn_bv': (0.0, 0.1),
     'L0_attn_bbeta': (0.0, 0.311),
     'L0_attn_bo': (0.0, 0.29),
     'L0_attn_b1': (0.0, 0.432),
     'L0_attn_b2': (0.0, 0.268),
     'L0_attn_ln1_scale': (1.0, 0.2),
     'L0_attn_ln2_scale': (1.0, 0.2)}
    factors = {}
    for name, (base, spread) in spreads.items():
        noise = np.random.default_rng([zlib.crc32(name.encode()), seed]).standard_normal(out[name].shape)
        drawn = base * np.exp(spread * noise) if base else spread * noise
        out[name] = jnp.asarray(drawn.astype(out[name].dtype))
    for name, factor in factors.items():
        out[name] = (out[name] * factor).astype(out[name].dtype)
    return out
```

```python
from contextlib import ExitStack

import concourse.bass as bass
from concourse import mybir

F32 = mybir.dt.float32
F16 = mybir.dt.float16
ALU = mybir.AluOpType
ACT = mybir.ActivationFunctionType

P = 128
B, S, D, H, FF = 16, 512, 256, 16, 1024
E = D // H
C = 32
CHUNKS = S // C
G4 = 4
BG = B // G4
KT = D // P
MT = FF // P
Q4 = 4
HH = 2
UN = BG * KT * HH
LN = B * KT * HH
SEL = P // LN
Q2 = Q4 // SEL
RH = G4 // 2
HN = RH * P
EPS_LN, EPS_RMS, EPS_K = 1e-5, 1e-6, 1e-6
R64 = 64

assert LN * SEL == P and BG * C == P and Q4 * C == P


class Rota:

    def __init__(self, banks, filled, act_read, dve_read, phases, done):
        self.banks, self.sems = banks, (filled, act_read, dve_read)
        self.done = done
        self.at, self.per = {}, {}
        kinds = [list(phases.values())[-1][-1][1]] * len(banks)
        for ph, fills in phases.items():
            counts = [[0, 0, 0] for _ in banks]
            for i, (name, kind) in enumerate(fills):
                b = i % len(banks)
                self.at[name] = (ph, b, tuple(counts[b]), kinds[b], kind)
                counts[b][0] += 1
                counts[b][1] += "A" in kind
                counts[b][2] += "V" in kind
                kinds[b] = kind
            self.per[ph] = counts

    def bank(self, name):
        return self.banks[self.at[name][1]]

    def count(self, name, which, p):
        ph, b, before, _, _ = self.at[name]
        total = before[which]
        for other, times in self.done(ph, p):
            total = total + times * self.per[other][b][which]
        return total

    def on_free(self, name, p):
        _, b, _, last, _ = self.at[name]
        which = 1 if last[-1] == "A" else 2
        return self.sems[which][b], self.count(name, which, p)

    def on_filled(self, name, p):
        return self.sems[0][self.at[name][1]], self.count(name, 0, p) + 1

    def on_act(self, name, p):
        return self.sems[1][self.at[name][1]], self.count(name, 1, p) + 1

    def on_dve(self, name, p):
        return self.sems[2][self.at[name][1]], self.count(name, 2, p) + 1

    def filled(self, name):
        return self.sems[0][self.at[name][1]]

    def act_read(self, name):
        return self.sems[1][self.at[name][1]]

    def dve_read(self, name):
        return self.sems[2][self.at[name][1]]


class Steps:

    def __init__(self):
        self.n = 0

    def one(self):
        self.n += 1
        return 1


def gated_delta_block(nc, A):
    x, out = A["L0_attn_x"], A["out"]
    ctx = ExitStack()
    with ctx:
        def sb(name, shape, dt=F32):
            return ctx.enter_context(nc.sbuf_tensor(name, shape, dt))

        def sem(name):
            return ctx.enter_context(nc.semaphore(name))

        ident = sb("ident", [P, P])
        quad_col = sb("quad_col", [P, Q4])
        head_col = sb("head_col", [P, Q4, HH])
        quad_mask = sb("quad_mask", [P, Q4, E], F16)
        head_mask = sb("head_mask", [P, 2 * Q4, E], F16)
        causal = sb("causal", [P, C])
        eps_ln, eps_rms = sb("eps_ln", [P, 1]), sb("eps_rms", [P, 1])
        ln_cols = sb("ln_cols", [P, 2, KT])
        qkv_bias = sb("qkv_bias", [P, 3, KT])
        beta_bias = sb("beta_bias", [P, 1])
        b1_cols = sb("b1_cols", [P, MT])
        bo_rows, b2_rows = sb("bo_rows", [P, D]), sb("b2_rows", [P, D])
        wqkv = sb("wqkv", [P, 2, 3, KT, D], F16)
        wbeta = sb("wbeta", [P, 2, KT, P], F16)
        wo = sb("wo", [P, 2, KT, D], F16)
        w1 = sb("w1", [P, 2, KT, FF], F16)
        w2 = sb("w2", [P, 2, MT, D], F16)
        wffn = sb("wffn", [P, 2, KT, D], F16)

        xa = sb("xa", [P, G4, D])
        bn6 = sb("bn6", [P, G4, 6])
        mv = sb("mv", [P, G4, 2])
        rstd = sb("rstd", [P, G4])
        sd1, ms, sd2, rr = (sb(n, [P, G4]) for n in ("sd1", "ms", "sd2", "rr"))
        hf = sb("hf", [P, 2, KT, B * C], F16)
        kq = sb("kq", [P, 2, 2, 2, KT, B * C], F16)
        vf = sb("vf", [P, 2, KT, B * C])
        kraw = sb("kraw", [P, KT, B * C])
        ksq = sb("ksq", [P, KT, B * C])
        sdk, rnk = sb("sdk", [P, KT, G4 * 2 * Q4]), sb("rnk", [P, KT, G4 * 2 * Q4])
        kblk = sb("kblk", [P, 2, UN * P], F16)
        beta_f = sb("beta_f", [P, B * C])
        beta_t = sb("beta_t", [P, B, C])
        beta_j = sb("beta_j", [P, LN])
        ptmp = sb("ptmp", [P, KT, BG * HH, C])
        pt = sb("pt", [P, 2, 2, KT, B, HH, C], F16)
        part = C * Q2 * C
        regI = sb("regI", [P, 4 * part])
        al = regI[:, 0:part].rearrange("p (i q j) -> p i q j", i=C, q=Q2)
        tl = regI[:, part:2 * part].rearrange("p (i q m) -> p i q m", i=C, q=Q2)
        gram = regI[:, 2 * part:3 * part].rearrange("p (l i) -> p l i", i=C)
        tt = regI[:, 3 * part:4 * part].bitcast(F16).rearrange("p (z l i) -> p z l i", z=2, i=C)
        bl = sb("bl", [P, Q2, C])
        prod = sb("prod", [P, Q2 * (C // 2) ** 2])
        st = sb("st", [P, 2, LN * E // HH], F16)
        sblk = sb("sblk", [P, 2, BG * KT, P], F16)
        rf, rj = sb("rf", [P, BG * KT, C]), sb("rj", [P, BG * KT, C])
        rr16 = sb("rr16", [P, 2, 2, BG * KT, C], F16)
        uc = sb("uc", [P, 2, 2, UN * E], F16)
        kj = sb("kj", [P, 2, BG * KT, C], F16)
        tblk = sb("tblk", [P, 2, UN, Q4, C], F16)
        kjb = sb("kjb", [P, 2, HH, BG * KT, P], F16)
        ub = sb("ub", [P, 2, HH, BG * KT, P], F16)
        of = sb("of", [P, 2, G4, KT, P], F16)
        xd = sb("xd", [P, G4, D])
        rsd, nmr = sb("rsd", [P, 2, G4]), sb("nmr", [P, 2, G4])
        x1 = sb("x1", [P, G4, D])
        ssq, sdr, rdr = sb("ssq", [P, G4]), sb("sdr", [P, G4]), sb("rdr", [P, G4])
        hd = sb("hd", [P, 2, KT, B * C], F16)
        ge = sb("ge", [P, 2, 2, HN])
        gg = sb("gg", [P, 2, MT, HN], F16)
        mv2, sdy, rdy = sb("mv2", [P, G4, 2]), sb("sdy", [P, G4]), sb("rdy", [P, G4])
        bn6d = sb("bn6d", [P, G4, 6])

        ps = [ctx.enter_context(nc.psum_tensor(f"ps{i}", [P, 512], F32)) for i in range(8)]
        state, ubank, xbank = ps[0], ps[1], [ps[2], ps[3]]

        w_loaded, setup_pool, setup_act = sem("w_loaded"), sem("setup_pool"), sem("setup_act")
        setup_dve, setup_pe = sem("setup_dve"), sem("setup_pe")
        x_loaded, stats_ready, sd1_ready = sem("x_loaded"), sem("stats_ready"), sem("sd1_ready")
        ms_ready, sd2_ready, hs_ready = sem("ms_ready"), sem("sd2_ready"), sem("hs_ready")
        rn_ready, knhi_ready = sem("rn_ready"), sem("knhi_ready")
        kn_split, kblk_ready, beta_ready = sem("kn_split"), sem("kblk_ready"), sem("beta_ready")
        phi_ready, p_ready = sem("phi_ready"), sem("p_ready")
        inv_ready = sem("inv_ready")
        sh_ready, sblk_ready, ksqs_done = sem("sh_ready"), sem("sblk_ready"), sem("ksqs_done")
        rj_ready, rh_ready, r_ready = sem("rj_ready"), sem("rh_ready"), sem("r_ready")
        thi_ready, tlo_ready = sem("thi_ready"), sem("tlo_ready")
        u_filled, uh_ready, ublk_ready = sem("u_filled"), sem("uh_ready"), sem("ublk_ready")
        ds_done, o_filled, oh_ready, o_ready = sem("ds_done"), sem("o_filled"), sem("oh_ready"), sem("o_ready")
        xd_loaded, x1_ready, ssq_ready = sem("xd_loaded"), sem("x1_ready"), sem("ssq_ready")
        sdr_ready, hs1_ready = sem("sdr_ready"), sem("hs1_ready")
        gl_ready, y_stats, sdy_ready = sem("gl_ready"), sem("y_stats"), sem("sdy_ready")
        hs2_ready, out_stored, xd_free = sem("hs2_ready"), sem("out_stored"), sem("xd_free")
        dve_step, pool_step = sem("dve_step"), sem("pool_step")
        pe_passed = sem("pe_passed")
        own, pown = Steps(), Steps()

        a_fills = [("hT0", "AV"), ("hT1", "AV"), ("k0", "A"), ("k1", "A"), ("q0", "AV"), ("q1", "AV"),
                   ("ks0", "A"), ("ks1", "A"), ("v0", "A"), ("v1", "A"), ("beta", "A"), ("kr0", "V"), ("kr1", "V")]
        a_fills += [(f"G{r}{g}", "AV") for r in range(G4) for g in range(KT)]
        a_fills += [(f"LA{i}", "A") for i in range(4)] + [("LB", "A")]
        d1_fills = [("x10", "V"), ("x11", "V"), ("h10", "AV"), ("h11", "AV")] + [(f"w10{m}", "A") for m in range(4)]
        d1_fills += [("w20", "V")]
        t_fills = [(f"TF{i}", "AV") for i in range(4)]
        d2_fills = [(f"w11{m}", "A") for m in range(4)] + [("w21", "V"), ("h20", "AV"), ("h21", "AV"),
                                                           ("ff0", "V"), ("ff1", "V")]

        def rota(tag, banks, phases, done):
            return Rota(banks, *[[sem(f"{tag}{w}{i}") for i in range(len(banks))]
                                 for w in ("_filled", "_act_read", "_dve_read")], phases, done)

        def floor0(v):
            return max(v, 0) if type(v) is int else v

        def before_cd(ph, c):
            if ph == "T":
                return [("D1", c), ("T", c), ("D2", floor0(c - 1))]
            t = c + (1 if ph == "D1" else 2)
            return [("D1", c + (ph == "D2")), ("T", min(t, CHUNKS) if type(t) is int else t), ("D2", c)]

        ra = rota("a", [ps[4], ps[5]], {"A": a_fills}, lambda ph, c: [("A", c)])
        rd = rota("d", [ps[6], ps[7]], {"D1": d1_fills, "T": t_fills, "D2": d2_fills}, before_cd)

        def tokens(ap, c, b):
            return ap.rearrange("(r b) t d -> b t r d", b=BG)[b, bass.ds(c * C, C), :, :]

        def mm3(out_, lh, rh, first, last=True, skip=False):
            passes = ((0, 0), (0, 1), (1, 0))
            for n, (a, b) in enumerate(passes):
                ins = nc.tensor.matmul(out_, lh(a), rh(b), start=first and n == 0,
                                       stop=last and n == 2, skip_group_check=skip)
            return ins

        def turn64(out_, in_, hp):
            if hp.start == 0:
                return nc.tensor.transpose(out_[hp], in_, ident[hp, hp])
            return nc.tensor.matmul(out_[hp], in_, ident[hp, hp], start=True, stop=True)

        def sp_load_a(sp, c, first=False):
            if not first:
                sp.wait_ge(*ra.on_filled("hT1", c - 1))
            for b in range(BG):
                sp.dma_start(xa[b * C:(b + 1) * C, :, :], tokens(x, c, b)).then_inc(x_loaded, 16)

        def sp_load_d(sp, d):
            for b in range(BG):
                sp.dma_start(xd[b * C:(b + 1) * C, :, :], tokens(x, d, b)).then_inc(xd_loaded, 16)

        def sp_store(sp, d):
            sp.wait_ge(*rd.on_dve("ff0", d))
            sp.wait_ge(*rd.on_dve("ff1", d))
            for b in range(BG):
                sp.dma_start(tokens(out, d, b), xd[b * C:(b + 1) * C, :, :]).then_inc(out_stored, 16)
            sp.wait_ge(out_stored, d * (16 * BG) + 16 * BG)
            sp.sem_inc(xd_free, 1)

        def pe_turn(pe, a):
            for h in range(2):
                n = f"hT{h}"
                pe.wait_ge(hs_ready, a * G4 + (h + 1) * RH)
                pe.wait_ge(*ra.on_free(n, a))
                for r in range(RH):
                    for t in range(KT):
                        s = (r * KT + t) * P
                        ins = nc.tensor.transpose(ra.bank(n)[:, s:s + P],
                                                  xa[:, h * RH + r, t * P:(t + 1) * P], ident[:, :])
                ins.then_inc(ra.filled(n), 1)

        def pe_project(pe, a, w):
            wi = "kqv".index(w)
            if w == "k":
                pe.wait_ge(*ra.on_dve("hT0", a))
                pe.wait_ge(*ra.on_dve("hT1", a))
            for g in range(KT):
                n = f"{w}{g}"
                pe.wait_ge(*ra.on_free(n, a))
                for t in range(KT):
                    ins = mm3(ra.bank(n)[:, :], lambda z: wqkv[:, z, wi, t, g * P:(g + 1) * P],
                              lambda z: hf[:, z, t, :], t == 0, t == KT - 1)
                ins.then_inc(ra.filled(n), 1)

        def pe_beta(pe, a):
            pe.wait_ge(*ra.on_free("beta", a))
            for t in range(KT):
                ins = mm3(ra.bank("beta")[:, :], lambda z: wbeta[:, z, t, :], lambda z: hf[:, z, t, :],
                          t == 0, t == KT - 1)
            ins.then_inc(ra.filled("beta"), 1)

        def pe_norms(pe, a):
            for g in range(KT):
                n = f"ks{g}"
                pe.wait_ge(*ra.on_act(f"k{g}", a))
                pe.wait_ge(*ra.on_free(n, a))
                for r in range(G4):
                    ins = nc.tensor.matmul(ra.bank(n)[:, r * 8:(r + 1) * 8], ksq[:, g, r * P:(r + 1) * P],
                                           head_col[:, :, :].rearrange("p q h -> p (q h)"), start=True, stop=True)
                ins.then_inc(ra.filled(n), 1)

        def pe_norms_back(pe, a):
            for g in range(KT):
                n = f"kr{g}"
                pe.wait_ge(rn_ready, a * KT + g + 1)
                pe.wait_ge(*ra.on_free(n, a))
                for r in range(G4):
                    ins = nc.tensor.transpose(ra.bank(n)[:, r * P:(r + 1) * P], ksq[:, g, r * P:(r + 1) * P],
                                              ident[:, :])
                ins.then_inc(ra.filled(n), 1)

        def pe_gram(pe, a, k, r):
            pe.wait_ge(kblk_ready, a * G4 + r + 1)
            for g in range(KT):
                n = f"G{r}{g}"
                pe.wait_ge(*ra.on_free(n, a))
                for b in range(BG):
                    for hh in range(HH):
                        s = (b * HH + hh) * 2 * C
                        u = (hh * KT + g) * BG + b
                        t0 = (r * BG + b) * C
                        ins = mm3(ra.bank(n)[:, s:s + 2 * C], lambda z: kblk[:, z, u * P:(u + 1) * P],
                                  lambda z: kq[:, z, k, :, g, t0:t0 + C], True)
                ins.then_inc(ra.filled(n), 1)

        def pe_lanes(pe, a):
            pe.wait_ge(*ra.on_act(f"G{G4 - 1}{KT - 1}", a))
            pe.wait_ge(*ra.on_act(f"G{G4 - 1}{KT - 2}", a))
            for i8 in range(4):
                n = f"LA{i8}"
                pe.wait_ge(*ra.on_free(n, a))
                pe.sem_inc(pe_passed, 1)
                for i in range(8):
                    for s in reversed(range(SEL)):
                        hp = slice(s * LN, (s + 1) * LN)
                        ins = turn64(ra.bank(n)[:, i * R64:(i + 1) * R64], gram[hp, :, i8 * 8 + i], hp)
                ins.then_inc(ra.filled(n), 1)
            pe.wait_ge(beta_ready, a + 1)
            pe.wait_ge(*ra.on_free("LB", a))
            pe.sem_inc(pe_passed, 1)
            for s in reversed(range(SEL)):
                hp = slice(s * LN, (s + 1) * LN)
                ins = turn64(ra.bank("LB")[:, 0:R64], beta_j[hp, :], hp)
            ins.then_inc(ra.filled("LB"), 1)

        def pe_t(pe, c):
            pe.wait_ge(inv_ready, c + 1)
            for i8 in range(4):
                n = f"TF{i8}"
                pe.wait_ge(*rd.on_free(n, c))
                pe.sem_inc(pe_passed, 1)
                for i in range(8):
                    for s in reversed(range(SEL)):
                        hp = slice(s * LN, (s + 1) * LN)
                        ins = turn64(rd.bank(n)[:, i * LN:(i + 1) * LN],
                                     tl[hp, i8 * 8 + i, :, :].rearrange("p q m -> p (q m)"), hp)
                ins.then_inc(rd.filled(n), 1)

        def pe_ksqs(pe, c, k, r):
            pe.wait_ge(sblk_ready, c * G4 + r + 1)
            pe.wait_ge(o_ready, floor0(c * G4 + r - 1))
            for b in range(BG):
                for g in range(KT):
                    u = b * KT + g
                    t0 = (r * BG + b) * C
                    ins = mm3(xbank[r % 2][:, u * 2 * C:(u + 1) * 2 * C], lambda z: sblk[:, z, u, :],
                              lambda z: kq[:, z, k, :, g, t0:t0 + C], u == 0, u == BG * KT - 1, True)
            ins.then_inc(ksqs_done, 1)

        def pe_u(pe, c, r):
            pe.wait_ge(thi_ready, c * G4 + r + 1)
            pe.wait_ge(tlo_ready, c * G4 + r + 1)
            pe.wait_ge(r_ready, c * G4 + r + 1)
            pe.wait_ge(ublk_ready, c * G4 + r)
            for b in range(BG):
                for g in range(KT):
                    for hh in range(HH):
                        u = (b * KT + g) * HH + hh
                        ins = mm3(ubank[:, u * E:(u + 1) * E],
                                  lambda z: tblk[:, z, u, :, :].rearrange("p q i -> p (q i)"),
                                  lambda z: rr16[:, z, r % 2, b * KT + g, hh * E:(hh + 1) * E], True)
            ins.then_inc(u_filled, 1)

        def pe_s_and_o(pe, c, k, r):
            pe.wait_ge(ublk_ready, c * G4 + r + 1)
            pe.wait_ge(p_ready, c * G4 + r + 1)
            for b in range(BG):
                for g in range(KT):
                    for hh in range(HH):
                        u = (b * KT + g) * HH + hh
                        s = ((r * BG + b) * KT + g) * E
                        ins = mm3(state[:, s:s + E], lambda z: kjb[:, z, hh, g * BG + b, :],
                                  lambda z: uc[:, z, r % 2, u * E:(u + 1) * E], False, True, True)
            ins.then_inc(ds_done, 1)
            for b in range(BG):
                for g in range(KT):
                    for hh in range(HH):
                        s = (b * KT + g) * 2 * C + C
                        ins = mm3(xbank[r % 2][:, s:s + C], lambda z: ub[:, z, hh, b * KT + g, :],
                                  lambda z: pt[:, z, k, g, r * BG + b, hh, :], False, True, True)
            ins.then_inc(o_filled, 1)

        def pe_out_proj(pe, d):
            for h in range(2):
                n = f"x1{h}"
                pe.wait_ge(o_ready, d * G4 + (h + 1) * RH)
                pe.wait_ge(*rd.on_free(n, d))
                for r in range(RH):
                    for t in range(KT):
                        ins = mm3(rd.bank(n)[:, r * D:(r + 1) * D], lambda z: of[:, z, h * RH + r, t, :],
                                  lambda z: wo[:, z, t, :], t == 0, t == KT - 1)
                ins.then_inc(rd.filled(n), 1)

        def pe_turn_d(pe, d, tag, ready):
            for h in range(2):
                n = f"{tag}{h}"
                pe.wait_ge(ready, d * G4 + (h + 1) * RH)
                pe.wait_ge(*rd.on_free(n, d))
                for r in range(RH):
                    for t in range(KT):
                        s = (r * KT + t) * P
                        ins = nc.tensor.transpose(rd.bank(n)[:, s:s + P], x1[:, h * RH + r, t * P:(t + 1) * P],
                                                  ident[:, :])
                ins.then_inc(rd.filled(n), 1)

        def pe_w1(pe, d, h):
            pe.wait_ge(*rd.on_dve(f"h1{h}", d))
            for m2 in range(4):
                n = f"w1{h}{m2}"
                pe.wait_ge(*rd.on_free(n, d))
                for j in range(2):
                    m = m2 * 2 + j
                    for t in range(KT):
                        ins = mm3(rd.bank(n)[:, j * HN:(j + 1) * HN], lambda z: w1[:, z, t, m * P:(m + 1) * P],
                                  lambda z: hd[:, z, t, h * HN:(h + 1) * HN], t == 0, t == KT - 1)
                ins.then_inc(rd.filled(n), 1)

        def pe_w2(pe, d, h):
            n = f"w2{h}"
            pe.wait_ge(*rd.on_free(n, d))
            pe.wait_ge(gl_ready, d * MT + (h + 1) * 4)
            for r in range(RH):
                for m in range(MT):
                    ins = mm3(rd.bank(n)[:, r * D:(r + 1) * D], lambda z: gg[:, z, m, r * P:(r + 1) * P],
                              lambda z: w2[:, z, m, :], m == 0, m == MT - 1)
            ins.then_inc(rd.filled(n), 1)

        def pe_ffn(pe, d):
            for h in range(2):
                n = f"ff{h}"
                pe.wait_ge(*rd.on_dve(f"h2{h}", d))
                pe.wait_ge(*rd.on_free(n, d))
                for r in range(RH):
                    s = (h * RH + r) * P
                    for t in range(KT):
                        ins = mm3(rd.bank(n)[:, r * D:(r + 1) * D], lambda z: hd[:, z, t, s:s + P],
                                  lambda z: wffn[:, z, t, :], t == 0, t == KT - 1)
                ins.then_inc(rd.filled(n), 1)

        def pe_chunk(pe, c, k, a=True, d=True):
            if a:
                pe_turn(pe, c + 1)
                pe_project(pe, c + 1, "k")
                pe_project(pe, c + 1, "q")
            if d:
                pe_out_proj(pe, c - 1)
            if a:
                pe_norms(pe, c + 1)
                pe_project(pe, c + 1, "v")
                pe_beta(pe, c + 1)
            if d:
                pe_turn_d(pe, c - 1, "h1", hs1_ready)
            if a:
                pe_norms_back(pe, c + 1)
            if d:
                pe_w1(pe, c - 1, 0)
            if a:
                pe_gram(pe, c + 1, 1 - k, 0)
            if d:
                pe_w2(pe, c - 1, 0)
            if a:
                pe_gram(pe, c + 1, 1 - k, 1)
            pe_t(pe, c)
            pe_ksqs(pe, c, k, 0)
            if a:
                pe_gram(pe, c + 1, 1 - k, 2)
            pe_u(pe, c, 0)
            if a:
                pe_gram(pe, c + 1, 1 - k, 3)
            pe_s_and_o(pe, c, k, 0)
            pe_ksqs(pe, c, k, 1)
            if a:
                pe_lanes(pe, c + 1)
            pe_u(pe, c, 1)
            pe_s_and_o(pe, c, k, 1)
            pe_ksqs(pe, c, k, 2)
            if d:
                pe_w1(pe, c - 1, 1)
            pe_u(pe, c, 2)
            if d:
                pe_w2(pe, c - 1, 1)
            pe_s_and_o(pe, c, k, 2)
            pe_ksqs(pe, c, k, 3)
            if d:
                pe_turn_d(pe, c - 1, "h2", hs2_ready)
            pe_u(pe, c, 3)
            if d:
                pe_ffn(pe, c - 1)
            pe_s_and_o(pe, c, k, 3)

        def row_halves(bank):
            return bank[:, :].rearrange("p (r t n) -> p t r n", r=RH, t=KT)

        def col_halves(tile, z, h):
            return tile[:, z, :, h * HN:(h + 1) * HN].rearrange("p t (r n) -> p t r n", r=RH)

        def act_norm(act, a):
            act.wait_ge(stats_ready, a + 1)
            nc.scalar.activation(sd1[:, :], mv[:, :, 1], ACT.Sqrt, bias=eps_ln[:, 0:1]).then_inc(sd1_ready, 1)
            act.wait_ge(ms_ready, a + 1)
            nc.scalar.activation(sd2[:, :], ms[:, :], ACT.Sqrt).then_inc(sd2_ready, 1)

        def act_turned(act, a):
            for h in range(2):
                n = f"hT{h}"
                act.wait_ge(*ra.on_filled(n, a))
                nc.scalar.activation(col_halves(hf, 0, h), row_halves(ra.bank(n)),
                                     ACT.Copy).then_inc(ra.act_read(n), 1)

        def act_keys(act, a):
            act.wait_ge(kn_split, a)
            for g in range(KT):
                n = f"k{g}"
                bias = qkv_bias[:, 0, g:g + 1]
                act.wait_ge(*ra.on_filled(n, a))
                nc.scalar.activation(kraw[:, g, :], ra.bank(n)[:, :], ACT.Identity, bias=bias)
                nc.scalar.activation(ksq[:, g, :], ra.bank(n)[:, :], ACT.Square,
                                     bias=bias).then_inc(ra.act_read(n), 1)

        def act_queries(act, a, k):
            for g in range(KT):
                n = f"q{g}"
                act.wait_ge(*ra.on_filled(n, a))
                nc.scalar.activation(kq[:, 0, k, 1, g, :], ra.bank(n)[:, :], ACT.Identity,
                                     bias=qkv_bias[:, 1, g:g + 1]).then_inc(ra.act_read(n), 1)

        def act_norms(act, a):
            for g in range(KT):
                n = f"ks{g}"
                act.wait_ge(*ra.on_filled(n, a))
                nc.scalar.activation(sdk[:, g, :], ra.bank(n)[:, 0:G4 * 8], ACT.Sqrt).then_inc(ra.act_read(n), 1)

        def act_values(act, a, k):
            for g in range(KT):
                n = f"v{g}"
                act.wait_ge(*ra.on_filled(n, a))
                nc.scalar.activation(vf[:, k, g, :], ra.bank(n)[:, :], ACT.Identity,
                                     bias=qkv_bias[:, 2, g:g + 1]).then_inc(ra.act_read(n), 1)

        def act_beta(act, a):
            act.wait_ge(*ra.on_filled("beta", a))
            act.wait_ge(beta_ready, a)
            nc.scalar.activation(beta_f[:, :], ra.bank("beta")[:, :], ACT.Tanh, bias=beta_bias[:, 0:1],
                                 scale=0.5).then_inc(ra.act_read("beta"), 1)

        def act_keys_high(act, a, k):
            for g in range(KT):
                act.wait_ge(*ra.on_dve(f"kr{g}", a))
                nc.scalar.activation(kq[:, 0, k, 0, g, :], kraw[:, g, :], ACT.Copy).then_inc(knhi_ready, 1)

        def act_gram(act, a, k, r):
            for g in range(KT):
                n = f"G{r}{g}"
                act.wait_ge(*ra.on_filled(n, a))
                src = ra.bank(n)[:, :].rearrange("p (b h s) -> p b h s", b=BG, h=HH)[:, :, :, 0:C]
                dst = gram.rearrange("p (b g h) i -> p b g h i", b=B, g=KT)
                nc.scalar.activation(dst[:, r * BG:(r + 1) * BG, g, :, :], src,
                                     ACT.Copy).then_inc(ra.act_read(n), 1)
            act.wait_ge(*ra.on_dve(f"G{r}0", a))
            act.wait_ge(*ra.on_dve(f"G{r}1", a))
            nc.scalar.activation(p_part(0, k, r), ptmp[:, :, :, :], ACT.Copy).then_inc(phi_ready, 1)

        def p_part(z, k, r):
            return pt[:, z, k, :, r * BG:(r + 1) * BG, :, :].rearrange("p g b h i -> p g (b h) i")

        def act_lanes(act, a):
            for i8 in range(4):
                n = f"LA{i8}"
                act.wait_ge(*ra.on_filled(n, a))
                nc.scalar.activation(al[:, i8 * 8:i8 * 8 + 8, :, :].rearrange("p i q j -> p (i q j)"),
                                     ra.bank(n)[:, :], ACT.Copy).then_inc(ra.act_read(n), 1)
            act.wait_ge(*ra.on_filled("LB", a))
            nc.scalar.activation(bl[:, :, :].rearrange("p q j -> p (q j)"), ra.bank("LB")[:, 0:R64],
                                 ACT.Copy).then_inc(ra.act_read("LB"), 1)

        def act_state(act, c):
            act.wait_ge(ds_done, c * G4)
            nc.scalar.activation(st[:, 0, :], state[:, :], ACT.Copy).then_inc(sh_ready, 1)

        def act_t(act, c):
            for i8 in range(4):
                n = f"TF{i8}"
                act.wait_ge(*rd.on_filled(n, c))
                nc.scalar.activation(tt[:, 0, :, i8 * 8:i8 * 8 + 8].rearrange("p l i -> p i l"),
                                     rd.bank(n)[:, :].rearrange("p (i l) -> p i l", i=8),
                                     ACT.Copy).then_inc(rd.act_read(n), 1)

        def act_t_blocks(act, c, r):
            act.wait_ge(u_filled, c * G4 + r)
            if r == 0:
                act.wait_ge(*rd.on_act("TF3", c))
            for q in range(Q4):
                ins = nc.scalar.activation(tblk[:, 0, :, q, :], tt[:, 0, r * UN:(r + 1) * UN, :], ACT.Copy,
                                           scale=quad_col[:, q:q + 1])
            ins.then_inc(thi_ready, 1)

        def act_r(act, c, r):
            act.wait_ge(rj_ready, c * G4 + r + 1)
            nc.scalar.activation(rr16[:, 0, r % 2, :, :], rj[:, :, :], ACT.Copy).then_inc(rh_ready, 1)

        def act_u(act, c, r):
            act.wait_ge(u_filled, c * G4 + r + 1)
            nc.scalar.activation(uc[:, 0, r % 2, :], ubank[:, 0:UN * E], ACT.Copy).then_inc(uh_ready, 1)

        def act_o(act, c, r, d):
            act.wait_ge(o_filled, c * G4 + r + 1)
            if d:
                act.wait_ge(*rd.on_filled(f"x1{r // RH}", c - 1))
            src = xbank[r % 2][:, :].rearrange("p (b g s) -> p g b s", b=BG, g=KT)[:, :, :, C:2 * C]
            dst = of[:, 0, r, :, :].rearrange("p g (b t) -> p g b t", b=BG)
            nc.scalar.activation(dst, src, ACT.Copy).then_inc(oh_ready, 1)

        def act_squares(act, d):
            for r in range(G4):
                act.wait_ge(x1_ready, d * G4 + r + 1)
                nc.scalar.activation(ge[:, r // 2, r % 2, :], x1[:, r, :], ACT.Square,
                                     accum_out=ssq[:, r:r + 1]).then_inc(ssq_ready, 1)
            act.wait_ge(ssq_ready, (d + 1) * G4)
            nc.scalar.activation(sdr[:, :], ssq[:, :], ACT.Sqrt, bias=eps_rms[:, 0:1],
                                 scale=1.0 / D).then_inc(sdr_ready, 1)

        def act_turned_d(act, d, tag):
            for h in range(2):
                n = f"{tag}{h}"
                act.wait_ge(*rd.on_filled(n, d))
                nc.scalar.activation(col_halves(hd, 0, h), row_halves(rd.bank(n)),
                                     ACT.Copy).then_inc(rd.act_read(n), 1)

        def act_gelu(act, d, h):
            for m2 in range(4):
                n = f"w1{h}{m2}"
                act.wait_ge(*rd.on_filled(n, d))
                if h or m2 >= 2:
                    act.wait_ge(gl_ready, d * MT + h * 4 + m2 - 1)
                for j in range(2):
                    m = m2 * 2 + j
                    nc.scalar.activation(ge[:, m2 % 2, j, :], rd.bank(n)[:, j * HN:(j + 1) * HN],
                                         ACT.Gelu_apprx_tanh, bias=b1_cols[:, m:m + 1])
                    ins = nc.scalar.activation(gg[:, 0, m, :], rd.bank(n)[:, j * HN:(j + 1) * HN],
                                               ACT.Gelu_apprx_tanh, bias=b1_cols[:, m:m + 1])
                ins.then_inc(rd.act_read(n), 1)

        def act_norm_y(act, d):
            act.wait_ge(y_stats, d + 1)
            nc.scalar.activation(sdy[:, :], mv2[:, :, 1], ACT.Sqrt, bias=eps_ln[:, 0:1]).then_inc(sdy_ready, 1)

        def act_chunk(act, c, k, a=True, d=True):
            if a:
                act_norm(act, c + 1)
            act_state(act, c)
            if a:
                act_turned(act, c + 1)
                act_keys(act, c + 1)
                act_queries(act, c + 1, 1 - k)
                act_norms(act, c + 1)
            if d:
                act_squares(act, c - 1)
            if a:
                act_values(act, c + 1, 1 - k)
                act_beta(act, c + 1)
            if d:
                act_turned_d(act, c - 1, "h1")
            if a:
                act_keys_high(act, c + 1, 1 - k)
            if d:
                act_gelu(act, c - 1, 0)
            if a:
                act_gram(act, c + 1, 1 - k, 0)
                act_gram(act, c + 1, 1 - k, 1)
            act_t(act, c)
            act_t_blocks(act, c, 0)
            act_r(act, c, 0)
            if a:
                act_gram(act, c + 1, 1 - k, 2)
            act_u(act, c, 0)
            if a:
                act_gram(act, c + 1, 1 - k, 3)
            act_t_blocks(act, c, 1)
            act_o(act, c, 0, d)
            act_r(act, c, 1)
            if a:
                act_lanes(act, c + 1)
            act_u(act, c, 1)
            act_t_blocks(act, c, 2)
            act_o(act, c, 1, d)
            act_r(act, c, 2)
            if d:
                act_gelu(act, c - 1, 1)
            act_u(act, c, 2)
            act_t_blocks(act, c, 3)
            if d:
                act_norm_y(act, c - 1)
            act_o(act, c, 2, d)
            act_r(act, c, 3)
            if d:
                act_turned_d(act, c - 1, "h2")
            act_u(act, c, 3)
            act_o(act, c, 3, d)

        V = nc.vector

        def dve_keep_norm(dve, k):
            V.tensor_copy(rsd[:, k, :], rstd[:, :])
            V.scalar_tensor_tensor(out=nmr[:, k, :], in0=mv[:, :, 0], scalar=-1.0, in1=rstd[:, :],
                                   op0=ALU.mult, op1=ALU.mult).then_inc(dve_step, own.one())
            dve.wait_ge(dve_step, own.n)

        def dve_norm(dve, a):
            dve.wait_ge(x_loaded, a * (16 * BG) + 16 * BG)
            for r in range(G4):
                V.bn_stats(bn6[:, r, :], xa[:, r, :]).then_inc(dve_step, own.one())
            dve.wait_ge(dve_step, own.n)
            for r in range(G4):
                ins = V.bn_aggr(mv[:, r, :], bn6[:, r, :])
            ins.then_inc(stats_ready, 1)
            dve.wait_ge(sd1_ready, a + 1)
            V.reciprocal(rstd[:, :], sd1[:, :]).then_inc(dve_step, own.one())
            dve.wait_ge(dve_step, own.n)
            V.tensor_tensor(ms[:, :], mv[:, :, 1], rstd[:, :], ALU.mult).then_inc(dve_step, own.one())
            dve.wait_ge(dve_step, own.n)
            V.tensor_tensor(ms[:, :], ms[:, :], rstd[:, :], ALU.mult).then_inc(dve_step, own.one())
            dve.wait_ge(dve_step, own.n)
            V.tensor_scalar(ms[:, :], ms[:, :], EPS_RMS, None, ALU.add).then_inc(ms_ready, 1)
            dve.wait_ge(sd2_ready, a + 1)
            V.reciprocal(rr[:, :], sd2[:, :]).then_inc(dve_step, own.one())
            dve.wait_ge(dve_step, own.n)
            V.tensor_tensor(rr[:, :], rr[:, :], rstd[:, :], ALU.mult).then_inc(dve_step, own.one())
            dve.wait_ge(dve_step, own.n)
            for r in range(G4):
                V.tensor_scalar(xa[:, r, :], xa[:, r, :], mv[:, r, 0:1], rr[:, r:r + 1],
                                ALU.subtract, ALU.mult).then_inc(hs_ready, 1)

        def dve_turned(dve, a):
            for h in range(2):
                n = f"hT{h}"
                dve.wait_ge(*ra.on_act(n, a))
                V.tensor_tensor(col_halves(hf, 1, h), row_halves(ra.bank(n)), col_halves(hf, 0, h),
                                ALU.subtract).then_inc(ra.dve_read(n), 1)

        def dve_queries(dve, a, k):
            for g in range(KT):
                n = f"q{g}"
                dve.wait_ge(*ra.on_act(n, a))
                V.scalar_tensor_tensor(out=kq[:, 1, k, 1, g, :], in0=ra.bank(n)[:, :],
                                       scalar=qkv_bias[:, 1, g:g + 1], in1=kq[:, 0, k, 1, g, :],
                                       op0=ALU.add, op1=ALU.subtract).then_inc(ra.dve_read(n), 1)

        def dve_norms(dve, a):
            for g in range(KT):
                dve.wait_ge(*ra.on_act(f"ks{g}", a))
            V.tensor_scalar(sdk[:, :, :], sdk[:, :, :], EPS_K, None, ALU.add).then_inc(dve_step, own.one())
            dve.wait_ge(dve_step, own.n)
            V.reciprocal(rnk[:, :, :], sdk[:, :, :]).then_inc(dve_step, own.one())
            dve.wait_ge(dve_step, own.n)
            for g in range(KT):
                dst = ksq[:, g, :].rearrange("p (h e) -> p h e", e=E)
                V.tensor_copy(dst, rnk[:, g, :].unsqueeze(2).to_broadcast([P, G4 * 8, E])).then_inc(rn_ready, 1)

        def dve_beta(dve, a):
            dve.wait_ge(*ra.on_act("beta", a))
            V.tensor_scalar(beta_f[:, :], beta_f[:, :], 0.5, 0.5, ALU.mult, ALU.add).then_inc(dve_step, own.one())
            dve.wait_ge(dve_step, own.n)
            V.transpose(beta_t[:, :, :].rearrange("p b t -> p (b t)"), beta_f[:, :]).then_inc(dve_step, own.one())
            dve.wait_ge(dve_step, own.n)
            V.tensor_copy(beta_j[:, :].rearrange("p (b g) -> p b g", g=KT * HH),
                          beta_t[:, :, 0:KT * HH]).then_inc(beta_ready, 1)

        def dve_keys(dve, a):
            for g in range(KT):
                n = f"kr{g}"
                dve.wait_ge(*ra.on_filled(n, a))
                V.tensor_tensor(kraw[:, g, :], kraw[:, g, :], ra.bank(n)[:, :], ALU.mult).then_inc(ra.dve_read(n), 1)

        def dve_keys_low(dve, a, k):
            dve.wait_ge(knhi_ready, a * KT + KT)
            V.tensor_tensor(kq[:, 1, k, 0, :, :], kraw[:, :, :], kq[:, 0, k, 0, :, :],
                            ALU.subtract).then_inc(kn_split, 1)
            dve.wait_ge(kn_split, a + 1)

        def dve_key_blocks(dve, a, k, r, first=False):
            if not (first and r == 0):
                dve.wait_ge(*ra.on_filled(f"G{(r - 1) % G4}1", a if r else a - 1))
            for z in range(2):
                dst = kblk[:, z, :].rearrange("p (h g b q t) -> p h g b q t", h=HH, g=KT, b=BG, q=Q4)
                src = kq[:, z, k, 0, :, r * P:(r + 1) * P].rearrange("p g (b t) -> p g b t", b=BG)
                for hh in range(HH):
                    for q in range(Q4):
                        ins = V.tensor_scalar(dst[:, hh, :, :, q, :], src, head_col[:, q, hh:hh + 1],
                                              None, ALU.mult)
            ins.then_inc(kblk_ready, 1)

        def dve_p_mask(dve, a, r):
            dve.wait_ge(p_ready, a * G4 + r)
            for g in range(KT):
                n = f"G{r}{g}"
                dve.wait_ge(*ra.on_act(n, a))
                src = ra.bank(n)[:, :].rearrange("p (u s) -> p u s", s=2 * C)[:, :, C:2 * C]
                V.tensor_tensor(ptmp[:, g, :, :], src, causal[:, :].unsqueeze(1).to_broadcast([P, BG * HH, C]),
                                ALU.mult).then_inc(ra.dve_read(n), 1)

        def dve_p_low(dve, a, k, r):
            dve.wait_ge(phi_ready, a * G4 + r + 1)
            V.tensor_tensor(p_part(1, k, r), ptmp[:, :, :, :], p_part(0, k, r), ALU.subtract).then_inc(p_ready, 1)

        def dve_state(dve, c):
            dve.wait_ge(sh_ready, c + 1)
            V.tensor_tensor(st[:, 1, :], state[:, :], st[:, 0, :], ALU.subtract).then_inc(dve_step, own.one())
            dve.wait_ge(dve_step, own.n)

        def dve_s_blocks(dve, c, r):
            dve.wait_ge(ksqs_done, c * G4 + r)
            for z in range(2):
                src = st[:, z, r * P:(r + 1) * P].rearrange("p (u d) -> p u d", d=E)
                ins = V.tensor_tensor(sblk[:, z, :, :].rearrange("p u (h d) -> p u h d", d=E),
                                      src.unsqueeze(2).to_broadcast([P, BG * KT, 2 * Q4, E]),
                                      head_mask[:, :, :].unsqueeze(1).to_broadcast([P, BG * KT, 2 * Q4, E]),
                                      ALU.mult)
            ins.then_inc(sblk_ready, 1)

        def dve_t(dve, c):
            for i8 in range(4):
                n = f"TF{i8}"
                dve.wait_ge(*rd.on_act(n, c))
                i8s = slice(i8 * 8, i8 * 8 + 8)
                V.tensor_tensor(tt[:, 1, :, i8s].rearrange("p l i -> p i l"),
                                rd.bank(n)[:, :].rearrange("p (i l) -> p i l", i=8),
                                tt[:, 0, :, i8s].rearrange("p l i -> p i l"), ALU.subtract).then_inc(rd.dve_read(n), 1)
            dve.wait_ge(*rd.on_dve("TF2", c))
            dve.wait_ge(*rd.on_dve("TF3", c))

        def dve_t_blocks(dve, c, r):
            dve.wait_ge(u_filled, c * G4 + r)
            for q in range(Q4):
                ins = V.tensor_scalar(tblk[:, 1, :, q, :], tt[:, 1, r * UN:(r + 1) * UN, :], quad_col[:, q:q + 1],
                                      None, ALU.mult)
            ins.then_inc(tlo_ready, 1)

        def dve_r(dve, c, k, r):
            dve.wait_ge(ksqs_done, c * G4 + r + 1)
            src = xbank[r % 2][:, :].rearrange("p (b g s) -> p b g s", b=BG, g=KT)[:, :, :, 0:C]
            val = vf[:, k, :, r * P:(r + 1) * P].rearrange("p g (b t) -> p b g t", b=BG)
            V.tensor_tensor(rf[:, :, :].rearrange("p (b g) t -> p b g t", b=BG), val, src,
                            ALU.subtract).then_inc(dve_step, own.one())
            dve.wait_ge(dve_step, own.n)
            V.transpose(rj[:, :, :].rearrange("p u t -> p (u t)"),
                        rf[:, :, :].rearrange("p u t -> p (u t)")).then_inc(rj_ready, 1)

        def dve_r_low(dve, c, r):
            dve.wait_ge(rh_ready, c * G4 + r + 1)
            V.tensor_tensor(rr16[:, 1, r % 2, :, :], rj[:, :, :], rr16[:, 0, r % 2, :, :],
                            ALU.subtract).then_inc(r_ready, 1)

        def dve_kj(dve, c, k, r):
            dve.wait_ge(ds_done, c * G4 + r)
            for z in range(2):
                V.transpose(kj[:, z, :, :].rearrange("p (g b) t -> p g (b t)", g=KT),
                            kq[:, z, k, 0, :, r * P:(r + 1) * P]).then_inc(dve_step, own.one())
            dve.wait_ge(dve_step, own.n)
            for z in range(2):
                for hh in range(HH):
                    dst = kjb[:, z, hh, :, :].rearrange("p u (q h e) -> p u q h e", q=Q4, h=HH)[:, :, :, hh, :]
                    src = kj[:, z, :, hh * E:(hh + 1) * E]
                    V.tensor_tensor(dst, src.unsqueeze(2).to_broadcast([P, BG * KT, Q4, E]),
                                    quad_mask[:, :, :].unsqueeze(1).to_broadcast([P, BG * KT, Q4, E]), ALU.mult)

        def dve_u(dve, c, r):
            dve.wait_ge(uh_ready, c * G4 + r + 1)
            V.tensor_tensor(uc[:, 1, r % 2, :], ubank[:, 0:UN * E], uc[:, 0, r % 2, :],
                            ALU.subtract).then_inc(dve_step, own.one())
            dve.wait_ge(o_filled, c * G4 + r)
            for z in range(2):
                if z:
                    dve.wait_ge(dve_step, own.n)
                for hh in range(HH):
                    dst = ub[:, z, hh, :, :].rearrange("p u (q h e) -> p u q h e", q=Q4, h=HH)[:, :, :, hh, :]
                    src = uc[:, z, r % 2, :].rearrange("p (u h d) -> p u h d", h=HH, d=E)[:, :, hh, :]
                    ins = V.tensor_tensor(dst, src.unsqueeze(2).to_broadcast([P, BG * KT, Q4, E]),
                                          quad_mask[:, :, :].unsqueeze(1).to_broadcast([P, BG * KT, Q4, E]),
                                          ALU.mult)
            ins.then_inc(ublk_ready, 1)

        def dve_o(dve, c, r):
            dve.wait_ge(oh_ready, c * G4 + r + 1)
            src = xbank[r % 2][:, :].rearrange("p (b g s) -> p g b s", b=BG, g=KT)[:, :, :, C:2 * C]
            dst = of[:, :, r, :, :].rearrange("p z g (b t) -> p z g b t", b=BG)
            V.tensor_tensor(dst[:, 1], src, dst[:, 0], ALU.subtract).then_inc(o_ready, 1)

        def dve_x1(dve, d, k):
            dve.wait_ge(xd_loaded, d * (16 * BG) + 16 * BG)
            for h in range(2):
                n = f"x1{h}"
                dve.wait_ge(*rd.on_filled(n, d))
                for r in range(h * RH, (h + 1) * RH):
                    ins = V.scalar_tensor_tensor(out=x1[:, r, :], in0=xd[:, r, :], scalar=rsd[:, k, r:r + 1],
                                                 in1=rd.bank(n)[:, (r % RH) * D:(r % RH + 1) * D],
                                                 op0=ALU.mult, op1=ALU.add)
                ins.then_inc(rd.dve_read(n), 1)
                dve.wait_ge(*rd.on_dve(n, d))
                for r in range(h * RH, (h + 1) * RH):
                    V.scalar_tensor_tensor(out=x1[:, r, :], in0=x1[:, r, :], scalar=nmr[:, k, r:r + 1],
                                           in1=bo_rows[:, :], op0=ALU.add, op1=ALU.add).then_inc(x1_ready, 1)

        def dve_rms(dve, d):
            dve.wait_ge(sdr_ready, d + 1)
            V.reciprocal(rdr[:, :], sdr[:, :]).then_inc(dve_step, own.one())
            V.tensor_tensor(xd[:, :, :], xd[:, :, :], x1[:, :, :], ALU.add).then_inc(dve_step, own.one())
            dve.wait_ge(dve_step, own.n)
            for r in range(G4):
                V.tensor_scalar(x1[:, r, :], x1[:, r, :], rdr[:, r:r + 1], None, ALU.mult).then_inc(hs1_ready, 1)
            V.tensor_tensor(xd[:, :, :], xd[:, :, :], b2_rows[:, :].unsqueeze(1).to_broadcast([P, G4, D]),
                            ALU.add).then_inc(dve_step, own.one())
            dve.wait_ge(dve_step, own.n)

        def dve_turned_d(dve, d, tag):
            for h in range(2):
                n = f"{tag}{h}"
                dve.wait_ge(*rd.on_act(n, d))
                V.tensor_tensor(col_halves(hd, 1, h), row_halves(rd.bank(n)), col_halves(hd, 0, h),
                                ALU.subtract).then_inc(rd.dve_read(n), 1)

        def dve_gelu(dve, d, h):
            for m2 in range(4):
                dve.wait_ge(*rd.on_act(f"w1{h}{m2}", d))
                ms2 = slice(m2 * 2, m2 * 2 + 2)
                V.tensor_tensor(gg[:, 1, ms2, :], ge[:, m2 % 2, :, :], gg[:, 0, ms2, :],
                                ALU.subtract).then_inc(gl_ready, 1)

        def dve_y(dve, d, h):
            n = f"w2{h}"
            dve.wait_ge(*rd.on_filled(n, d))
            rs = slice(h * RH, (h + 1) * RH)
            V.tensor_tensor(xd[:, rs, :], rd.bank(n)[:, :].rearrange("p (r d) -> p r d", r=RH), xd[:, rs, :],
                            ALU.add).then_inc(rd.dve_read(n), 1)
            dve.wait_ge(*rd.on_dve(n, d))
            for r in range(h * RH, (h + 1) * RH):
                V.bn_stats(bn6d[:, r, :], xd[:, r, :]).then_inc(dve_step, own.one())

        def dve_y_stats(dve, d):
            dve.wait_ge(dve_step, own.n)
            for r in range(G4):
                ins = V.bn_aggr(mv2[:, r, :], bn6d[:, r, :])
            ins.then_inc(y_stats, 1)

        def dve_y_norm(dve, d):
            dve.wait_ge(sdy_ready, d + 1)
            V.reciprocal(rdy[:, :], sdy[:, :]).then_inc(dve_step, own.one())
            dve.wait_ge(dve_step, own.n)
            for r in range(G4):
                V.tensor_scalar(x1[:, r, :], xd[:, r, :], mv2[:, r, 0:1], rdy[:, r:r + 1],
                                ALU.subtract, ALU.mult).then_inc(hs2_ready, 1)

        def dve_out(dve, d):
            for h in range(2):
                n = f"ff{h}"
                dve.wait_ge(*rd.on_filled(n, d))
                rs = slice(h * RH, (h + 1) * RH)
                V.tensor_tensor(xd[:, rs, :], rd.bank(n)[:, :].rearrange("p (r d) -> p r d", r=RH), xd[:, rs, :],
                                ALU.add).then_inc(rd.dve_read(n), 1)

        def dve_a(dve, a, k, first=False):
            dve_norm(dve, a)
            dve_turned(dve, a)
            dve_queries(dve, a, k)
            dve_norms(dve, a)
            dve_beta(dve, a)
            dve_keys(dve, a)
            dve_keys_low(dve, a, k)
            for r in range(G4):
                dve_key_blocks(dve, a, k, r, first)
                dve_p_mask(dve, a, r)
                dve_p_low(dve, a, k, r)

        def dve_chunk(dve, c, k, a=True, d=True):
            n, l = c + 1, c - 1
            dve_keep_norm(dve, k)
            if a:
                dve_norm(dve, n)
            dve_state(dve, c)
            dve_s_blocks(dve, c, 0)
            dve_kj(dve, c, k, 0)
            if a:
                dve_turned(dve, n)
                dve_queries(dve, n, 1 - k)
            if d:
                dve_x1(dve, l, 1 - k)
            if a:
                dve_norms(dve, n)
            if d:
                dve_rms(dve, l)
            if a:
                dve_keys(dve, n)
                dve_beta(dve, n)
            if d:
                dve_turned_d(dve, l, "h1")
            if a:
                dve_keys_low(dve, n, 1 - k)
                dve_key_blocks(dve, n, 1 - k, 0)
            if d:
                dve_gelu(dve, l, 0)
            if a:
                dve_key_blocks(dve, n, 1 - k, 1)
                dve_p_mask(dve, n, 0)
            if d:
                dve_y(dve, l, 0)
            if a:
                dve_p_low(dve, n, 1 - k, 0)
                dve_key_blocks(dve, n, 1 - k, 2)
                dve_p_mask(dve, n, 1)
            dve_t(dve, c)
            dve_t_blocks(dve, c, 0)
            dve_r(dve, c, k, 0)
            if a:
                dve_p_low(dve, n, 1 - k, 1)
            dve_r_low(dve, c, 0)
            if a:
                dve_key_blocks(dve, n, 1 - k, 3)
                dve_p_mask(dve, n, 2)
            dve_s_blocks(dve, c, 1)
            dve_u(dve, c, 0)
            if a:
                dve_p_low(dve, n, 1 - k, 2)
                dve_p_mask(dve, n, 3)
            dve_t_blocks(dve, c, 1)
            dve_kj(dve, c, k, 1)
            dve_o(dve, c, 0)
            dve_r(dve, c, k, 1)
            if a:
                dve_p_low(dve, n, 1 - k, 3)
            dve_r_low(dve, c, 1)
            dve_s_blocks(dve, c, 2)
            dve_u(dve, c, 1)
            dve_t_blocks(dve, c, 2)
            dve_kj(dve, c, k, 2)
            dve_o(dve, c, 1)
            dve_r(dve, c, k, 2)
            dve_r_low(dve, c, 2)
            dve_s_blocks(dve, c, 3)
            if d:
                dve_gelu(dve, l, 1)
            dve_u(dve, c, 2)
            dve_t_blocks(dve, c, 3)
            if d:
                dve_y(dve, l, 1)
                dve_y_stats(dve, l)
            dve_kj(dve, c, k, 3)
            if d:
                dve_y_norm(dve, l)
            dve_o(dve, c, 2)
            dve_r(dve, c, k, 3)
            dve_r_low(dve, c, 3)
            if d:
                dve_turned_d(dve, l, "h2")
            dve_u(dve, c, 3)
            if d:
                dve_out(dve, l)
            dve_o(dve, c, 3)

        def pool_inverse(pool, a):
            g = nc.gpsimd
            pool.wait_ge(*ra.on_act("LA3", a))
            pool.wait_ge(*ra.on_act("LA2", a))
            pool.wait_ge(*ra.on_act("LB", a))
            beta_i = bl[:, :, :].rearrange("p q i -> p i q")
            g.tensor_tensor(al[:, :, :, :], al[:, :, :, :], beta_i.unsqueeze(3).to_broadcast([P, C, Q2, C]),
                            ALU.mult).then_inc(pool_step, pown.one())
            g.memset(tl[:, :, :, :].rearrange("p i q m -> p (i q m)"), 0.0).then_inc(pool_step, pown.one())
            pool.wait_ge(pool_step, pown.n)
            tflat = tl[:, :, :, :].rearrange("p i q m -> p (i q m)")
            for q in range(Q2):
                diag = tflat[:, q * C:q * C + (C - 1) * (Q2 * C + 1) + 1:Q2 * C + 1]
                ins = g.tensor_copy(diag, bl[:, q, :])
            ins.then_inc(pool_step, pown.one())
            pool.wait_ge(pool_step, pown.n)
            for j in range(C - 1):
                rows, cols = C - 1 - j, j + 1
                tmp = prod[:, 0:rows * Q2 * cols].rearrange("p (i q m) -> p i q m", i=rows, q=Q2)
                shape = [P, rows, Q2, cols]
                g.tensor_tensor(tmp, al[:, j + 1:C, :, j:j + 1].to_broadcast(shape),
                                tl[:, j:j + 1, :, 0:cols].to_broadcast(shape), ALU.mult).then_inc(pool_step, pown.one())
                pool.wait_ge(pool_step, pown.n)
                dst = tl[:, j + 1:C, :, 0:cols]
                last = g.tensor_tensor(dst, dst, tmp, ALU.subtract)
                if j == C - 2:
                    last.then_inc(inv_ready, 1)
                else:
                    last.then_inc(pool_step, pown.one())
                    pool.wait_ge(pool_step, pown.n)

        stage_a, stage_t = regI[:, 0:2 * part], regI[:, 2 * part:4 * part]
        w1_in = stage_a[:, 0:KT * FF].rearrange("p (t n) -> p t n", t=KT)
        w2_in = stage_a[:, KT * FF:KT * FF + MT * D].rearrange("p (t n) -> p t n", t=MT)
        sq_in = stage_t[:, 0:6 * KT * D].rearrange("p (w t n) -> p w t n", w=6, t=KT)
        dish = stage_t[:, 3072:3072 + D]
        wb_in = stage_t[:, 3328:3328 + KT * H].rearrange("p (t h) -> p t h", t=KT)
        wb_pad = stage_t[:, 3584:3584 + KT * P].rearrange("p (t h) -> p t h", t=KT)

        def rows(ap):
            return ap.rearrange("(t p) n -> p t n", p=P)

        loads = [(w1_in, rows(A["L0_attn_w1"])), (w2_in, rows(A["L0_attn_w2"])),
                 (sq_in[:, 0], rows(A["L0_attn_wk"])), (sq_in[:, 1], rows(A["L0_attn_wq"])),
                 (sq_in[:, 2], rows(A["L0_attn_wv"])), (sq_in[:, 3], rows(A["L0_attn_wo"])),
                 (sq_in[:, 4], rows(A["L0_ffn_weight"])), (wb_in, rows(A["L0_attn_wbeta"])),
                 (dish[0:R64, :], A["L0_ffn_disha"]), (dish[R64:P, :], A["L0_ffn_disha"]),
                 (ln_cols[:, 0, :], A["L0_attn_ln1_scale"].rearrange("(t p) -> p t", p=P)),
                 (ln_cols[:, 1, :], A["L0_attn_ln2_scale"].rearrange("(t p) -> p t", p=P)),
                 (b1_cols[:, :], A["L0_attn_b1"].rearrange("(t p) -> p t", p=P)),
                 (bo_rows[:, :], A["L0_attn_bo"].rearrange("(a n) -> a n", a=1).to_broadcast([P, D])),
                 (b2_rows[:, :], A["L0_attn_b2"].rearrange("(a n) -> a n", a=1).to_broadcast([P, D]))]
        for i, w in enumerate(("bk", "bq", "bv")):
            loads.append((qkv_bias[:, i, :], A[f"L0_attn_{w}"].rearrange("(t p) -> p t", p=P)))
        bb = A["L0_attn_bbeta"].rearrange("(g q h a) -> g q h a", g=KT, q=Q4, a=1)
        late = [(beta_bias[q * C + g * HH:q * C + (g + 1) * HH, :], bb[g, q]) for g in range(KT) for q in range(Q4)]

        block = ctx.enter_context(nc.Block())

        @block.sync
        def _(sp):
            for dst, src in loads:
                sp.dma_start(dst, src, allow_slow_non_contiguous=True).then_inc(w_loaded, 16)
            sp.wait_ge(setup_pool, 1)
            for dst, src in late:
                sp.dma_start(dst, src).then_inc(w_loaded, 16)
            sp_load_a(sp, 0, True)
            sp_load_a(sp, 1)
            sp_load_a(sp, 2)
            with sp.Fori(1, CHUNKS // 2 - 1) as p:
                for c in (p * 2 - 1, p * 2):
                    sp_load_d(sp, c - 1)
                    sp_load_a(sp, c + 2)
                    sp_store(sp, c - 1)
            for c in range(CHUNKS - 3, CHUNKS + 1):
                sp_load_d(sp, c - 1)
                if c + 2 < CHUNKS:
                    sp_load_a(sp, c + 2)
                sp_store(sp, c - 1)

        @block.gpsimd
        def _(pool):
            g = nc.gpsimd
            g.memset(beta_bias[:, :], 0.0).then_inc(setup_pool, 1)
            for t in (ident, quad_col, head_col, causal):
                t2 = t[:, :] if len(t.shape) == 2 else t[:, :, :]
                ins = g.memset(t2, 0.0 if t is ident else 1.0)
            for t, v in ((eps_ln, EPS_LN), (eps_rms, EPS_RMS)):
                ins = g.memset(t[:, :], v)
            for t in (kjb, ub):
                ins = g.memset(t[:, :, :, :, :].rearrange("p a b c d -> p (a b c d)"), 0.0)
            ins.then_inc(pool_step, pown.one())
            pool.wait_ge(pool_step, pown.n)
            g.affine_select(out=ident[:, :], in_=ident[:, :], compare_op=ALU.not_equal, fill=1.0, base=0,
                                 pattern=[[-1, P]], channel_multiplier=1).then_inc(pool_step, pown.one())
            pool.wait_ge(pool_step, pown.n)
            hc = head_col[:, :, :].rearrange("p q h -> p (q h)")
            g.affine_select(out=hc, in_=hc, compare_op=ALU.is_ge, fill=0.0, base=0,
                                 pattern=[[-E, 8]], channel_multiplier=1).then_inc(pool_step, pown.one())
            pool.wait_ge(pool_step, pown.n)
            g.affine_select(out=hc, in_=hc, compare_op=ALU.is_ge, fill=0.0, base=E - 1,
                                 pattern=[[E, 8]], channel_multiplier=-1).then_inc(pool_step, pown.one())
            pool.wait_ge(pool_step, pown.n)
            g.affine_select(out=quad_col[:, :], in_=quad_col[:, :], compare_op=ALU.is_ge, fill=0.0, base=0,
                                 pattern=[[-C, Q4]], channel_multiplier=1).then_inc(pool_step, pown.one())
            pool.wait_ge(pool_step, pown.n)
            g.affine_select(out=quad_col[:, :], in_=quad_col[:, :], compare_op=ALU.is_ge, fill=0.0,
                                 base=C - 1, pattern=[[C, Q4]], channel_multiplier=-1).then_inc(pool_step, pown.one())
            pool.wait_ge(pool_step, pown.n)
            for q in range(Q4):
                c = causal[q * C:(q + 1) * C, :]
                g.affine_select(out=c, in_=c, compare_op=ALU.is_ge, fill=0.0, base=0,
                                     pattern=[[1, C]], channel_multiplier=-1).then_inc(pool_step, pown.one())
                pool.wait_ge(pool_step, pown.n)
            hb = hc.unsqueeze(2).to_broadcast([P, 8, E])
            g.tensor_copy(head_mask[:, :, :], hb)
            g.tensor_copy(quad_mask[:, :, :], quad_col[:, :].unsqueeze(2).to_broadcast([P, Q4, E])
                          ).then_inc(setup_pool, 1)
            pool.wait_ge(setup_act, 1)
            pool.wait_ge(setup_dve, 3)
            pool.wait_ge(pool_step, pown.n)
            pool.sem_clear(pool_step)
            pown.n = 0
            pool_inverse(pool, 0)
            pool_inverse(pool, 1)
            pool.wait_ge(pool_step, pown.n)
            pool.sem_clear(pool_step)
            pown.n = 0
            with pool.Fori(1, CHUNKS // 2) as p:
                pool_inverse(pool, p * 2)
                pool_inverse(pool, p * 2 + 1)
                pool.wait_ge(pool_step, pown.n)
                pool.sem_clear(pool_step)
                pown.n = 0

        @block.scalar
        def _(act):
            act.wait_ge(setup_dve, 2)
            for w in range(3):
                nc.scalar.activation(wqkv[:, 0, w, :, :], sq_in[:, w], ACT.Copy)
            nc.scalar.activation(wo[:, 0, :, :], sq_in[:, 3], ACT.Copy)
            nc.scalar.activation(wffn[:, 0, :, :], sq_in[:, 5], ACT.Copy)
            nc.scalar.activation(wbeta[:, 0, :, :], wb_pad, ACT.Copy)
            nc.scalar.activation(w1[:, 0, :, :], w1_in, ACT.Copy)
            nc.scalar.activation(w2[:, 0, :, :], w2_in, ACT.Copy).then_inc(setup_act, 1)
            act_norm(act, 0)
            act_turned(act, 0)
            act_keys(act, 0)
            act_queries(act, 0, 0)
            act_norms(act, 0)
            act_values(act, 0, 0)
            act_beta(act, 0)
            act_keys_high(act, 0, 0)
            for r in range(G4):
                act_gram(act, 0, 0, r)
            act_lanes(act, 0)
            act_chunk(act, 0, 0, d=False)
            with act.Fori(1, CHUNKS // 2) as p:
                act_chunk(act, p * 2 - 1, 1)
                act_chunk(act, p * 2, 0)
            act_chunk(act, CHUNKS - 1, 1, a=False)
            last = CHUNKS - 1
            act_squares(act, last)
            act_turned_d(act, last, "h1")
            act_gelu(act, last, 0)
            act_gelu(act, last, 1)
            act_norm_y(act, last)
            act_turned_d(act, last, "h2")

        @block.tensor
        def _(pe):
            pe.wait_ge(setup_pool, 2)
            pe.wait_ge(w_loaded, 16 * (len(loads) + len(late)))
            nc.tensor.matmul(state[:, :], kjb[:, 0, 0, 0, :], kjb[:, 0, 0, 0:4, :].rearrange("p u n -> p (u n)"),
                             start=True, stop=True)
            for t in range(KT):
                for o in range(KT):
                    ins = nc.tensor.transpose(ps[4][:, (t * KT + o) * P:(t * KT + o + 1) * P],
                                              sq_in[:, 4, o, t * P:(t + 1) * P], ident[:, :])
            ins.then_inc(setup_pe, 1)
            pe.wait_ge(setup_dve, 3)
            pe_turn(pe, 0)
            pe_project(pe, 0, "k")
            pe_project(pe, 0, "q")
            pe_norms(pe, 0)
            pe_project(pe, 0, "v")
            pe_beta(pe, 0)
            pe_norms_back(pe, 0)
            for r in range(G4):
                pe_gram(pe, 0, 0, r)
            pe_lanes(pe, 0)
            pe_chunk(pe, 0, 0, d=False)
            with pe.Fori(1, CHUNKS // 2) as p:
                pe_chunk(pe, p * 2 - 1, 1)
                pe_chunk(pe, p * 2, 0)
            pe_chunk(pe, CHUNKS - 1, 1, a=False)
            last = CHUNKS - 1
            pe_out_proj(pe, last)
            pe_turn_d(pe, last, "h1", hs1_ready)
            for h in range(2):
                pe_w1(pe, last, h)
                pe_w2(pe, last, h)
            pe_turn_d(pe, last, "h2", hs2_ready)
            pe_ffn(pe, last)

        @block.vector
        def _(dve):
            dve.wait_ge(w_loaded, 16 * (len(loads) + len(late)))
            dve.wait_ge(setup_pool, 2)
            V.tensor_scalar(beta_bias[:, :], beta_bias[:, :], 0.5, None, ALU.mult)
            V.memset(wb_pad.rearrange("p t h -> p (t h)"), 0.0).then_inc(dve_step, own.one())
            n = own.n
            dve.wait_ge(dve_step, n)
            for t in range(KT):
                for w in range(3):
                    V.tensor_scalar(sq_in[:, w, t, :], sq_in[:, w, t, :], ln_cols[:, 0, t:t + 1], None, ALU.mult)
                V.tensor_scalar(w1_in[:, t, :], w1_in[:, t, :], ln_cols[:, 1, t:t + 1], None, ALU.mult)
                src = wb_in[:, t, :].rearrange("p (g q h) -> p q g h", g=KT, q=Q4)
                dst = wb_pad[:, t, :].rearrange("p (q s) -> p q s", q=Q4)[:, :, 0:4].rearrange(
                    "p q (g h) -> p q g h", g=KT)
                ins = V.tensor_scalar(dst, src, ln_cols[:, 0, t:t + 1], None, ALU.mult)
            ins.then_inc(setup_dve, 1)
            dve.wait_ge(setup_pe, 1)
            for t in range(KT):
                ins = V.tensor_tensor(sq_in[:, 5, t, :], ps[4][:, t * D:(t + 1) * D], dish, ALU.add)
            ins.then_inc(setup_dve, 1)
            dve.wait_ge(setup_act, 1)
            for w in range(3):
                V.tensor_tensor(wqkv[:, 1, w, :, :], sq_in[:, w], wqkv[:, 0, w, :, :], ALU.subtract)
            V.tensor_tensor(wo[:, 1, :, :], sq_in[:, 3], wo[:, 0, :, :], ALU.subtract)
            V.tensor_tensor(wffn[:, 1, :, :], sq_in[:, 5], wffn[:, 0, :, :], ALU.subtract)
            V.tensor_tensor(wbeta[:, 1, :, :], wb_pad, wbeta[:, 0, :, :], ALU.subtract)
            V.tensor_tensor(w1[:, 1, :, :], w1_in, w1[:, 0, :, :], ALU.subtract)
            V.tensor_tensor(w2[:, 1, :, :], w2_in, w2[:, 0, :, :], ALU.subtract).then_inc(setup_dve, 1)
            dve_a(dve, 0, 0, True)
            dve_chunk(dve, 0, 0, d=False)
            dve.wait_ge(dve_step, own.n)
            dve.sem_clear(dve_step)
            own.n = 0
            with dve.Fori(1, CHUNKS // 2) as p:
                dve_chunk(dve, p * 2 - 1, 1)
                dve_chunk(dve, p * 2, 0)
                dve.wait_ge(dve_step, own.n)
                dve.sem_clear(dve_step)
                own.n = 0
            dve_chunk(dve, CHUNKS - 1, 1, a=False)
            last = CHUNKS - 1
            dve_x1(dve, last, 1)
            dve_rms(dve, last)
            dve_turned_d(dve, last, "h1")
            dve_gelu(dve, last, 0)
            dve_y(dve, last, 0)
            dve_gelu(dve, last, 1)
            dve_y(dve, last, 1)
            dve_y_stats(dve, last)
            dve_y_norm(dve, last)
            dve_turned_d(dve, last, "h2")
            dve_out(dve, last)


_INS = ['L0_attn_x', 'L0_attn_wq', 'L0_attn_bq', 'L0_attn_wk', 'L0_attn_bk', 'L0_attn_wv', 'L0_attn_bv',
        'L0_attn_wbeta', 'L0_attn_bbeta', 'L0_attn_wo', 'L0_attn_bo', 'L0_attn_w1', 'L0_attn_b1', 'L0_attn_w2',
        'L0_attn_b2', 'L0_attn_ln1_scale', 'L0_attn_ln2_scale', 'L0_ffn_weight', 'L0_ffn_disha']


def kernel(**inputs):
    import numpy as _np
    import concourse.bacc as _bacc
    from concourse import mybir as _mybir
    from concourse.bass_utils import run_bass_kernel_spmd as _run

    nc = _bacc.Bacc("TRN2", target_bir_lowering=False, num_devices=1)
    arrays, args = {}, {}
    for name in _INS:
        a = _np.ascontiguousarray(inputs[name])
        arrays[f"in_{name}_dram"] = a
        args[name] = nc.dram_tensor(f"in_{name}_dram", a.shape, _mybir.dt.from_np(a.dtype), kind="ExternalInput").ap()
    args["out"] = nc.dram_tensor("out_0_dram", (16, 512, 256), _mybir.dt.float32, kind="ExternalOutput").ap()
    gated_delta_block(nc, args)
    r = _run(nc, [arrays], core_ids=[0])
    return r.results[0]["out_0_dram"]
```

```python
from contextlib import ExitStack

import concourse.bass as bass
from concourse import mybir

F32 = mybir.dt.float32
F16 = mybir.dt.float16
ALU = mybir.AluOpType
ACT = mybir.ActivationFunctionType

P = 128
B, S, D, H, FF = 16, 512, 256, 16, 1024
E = D // H
C = 32
CHUNKS = S // C
G4 = 4
BG = B // G4
KT = D // P
MT = FF // P
Q4 = 4
HH = 2
UN = BG * KT * HH
LN = B * KT * HH
SEL = P // LN
Q2 = Q4 // SEL
RH = G4 // 2
HN = RH * P
EPS_LN, EPS_RMS, EPS_K = 1e-5, 1e-6, 1e-6
R64 = 64

assert LN * SEL == P and BG * C == P and Q4 * C == P


class Rota:

    def __init__(self, banks, filled, act_read, dve_read, phases, done):
        self.banks, self.sems = banks, (filled, act_read, dve_read)
        self.done = done
        self.at, self.per = {}, {}
        kinds = [list(phases.values())[-1][-1][1]] * len(banks)
        for ph, fills in phases.items():
            counts = [[0, 0, 0] for _ in banks]
            for i, (name, kind) in enumerate(fills):
                b = i % len(banks)
                self.at[name] = (ph, b, tuple(counts[b]), kinds[b], kind)
                counts[b][0] += 1
                counts[b][1] += "A" in kind
                counts[b][2] += "V" in kind
                kinds[b] = kind
            self.per[ph] = counts

    def bank(self, name):
        return self.banks[self.at[name][1]]

    def count(self, name, which, p):
        ph, b, before, _, _ = self.at[name]
        total = before[which]
        for other, times in self.done(ph, p):
            total = total + times * self.per[other][b][which]
        return total

    def on_free(self, name, p):
        _, b, _, last, _ = self.at[name]
        which = 1 if last[-1] == "A" else 2
        return self.sems[which][b], self.count(name, which, p)

    def on_filled(self, name, p):
        return self.sems[0][self.at[name][1]], self.count(name, 0, p) + 1

    def on_act(self, name, p):
        return self.sems[1][self.at[name][1]], self.count(name, 1, p) + 1

    def on_dve(self, name, p):
        return self.sems[2][self.at[name][1]], self.count(name, 2, p) + 1

    def filled(self, name):
        return self.sems[0][self.at[name][1]]

    def act_read(self, name):
        return self.sems[1][self.at[name][1]]

    def dve_read(self, name):
        return self.sems[2][self.at[name][1]]


class Steps:

    def __init__(self):
        self.n = 0

    def one(self):
        self.n += 1
        return 1


def gated_delta_block(nc, A):
    x, out = A["L0_attn_x"], A["out"]
    ctx = ExitStack()
    with ctx:
        def sb(name, shape, dt=F32):
            return ctx.enter_context(nc.sbuf_tensor(name, shape, dt))

        def sem(name):
            return ctx.enter_context(nc.semaphore(name))

        ident = sb("ident", [P, P])
        quad_col = sb("quad_col", [P, Q4])
        head_col = sb("head_col", [P, Q4, HH])
        par_col = sb("par_col", [P, HH])
        quad_mask = sb("quad_mask", [P, Q4, E], F16)
        head_mask = sb("head_mask", [P, 2 * Q4, E], F16)
        causal = sb("causal", [P, C])
        eps_ln, eps_rms = sb("eps_ln", [P, 1]), sb("eps_rms", [P, 1])
        ln_cols = sb("ln_cols", [P, 2, KT])
        qkv_bias = sb("qkv_bias", [P, 3, KT])
        beta_bias = sb("beta_bias", [P, 1])
        b1_cols = sb("b1_cols", [P, MT])
        bias_in = sb("bias_in", [1, 2, D])
        bias_rows = sb("bias_rows", [1, 2, 2, D], F16)
        ones_row = sb("ones_row", [1, P], F16)
        wqkv = sb("wqkv", [P, 2, 3, KT, D], F16)
        wbeta = sb("wbeta", [P, 2, KT, P], F16)
        wo = sb("wo", [P, 2, KT, D], F16)
        w1 = sb("w1", [P, 2, KT, FF], F16)
        w2 = sb("w2", [P, 2, MT, D], F16)
        wffn = sb("wffn", [P, 2, KT, D], F16)

        xa = sb("xa", [P, G4, D])
        bn6 = sb("bn6", [P, G4, 6])
        mv = sb("mv", [P, G4, 2])
        rstd = sb("rstd", [P, G4])
        sd1, ms, sd2, rr = (sb(n, [P, G4]) for n in ("sd1", "ms", "sd2", "rr"))
        hf = sb("hf", [P, 2, KT, B * C], F16)
        kq = sb("kq", [P, 2, 2, 2, KT, B * C], F16)
        vf = sb("vf", [P, 2, KT, B * C])
        kraw = sb("kraw", [P, KT, B * C])
        ksq = sb("ksq", [P, KT, B * C])
        sdk, rnk = sb("sdk", [P, KT, G4 * 2 * Q4]), sb("rnk", [P, KT, G4 * 2 * Q4])
        kblk = sb("kblk", [P, 2, KT * BG, Q4, C], F16)
        kqm = sb("kqm", [P, 2, KT * BG, HH, 2, C], F16)
        beta_f = sb("beta_f", [P, B * C])
        beta_t = sb("beta_t", [P, B, C])
        beta_j = sb("beta_j", [P, LN])
        ptmp = sb("ptmp", [P, KT, BG * HH, C])
        pt = sb("pt", [P, 2, 2, KT, B, HH, C], F16)
        part = C * Q2 * C
        regI = sb("regI", [P, 4 * part])
        al = regI[:, 0:part].rearrange("p (i q j) -> p i q j", i=C, q=Q2)
        tl = regI[:, part:2 * part].rearrange("p (i q m) -> p i q m", i=C, q=Q2)
        gram = regI[:, 2 * part:3 * part].rearrange("p (l i) -> p l i", i=C)
        tt = regI[:, 3 * part:4 * part].bitcast(F16).rearrange("p (z l i) -> p z l i", z=2, i=C)
        bl = sb("bl", [P, Q2, C])
        prod = sb("prod", [P, Q2 * (C // 2) ** 2])
        st = sb("st", [P, 2, LN * E // HH], F16)
        sblk = sb("sblk", [P, 2, BG * KT, P], F16)
        rf, rj = sb("rf", [P, BG * KT, C]), sb("rj", [P, BG * KT, C])
        rr16 = sb("rr16", [P, 2, 2, BG * KT, C], F16)
        uc = sb("uc", [P, 2, 2, UN * E], F16)
        kj = sb("kj", [P, 2, BG * KT, C], F16)
        tblk = sb("tblk", [P, 2, UN, Q4, C], F16)
        bw = 2 * BG * KT * P

        def head_blocks(name):
            flat = sb(name, [P, HH * (bw + E)], F16)
            blocks = flat[:, 0:HH * bw].rearrange("p (h z u n) -> p h z u n", h=HH, z=2, n=P)
            diag = flat[:, :].rearrange("p (h w) -> p h w", h=HH)[:, :, 0:bw].rearrange("p h (v n) -> p h v n", n=P)
            return flat, blocks, diag

        kjb_flat, kjb, kjb_diag = head_blocks("kjb")
        ub_flat, ub, ub_diag = head_blocks("ub")
        of = sb("of", [P, 2, G4, KT, P], F16)
        xd = sb("xd", [P, 2, G4, D])
        rsd, nmr = sb("rsd", [P, 2, G4]), sb("nmr", [P, 2, G4])
        x1 = sb("x1", [P, G4, D])
        ssq, sdr, rdr = sb("ssq", [P, G4]), sb("sdr", [P, G4]), sb("rdr", [P, G4])
        hd = sb("hd", [P, 2, KT, B * C], F16)
        ge = sb("ge", [P, 2, 2, HN])
        gg = sb("gg", [P, 2, MT, HN], F16)
        mv2, sdy, rdy = sb("mv2", [P, G4, 2]), sb("sdy", [P, G4]), sb("rdy", [P, G4])
        bn6d = sb("bn6d", [P, G4, 6])

        ps = [ctx.enter_context(nc.psum_tensor(f"ps{i}", [P, 512], F32)) for i in range(8)]
        state, ubank, xbank = ps[0], ps[1], [ps[2], ps[3]]

        w_loaded, setup_pool, setup_act = sem("w_loaded"), sem("setup_pool"), sem("setup_act")
        setup_dve, setup_pe = sem("setup_dve"), sem("setup_pe")
        x_loaded, stats_ready, sd1_ready = sem("x_loaded"), sem("stats_ready"), sem("sd1_ready")
        ms_ready, sd2_ready, hs_ready = sem("ms_ready"), sem("sd2_ready"), sem("hs_ready")
        rn_ready, knhi_ready = sem("rn_ready"), sem("knhi_ready")
        kn_split, kblk_ready, beta_ready = sem("kn_split"), sem("kblk_ready"), sem("beta_ready")
        phi_ready, p_ready = sem("phi_ready"), sem("p_ready")
        inv_ready = sem("inv_ready")
        sh_ready, sblk_ready, ksqs_done = sem("sh_ready"), sem("sblk_ready"), sem("ksqs_done")
        rj_ready, rh_ready, r_ready = sem("rj_ready"), sem("rh_ready"), sem("r_ready")
        thi_ready, tlo_ready = sem("thi_ready"), sem("tlo_ready")
        u_filled, uh_ready, ublk_ready = sem("u_filled"), sem("uh_ready"), sem("ublk_ready")
        ds_done, o_filled, oh_ready, o_ready = sem("ds_done"), sem("o_filled"), sem("oh_ready"), sem("o_ready")
        xd_loaded, lnx_ready, ssq_ready = sem("xd_loaded"), sem("lnx_ready"), sem("ssq_ready")
        sdr_ready, hs1_ready = sem("sdr_ready"), sem("hs1_ready")
        gl_ready, y_stats, sdy_ready = sem("gl_ready"), sem("y_stats"), sem("sdy_ready")
        hs2_ready, out_stored, xd_free = sem("hs2_ready"), sem("out_stored"), sem("xd_free")
        dve_step, pool_step = sem("dve_step"), sem("pool_step")
        pe_passed = sem("pe_passed")
        own, pown = Steps(), Steps()

        a_fills = [("hT0", "AV"), ("hT1", "AV"), ("k0", "A"), ("k1", "A"), ("q0", "AV"), ("q1", "AV"),
                   ("ks0", "A"), ("ks1", "A"), ("kr0", "V"), ("kr1", "V"), ("v0", "A"), ("v1", "A"), ("beta", "A")]
        a_fills += [(f"G{r}{g}", "AV") for r in range(G4) for g in range(KT)]
        a_fills += [(f"LA{i}", "A") for i in range(4)] + [("LB", "A")]
        d1_fills = [("x10", "V"), ("x11", "V"), ("h10", "AV"), ("h11", "AV")] + [(f"w10{m}", "A") for m in range(4)]
        t_fills = [(f"TF{i}", "AV") for i in range(4)]
        d2_fills = [("w20", "V")] + [(f"w11{m}", "A") for m in range(4)] + [("w21", "V"), ("h20", "AV"), ("h21", "AV"),
                                                           ("ff0", "V"), ("ff1", "V")]

        def rota(tag, banks, phases, done):
            return Rota(banks, *[[sem(f"{tag}{w}{i}") for i in range(len(banks))]
                                 for w in ("_filled", "_act_read", "_dve_read")], phases, done)

        def floor0(v):
            return max(v, 0) if type(v) is int else v

        def before_cd(ph, c):
            if ph == "T":
                return [("D1", c), ("T", c), ("D2", floor0(c - 1))]
            t = c + (1 if ph == "D1" else 2)
            return [("D1", c + (ph == "D2")), ("T", min(t, CHUNKS) if type(t) is int else t), ("D2", c)]

        ra = rota("a", [ps[4], ps[5]], {"A": a_fills}, lambda ph, c: [("A", c)])
        rd = rota("d", [ps[6], ps[7]], {"D1": d1_fills, "T": t_fills, "D2": d2_fills}, before_cd)

        def tokens(ap, c, b):
            return ap.rearrange("(r b) t d -> b t r d", b=BG)[b, bass.ds(c * C, C), :, :]

        def mm3(out_, lh, rh, first, last=True, skip=False):
            passes = ((0, 0), (0, 1), (1, 0))
            for n, (a, b) in enumerate(passes):
                ins = nc.tensor.matmul(out_, lh(a), rh(b), start=first and n == 0,
                                       stop=last and n == 2, skip_group_check=skip)
            return ins

        def turn64(out_, in_, hp):
            if hp.start == 0:
                return nc.tensor.transpose(out_[hp], in_, ident[hp, hp])
            return nc.tensor.matmul(out_[hp], in_, ident[hp, hp], start=True, stop=True)

        def sp_load_a(sp, c, first=False):
            if not first:
                sp.wait_ge(*ra.on_filled("hT1", c - 1))
            for b in range(BG):
                sp.dma_start(xa[b * C:(b + 1) * C, :, :], tokens(x, c, b)).then_inc(x_loaded, 16)

        def sp_load_d(sp, d, k):
            for b in range(BG):
                sp.dma_start(xd[b * C:(b + 1) * C, k, :, :], tokens(x, d, b)).then_inc(xd_loaded, 16)

        def sp_store(sp, d, k):
            sp.wait_ge(*rd.on_dve("ff0", d))
            sp.wait_ge(*rd.on_dve("ff1", d))
            for b in range(BG):
                sp.dma_start(tokens(out, d, b), xd[b * C:(b + 1) * C, k, :, :]).then_inc(out_stored, 16)
            sp.wait_ge(out_stored, d * (16 * BG) + 16 * BG)
            sp.sem_inc(xd_free, 1)

        def pe_turn(pe, a):
            for h in range(2):
                n = f"hT{h}"
                pe.wait_ge(hs_ready, a * G4 + (h + 1) * RH)
                pe.wait_ge(*ra.on_free(n, a))
                for r in range(RH):
                    for t in range(KT):
                        s = (r * KT + t) * P
                        ins = nc.tensor.transpose(ra.bank(n)[:, s:s + P],
                                                  xa[:, h * RH + r, t * P:(t + 1) * P], ident[:, :])
                ins.then_inc(ra.filled(n), 1)

        def pe_project(pe, a, w):
            wi = "kqv".index(w)
            if w == "k":
                pe.wait_ge(*ra.on_dve("hT0", a))
                pe.wait_ge(*ra.on_dve("hT1", a))
            for g in range(KT):
                n = f"{w}{g}"
                pe.wait_ge(*ra.on_free(n, a))
                for t in range(KT):
                    ins = mm3(ra.bank(n)[:, :], lambda z: wqkv[:, z, wi, t, g * P:(g + 1) * P],
                              lambda z: hf[:, z, t, :], t == 0, t == KT - 1)
                ins.then_inc(ra.filled(n), 1)

        def pe_beta(pe, a):
            pe.wait_ge(*ra.on_free("beta", a))
            for t in range(KT):
                ins = mm3(ra.bank("beta")[:, :], lambda z: wbeta[:, z, t, :], lambda z: hf[:, z, t, :],
                          t == 0, t == KT - 1)
            ins.then_inc(ra.filled("beta"), 1)

        def pe_norms(pe, a):
            for g in range(KT):
                n = f"ks{g}"
                pe.wait_ge(*ra.on_act(f"k{g}", a))
                pe.wait_ge(*ra.on_free(n, a))
                for r in range(G4):
                    ins = nc.tensor.matmul(ra.bank(n)[:, r * 8:(r + 1) * 8], ksq[:, g, r * P:(r + 1) * P],
                                           head_col[:, :, :].rearrange("p q h -> p (q h)"), start=True, stop=True)
                ins.then_inc(ra.filled(n), 1)

        def pe_norms_back(pe, a):
            for g in range(KT):
                n = f"kr{g}"
                pe.wait_ge(rn_ready, a * KT + g + 1)
                pe.wait_ge(*ra.on_free(n, a))
                for r in range(G4):
                    ins = nc.tensor.transpose(ra.bank(n)[:, r * P:(r + 1) * P], ksq[:, g, r * P:(r + 1) * P],
                                              ident[:, :])
                ins.then_inc(ra.filled(n), 1)

        def pe_gram(pe, a, r):
            pe.wait_ge(kblk_ready, a * G4 + r + 1)
            for g in range(KT):
                n = f"G{r}{g}"
                pe.wait_ge(*ra.on_free(n, a))
                for b in range(BG):
                    u = g * BG + b
                    ins = mm3(ra.bank(n)[:, b * P:(b + 1) * P],
                              lambda z: kblk[:, z, u, :, :].rearrange("p q t -> p (q t)"),
                              lambda z: kqm[:, z, u, :, :, :].rearrange("p h a t -> p (h a t)"), True)
                ins.then_inc(ra.filled(n), 1)

        def pe_lanes(pe, a):
            pe.wait_ge(*ra.on_act(f"G{G4 - 1}{KT - 1}", a))
            pe.wait_ge(*ra.on_act(f"G{G4 - 1}{KT - 2}", a))
            for i8 in range(4):
                n = f"LA{i8}"
                pe.wait_ge(*ra.on_free(n, a))
                pe.sem_inc(pe_passed, 1)
                for i in range(8):
                    for s in reversed(range(SEL)):
                        hp = slice(s * LN, (s + 1) * LN)
                        ins = turn64(ra.bank(n)[:, i * R64:(i + 1) * R64], gram[hp, :, i8 * 8 + i], hp)
                ins.then_inc(ra.filled(n), 1)
            pe.wait_ge(beta_ready, a + 1)
            pe.wait_ge(*ra.on_free("LB", a))
            pe.sem_inc(pe_passed, 1)
            for s in reversed(range(SEL)):
                hp = slice(s * LN, (s + 1) * LN)
                ins = turn64(ra.bank("LB")[:, 0:R64], beta_j[hp, :], hp)
            ins.then_inc(ra.filled("LB"), 1)

        def pe_t(pe, c):
            pe.wait_ge(inv_ready, c + 1)
            for i8 in range(4):
                n = f"TF{i8}"
                pe.wait_ge(*rd.on_free(n, c))
                pe.sem_inc(pe_passed, 1)
                for i in range(8):
                    for s in reversed(range(SEL)):
                        hp = slice(s * LN, (s + 1) * LN)
                        ins = turn64(rd.bank(n)[:, i * LN:(i + 1) * LN],
                                     tl[hp, i8 * 8 + i, :, :].rearrange("p q m -> p (q m)"), hp)
                ins.then_inc(rd.filled(n), 1)

        def pe_ksqs(pe, c, k, r):
            pe.wait_ge(sblk_ready, c * G4 + r + 1)
            pe.wait_ge(o_ready, floor0(c * G4 + r - 1))
            for b in range(BG):
                for g in range(KT):
                    u = b * KT + g
                    t0 = (r * BG + b) * C
                    ins = mm3(xbank[r % 2][:, u * 2 * C:(u + 1) * 2 * C], lambda z: sblk[:, z, u, :],
                              lambda z: kq[:, z, k, :, g, t0:t0 + C], u == 0, u == BG * KT - 1, True)
            ins.then_inc(ksqs_done, 1)

        def pe_u(pe, c, r):
            pe.wait_ge(thi_ready, c * G4 + r + 1)
            pe.wait_ge(tlo_ready, c * G4 + r + 1)
            pe.wait_ge(r_ready, c * G4 + r + 1)
            pe.wait_ge(ublk_ready, c * G4 + r)
            for b in range(BG):
                for g in range(KT):
                    for hh in range(HH):
                        u = (b * KT + g) * HH + hh
                        ins = mm3(ubank[:, u * E:(u + 1) * E],
                                  lambda z: tblk[:, z, u, :, :].rearrange("p q i -> p (q i)"),
                                  lambda z: rr16[:, z, r % 2, b * KT + g, hh * E:(hh + 1) * E], True)
            ins.then_inc(u_filled, 1)

        def pe_s_and_o(pe, c, k, r):
            pe.wait_ge(ublk_ready, c * G4 + r + 1)
            pe.wait_ge(p_ready, c * G4 + r + 1)
            for b in range(BG):
                for g in range(KT):
                    for hh in range(HH):
                        u = (b * KT + g) * HH + hh
                        s = ((r * BG + b) * KT + g) * E
                        ins = mm3(state[:, s:s + E], lambda z: kjb[:, hh, z, g * BG + b, :],
                                  lambda z: uc[:, r % 2, z, u * E:(u + 1) * E], False, True, True)
            ins.then_inc(ds_done, 1)
            for b in range(BG):
                for g in range(KT):
                    for hh in range(HH):
                        s = (b * KT + g) * 2 * C + C
                        ins = mm3(xbank[r % 2][:, s:s + C], lambda z: ub[:, hh, z, b * KT + g, :],
                                  lambda z: pt[:, z, k, g, r * BG + b, hh, :], False, True, True)
            ins.then_inc(o_filled, 1)

        def add_row(out_, which):
            nc.tensor.matmul(out_, ones_row[:, :], bias_rows[:, 0, which, :], start=True, stop=False)
            nc.tensor.matmul(out_, ones_row[:, :], bias_rows[:, 1, which, :], start=False, stop=False)

        def pe_out_proj(pe, d, h):
            n = f"x1{h}"
            pe.wait_ge(o_ready, d * G4 + (h + 1) * RH)
            pe.wait_ge(*rd.on_free(n, d))
            for r in range(RH):
                add_row(rd.bank(n)[:, r * D:(r + 1) * D], 0)
                for t in range(KT):
                    ins = mm3(rd.bank(n)[:, r * D:(r + 1) * D], lambda z: of[:, z, h * RH + r, t, :],
                              lambda z: wo[:, z, t, :], False, t == KT - 1)
            ins.then_inc(rd.filled(n), 1)

        def pe_turn_d(pe, d, tag, ready):
            for h in range(2):
                n = f"{tag}{h}"
                pe.wait_ge(ready, d * G4 + (h + 1) * RH)
                pe.wait_ge(*rd.on_free(n, d))
                for r in range(RH):
                    for t in range(KT):
                        s = (r * KT + t) * P
                        ins = nc.tensor.transpose(rd.bank(n)[:, s:s + P], x1[:, h * RH + r, t * P:(t + 1) * P],
                                                  ident[:, :])
                ins.then_inc(rd.filled(n), 1)

        def pe_w1(pe, d, h, fills):
            pe.wait_ge(*rd.on_dve(f"h1{h}", d))
            for m2 in fills:
                n = f"w1{h}{m2}"
                pe.wait_ge(*rd.on_free(n, d))
                for j in range(2):
                    m = m2 * 2 + j
                    for t in range(KT):
                        ins = mm3(rd.bank(n)[:, j * HN:(j + 1) * HN], lambda z: w1[:, z, t, m * P:(m + 1) * P],
                                  lambda z: hd[:, z, t, h * HN:(h + 1) * HN], t == 0, t == KT - 1)
                ins.then_inc(rd.filled(n), 1)

        def pe_w2(pe, d, h, r):
            n = f"w2{h}"
            if r == 0:
                pe.wait_ge(*rd.on_free(n, d))
                pe.wait_ge(gl_ready, d * MT + (h + 1) * 4)
            add_row(rd.bank(n)[:, r * D:(r + 1) * D], 1)
            for m in range(MT):
                ins = mm3(rd.bank(n)[:, r * D:(r + 1) * D], lambda z: gg[:, z, m, r * P:(r + 1) * P],
                          lambda z: w2[:, z, m, :], False, m == MT - 1)
            if r == RH - 1:
                ins.then_inc(rd.filled(n), 1)

        def pe_ffn(pe, d):
            for h in range(2):
                n = f"ff{h}"
                pe.wait_ge(*rd.on_dve(f"h2{h}", d))
                pe.wait_ge(*rd.on_free(n, d))
                for r in range(RH):
                    s = (h * RH + r) * P
                    for t in range(KT):
                        ins = mm3(rd.bank(n)[:, r * D:(r + 1) * D], lambda z: hd[:, z, t, s:s + P],
                                  lambda z: wffn[:, z, t, :], t == 0, t == KT - 1)
                ins.then_inc(rd.filled(n), 1)

        def pe_chunk(pe, c, k, t=True, a=True, d=True):
            if a:
                pe_project(pe, c + 1, "k")
                pe_project(pe, c + 1, "q")
                pe_norms(pe, c + 1)
            if d:
                pe_out_proj(pe, c - 1, 0)
            if a:
                pe_norms_back(pe, c + 1)
            if d:
                pe_out_proj(pe, c - 1, 1)
            if a:
                pe_project(pe, c + 1, "v")
                pe_beta(pe, c + 1)
                pe_gram(pe, c + 1, 0)
            if d:
                pe_turn_d(pe, c - 1, "h1", hs1_ready)
            if a:
                pe_gram(pe, c + 1, 1)
            if d:
                pe_w1(pe, c - 1, 0, [0])
            if a:
                pe_gram(pe, c + 1, 2)
            if d:
                pe_w1(pe, c - 1, 0, [1])
            if a:
                pe_gram(pe, c + 1, 3)
            if d:
                pe_w1(pe, c - 1, 0, [2])
            pe_ksqs(pe, c, k, 0)
            if d:
                pe_w1(pe, c - 1, 0, [3])
            if a:
                pe_lanes(pe, c + 1)
            pe_ksqs(pe, c, k, 1)
            pe_t(pe, c)
            if d:
                pe_w2(pe, c - 1, 0, 0)
            pe_u(pe, c, 0)
            if d:
                pe_w2(pe, c - 1, 0, 1)
            pe_s_and_o(pe, c, k, 0)
            pe_u(pe, c, 1)
            if d:
                pe_w1(pe, c - 1, 1, [0, 1])
            pe_ksqs(pe, c, k, 2)
            if d:
                pe_w1(pe, c - 1, 1, [2, 3])
            pe_s_and_o(pe, c, k, 1)
            pe_u(pe, c, 2)
            if d:
                pe_w2(pe, c - 1, 1, 0)
            pe_ksqs(pe, c, k, 3)
            pe_s_and_o(pe, c, k, 2)
            pe_u(pe, c, 3)
            if d:
                pe_w2(pe, c - 1, 1, 1)
            pe_s_and_o(pe, c, k, 3)
            if t:
                pe_turn(pe, c + 2)
            if d:
                pe_turn_d(pe, c - 1, "h2", hs2_ready)
                pe_ffn(pe, c - 1)

        def row_halves(bank):
            return bank[:, :].rearrange("p (r t n) -> p t r n", r=RH, t=KT)

        def col_halves(tile, z, h):
            return tile[:, z, :, h * HN:(h + 1) * HN].rearrange("p t (r n) -> p t r n", r=RH)

        def act_norm1(act, a):
            act.wait_ge(stats_ready, a + 1)
            nc.scalar.activation(sd1[:, :], mv[:, :, 1], ACT.Sqrt, bias=eps_ln[:, 0:1]).then_inc(sd1_ready, 1)

        def act_norm2(act, a):
            act.wait_ge(ms_ready, a + 1)
            nc.scalar.activation(sd2[:, :], ms[:, :], ACT.Sqrt).then_inc(sd2_ready, 1)

        def act_turned(act, a):
            for h in range(2):
                n = f"hT{h}"
                act.wait_ge(*ra.on_filled(n, a))
                nc.scalar.activation(col_halves(hf, 0, h), row_halves(ra.bank(n)),
                                     ACT.Copy).then_inc(ra.act_read(n), 1)

        def act_keys(act, a):
            act.wait_ge(kn_split, a)
            for g in range(KT):
                n = f"k{g}"
                bias = qkv_bias[:, 0, g:g + 1]
                act.wait_ge(*ra.on_filled(n, a))
                nc.scalar.activation(kraw[:, g, :], ra.bank(n)[:, :], ACT.Identity, bias=bias)
                nc.scalar.activation(ksq[:, g, :], ra.bank(n)[:, :], ACT.Square,
                                     bias=bias).then_inc(ra.act_read(n), 1)

        def act_queries(act, a, k):
            for g in range(KT):
                n = f"q{g}"
                act.wait_ge(*ra.on_filled(n, a))
                nc.scalar.activation(kq[:, 0, k, 1, g, :], ra.bank(n)[:, :], ACT.Identity,
                                     bias=qkv_bias[:, 1, g:g + 1]).then_inc(ra.act_read(n), 1)

        def act_norms(act, a):
            for g in range(KT):
                n = f"ks{g}"
                act.wait_ge(*ra.on_filled(n, a))
                nc.scalar.activation(sdk[:, g, :], ra.bank(n)[:, 0:G4 * 8], ACT.Sqrt).then_inc(ra.act_read(n), 1)

        def act_values(act, a, k):
            for g in range(KT):
                n = f"v{g}"
                act.wait_ge(*ra.on_filled(n, a))
                nc.scalar.activation(vf[:, k, g, :], ra.bank(n)[:, :], ACT.Identity,
                                     bias=qkv_bias[:, 2, g:g + 1]).then_inc(ra.act_read(n), 1)

        def act_beta(act, a):
            act.wait_ge(*ra.on_filled("beta", a))
            act.wait_ge(beta_ready, a)
            nc.scalar.activation(beta_f[:, :], ra.bank("beta")[:, :], ACT.Tanh, bias=beta_bias[:, 0:1],
                                 scale=0.5).then_inc(ra.act_read("beta"), 1)

        def act_keys_high(act, a, k):
            for g in range(KT):
                act.wait_ge(*ra.on_dve(f"kr{g}", a))
                nc.scalar.activation(kq[:, 0, k, 0, g, :], kraw[:, g, :], ACT.Copy).then_inc(knhi_ready, 1)

        def act_gram(act, a, r):
            for g in range(KT):
                n = f"G{r}{g}"
                act.wait_ge(*ra.on_filled(n, a))
                src = ra.bank(n)[:, :].rearrange("p (b h s) -> p b h s", b=BG, h=HH)[:, :, :, 0:C]
                dst = gram.rearrange("p (b g h) i -> p b g h i", b=B, g=KT)
                nc.scalar.activation(dst[:, r * BG:(r + 1) * BG, g, :, :], src,
                                     ACT.Copy).then_inc(ra.act_read(n), 1)

        def act_p_high(act, a, k, r):
            act.wait_ge(*ra.on_dve(f"G{r}0", a))
            act.wait_ge(*ra.on_dve(f"G{r}1", a))
            nc.scalar.activation(p_part(0, k, r), ptmp[:, :, :, :], ACT.Copy).then_inc(phi_ready, 1)

        def p_part(z, k, r):
            return pt[:, z, k, :, r * BG:(r + 1) * BG, :, :].rearrange("p g b h i -> p g (b h) i")

        def act_lanes(act, a):
            act.wait_ge(inv_ready, a)
            for i8 in range(4):
                n = f"LA{i8}"
                act.wait_ge(*ra.on_filled(n, a))
                nc.scalar.activation(al[:, i8 * 8:i8 * 8 + 8, :, :].rearrange("p i q j -> p (i q j)"),
                                     ra.bank(n)[:, :], ACT.Copy).then_inc(ra.act_read(n), 1)
            act.wait_ge(*ra.on_filled("LB", a))
            nc.scalar.activation(bl[:, :, :].rearrange("p q j -> p (q j)"), ra.bank("LB")[:, 0:R64],
                                 ACT.Copy).then_inc(ra.act_read("LB"), 1)

        def act_state(act, c):
            act.wait_ge(ds_done, c * G4)
            nc.scalar.activation(st[:, 0, :], state[:, :], ACT.Copy).then_inc(sh_ready, 1)

        def act_t(act, c):
            for i8 in range(4):
                n = f"TF{i8}"
                act.wait_ge(*rd.on_filled(n, c))
                nc.scalar.activation(tt[:, 0, :, i8 * 8:i8 * 8 + 8].rearrange("p l i -> p i l"),
                                     rd.bank(n)[:, :].rearrange("p (i l) -> p i l", i=8),
                                     ACT.Copy).then_inc(rd.act_read(n), 1)

        def act_t_blocks(act, c, r):
            act.wait_ge(u_filled, c * G4 + r)
            if r == 0:
                act.wait_ge(*rd.on_act("TF3", c))
            for q in range(Q4):
                ins = nc.scalar.activation(tblk[:, 0, :, q, :], tt[:, 0, r * UN:(r + 1) * UN, :], ACT.Copy,
                                           scale=quad_col[:, q:q + 1])
            ins.then_inc(thi_ready, 1)

        def act_r(act, c, r):
            act.wait_ge(rj_ready, c * G4 + r + 1)
            nc.scalar.activation(rr16[:, 0, r % 2, :, :], rj[:, :, :], ACT.Copy).then_inc(rh_ready, 1)

        def act_u(act, c, r):
            act.wait_ge(u_filled, c * G4 + r + 1)
            nc.scalar.activation(uc[:, r % 2, 0, :], ubank[:, 0:UN * E], ACT.Copy).then_inc(uh_ready, 1)

        def act_o(act, c, r, d):
            act.wait_ge(o_filled, c * G4 + r + 1)
            if d:
                act.wait_ge(*rd.on_filled(f"x1{r // RH}", c - 1))
            src = xbank[r % 2][:, :].rearrange("p (b g s) -> p g b s", b=BG, g=KT)[:, :, :, C:2 * C]
            dst = of[:, 0, r, :, :].rearrange("p g (b t) -> p g b t", b=BG)
            nc.scalar.activation(dst, src, ACT.Copy).then_inc(oh_ready, 1)

        def act_layer_norm(act, d, k):
            act.wait_ge(xd_loaded, d * (16 * BG) + 16 * BG)
            for r in range(G4):
                ins = nc.scalar.activation(x1[:, r, :], xd[:, k, r, :], ACT.Identity, bias=nmr[:, k, r:r + 1],
                                           scale=rsd[:, k, r:r + 1])
            ins.then_inc(lnx_ready, 1)

        def act_squares(act, d):
            for r in range(G4):
                act.wait_ge(*rd.on_dve(f"x1{r // RH}", d))
                nc.scalar.activation(ge[:, r // 2, r % 2, :], x1[:, r, :], ACT.Square,
                                     accum_out=ssq[:, r:r + 1]).then_inc(ssq_ready, 1)
            act.wait_ge(ssq_ready, (d + 1) * G4)
            nc.scalar.activation(sdr[:, :], ssq[:, :], ACT.Sqrt, bias=eps_rms[:, 0:1],
                                 scale=1.0 / D).then_inc(sdr_ready, 1)

        def act_turned_d(act, d, tag):
            for h in range(2):
                n = f"{tag}{h}"
                act.wait_ge(*rd.on_filled(n, d))
                nc.scalar.activation(col_halves(hd, 0, h), row_halves(rd.bank(n)),
                                     ACT.Copy).then_inc(rd.act_read(n), 1)

        def act_gelu(act, d, h, fills):
            for m2 in fills:
                n = f"w1{h}{m2}"
                act.wait_ge(*rd.on_filled(n, d))
                if h or m2 >= 2:
                    act.wait_ge(gl_ready, d * MT + h * 4 + m2 - 1)
                for j in range(2):
                    m = m2 * 2 + j
                    nc.scalar.activation(ge[:, m2 % 2, j, :], rd.bank(n)[:, j * HN:(j + 1) * HN],
                                         ACT.Gelu_apprx_tanh, bias=b1_cols[:, m:m + 1])
                    ins = nc.scalar.activation(gg[:, 0, m, :], rd.bank(n)[:, j * HN:(j + 1) * HN],
                                               ACT.Gelu_apprx_tanh, bias=b1_cols[:, m:m + 1])
                ins.then_inc(rd.act_read(n), 1)

        def act_norm_y(act, d):
            act.wait_ge(y_stats, d + 1)
            nc.scalar.activation(sdy[:, :], mv2[:, :, 1], ACT.Sqrt, bias=eps_ln[:, 0:1]).then_inc(sdy_ready, 1)

        def act_chunk(act, c, k, t=True, a=True, d=True):
            act_state(act, c)
            if d:
                act_layer_norm(act, c - 1, 1 - k)
            if a:
                act_keys(act, c + 1)
                act_queries(act, c + 1, 1 - k)
                act_norms(act, c + 1)
                act_keys_high(act, c + 1, 1 - k)
            if d:
                act_squares(act, c - 1)
            if a:
                act_values(act, c + 1, 1 - k)
                act_beta(act, c + 1)
                act_gram(act, c + 1, 0)
            if d:
                act_turned_d(act, c - 1, "h1")
            if a:
                act_p_high(act, c + 1, 1 - k, 0)
                act_gram(act, c + 1, 1)
            if d:
                act_gelu(act, c - 1, 0, [0])
            if a:
                act_p_high(act, c + 1, 1 - k, 1)
                act_gram(act, c + 1, 2)
            if d:
                act_gelu(act, c - 1, 0, [1])
            if a:
                act_p_high(act, c + 1, 1 - k, 2)
                act_gram(act, c + 1, 3)
            if d:
                act_gelu(act, c - 1, 0, [2])
            if a:
                act_p_high(act, c + 1, 1 - k, 3)
            act_r(act, c, 0)
            if d:
                act_gelu(act, c - 1, 0, [3])
            if a:
                act_lanes(act, c + 1)
            act_r(act, c, 1)
            act_t(act, c)
            act_t_blocks(act, c, 0)
            act_u(act, c, 0)
            act_t_blocks(act, c, 1)
            act_o(act, c, 0, d)
            act_u(act, c, 1)
            act_t_blocks(act, c, 2)
            if d:
                act_gelu(act, c - 1, 1, [0, 1])
            act_r(act, c, 2)
            if d:
                act_gelu(act, c - 1, 1, [2, 3])
            if t:
                act_norm1(act, c + 2)
            act_o(act, c, 1, d)
            act_u(act, c, 2)
            act_t_blocks(act, c, 3)
            act_r(act, c, 3)
            if t:
                act_norm2(act, c + 2)
            act_o(act, c, 2, d)
            act_u(act, c, 3)
            if d:
                act_norm_y(act, c - 1)
            act_o(act, c, 3, d)
            if t:
                act_turned(act, c + 2)
            if d:
                act_turned_d(act, c - 1, "h2")

        V = nc.vector

        def dve_keep_norm(dve, n, k, d):
            if d:
                dve.wait_ge(lnx_ready, n - 1)
            V.tensor_copy(rsd[:, k, :], rstd[:, :])
            V.scalar_tensor_tensor(out=nmr[:, k, :], in0=mv[:, :, 0], scalar=-1.0, in1=rstd[:, :],
                                   op0=ALU.mult, op1=ALU.mult).then_inc(dve_step, own.one())
            dve.wait_ge(dve_step, own.n)

        def dve_norm1(dve, a):
            dve.wait_ge(x_loaded, a * (16 * BG) + 16 * BG)
            for r in range(G4):
                V.bn_stats(bn6[:, r, :], xa[:, r, :]).then_inc(dve_step, own.one())
            dve.wait_ge(dve_step, own.n)
            for r in range(G4):
                ins = V.bn_aggr(mv[:, r, :], bn6[:, r, :])
            ins.then_inc(stats_ready, 1)

        def dve_norm2(dve, a):
            dve.wait_ge(sd1_ready, a + 1)
            V.reciprocal(rstd[:, :], sd1[:, :]).then_inc(dve_step, own.one())
            dve.wait_ge(dve_step, own.n)
            V.tensor_tensor(ms[:, :], mv[:, :, 1], rstd[:, :], ALU.mult).then_inc(dve_step, own.one())
            dve.wait_ge(dve_step, own.n)
            V.tensor_tensor(ms[:, :], ms[:, :], rstd[:, :], ALU.mult).then_inc(dve_step, own.one())
            dve.wait_ge(dve_step, own.n)
            V.tensor_scalar(ms[:, :], ms[:, :], EPS_RMS, None, ALU.add).then_inc(ms_ready, 1)

        def dve_norm3(dve, a):
            dve.wait_ge(sd2_ready, a + 1)
            V.reciprocal(rr[:, :], sd2[:, :]).then_inc(dve_step, own.one())
            dve.wait_ge(dve_step, own.n)
            V.tensor_tensor(rr[:, :], rr[:, :], rstd[:, :], ALU.mult).then_inc(dve_step, own.one())
            dve.wait_ge(dve_step, own.n)
            for r in range(G4):
                V.tensor_scalar(xa[:, r, :], xa[:, r, :], mv[:, r, 0:1], rr[:, r:r + 1],
                                ALU.subtract, ALU.mult).then_inc(hs_ready, 1)

        def dve_turned(dve, a):
            for h in range(2):
                n = f"hT{h}"
                dve.wait_ge(*ra.on_act(n, a))
                V.tensor_tensor(col_halves(hf, 1, h), row_halves(ra.bank(n)), col_halves(hf, 0, h),
                                ALU.subtract).then_inc(ra.dve_read(n), 1)

        def dve_queries(dve, a, k):
            for g in range(KT):
                n = f"q{g}"
                dve.wait_ge(*ra.on_act(n, a))
                V.scalar_tensor_tensor(out=kq[:, 1, k, 1, g, :], in0=ra.bank(n)[:, :],
                                       scalar=qkv_bias[:, 1, g:g + 1], in1=kq[:, 0, k, 1, g, :],
                                       op0=ALU.add, op1=ALU.subtract).then_inc(ra.dve_read(n), 1)

        def dve_norms(dve, a):
            for g in range(KT):
                dve.wait_ge(*ra.on_act(f"ks{g}", a))
            V.tensor_scalar(sdk[:, :, :], sdk[:, :, :], EPS_K, None, ALU.add).then_inc(dve_step, own.one())
            dve.wait_ge(dve_step, own.n)
            V.reciprocal(rnk[:, :, :], sdk[:, :, :]).then_inc(dve_step, own.one())
            dve.wait_ge(dve_step, own.n)
            for g in range(KT):
                dst = ksq[:, g, :].rearrange("p (h e) -> p h e", e=E)
                V.tensor_copy(dst, rnk[:, g, :].unsqueeze(2).to_broadcast([P, G4 * 8, E])).then_inc(rn_ready, 1)

        def dve_beta(dve, a):
            dve.wait_ge(*ra.on_act("beta", a))
            V.tensor_scalar(beta_f[:, :], beta_f[:, :], 0.5, 0.5, ALU.mult, ALU.add).then_inc(dve_step, own.one())
            dve.wait_ge(dve_step, own.n)
            V.transpose(beta_t[:, :, :].rearrange("p b t -> p (b t)"), beta_f[:, :]).then_inc(dve_step, own.one())
            dve.wait_ge(dve_step, own.n)
            V.tensor_copy(beta_j[:, :].rearrange("p (b g) -> p b g", g=KT * HH),
                          beta_t[:, :, 0:KT * HH]).then_inc(beta_ready, 1)

        def dve_keys(dve, a):
            for g in range(KT):
                n = f"kr{g}"
                dve.wait_ge(*ra.on_filled(n, a))
                V.tensor_tensor(kraw[:, g, :], kraw[:, g, :], ra.bank(n)[:, :], ALU.mult).then_inc(ra.dve_read(n), 1)

        def dve_keys_low(dve, a, k):
            dve.wait_ge(knhi_ready, a * KT + KT)
            V.tensor_tensor(kq[:, 1, k, 0, :, :], kraw[:, :, :], kq[:, 0, k, 0, :, :],
                            ALU.subtract).then_inc(kn_split, 1)
            dve.wait_ge(kn_split, a + 1)

        def dve_key_blocks(dve, a, k, r, first=False):
            if not (first and r == 0):
                dve.wait_ge(*ra.on_filled(f"G{(r - 1) % G4}1", a if r else a - 1))
            for z in range(2):
                src = kq[:, z, k, :, :, r * P:(r + 1) * P].rearrange("p w g (b t) -> p w g b t", b=BG)
                for hh in range(HH):
                    V.tensor_scalar(kqm[:, z, :, hh, :, :].rearrange("p (g b) w t -> p w g b t", g=KT), src,
                                    par_col[:, hh:hh + 1], None, ALU.mult)
            src = kq[:, :, k, 0, :, r * P:(r + 1) * P].rearrange("p z g (b t) -> p z g b t", b=BG)
            for q in range(Q4):
                ins = V.tensor_scalar(kblk[:, :, :, q, :].rearrange("p z (g b) t -> p z g b t", g=KT), src,
                                      quad_col[:, q:q + 1], None, ALU.mult)
            ins.then_inc(kblk_ready, 1)

        def dve_p_mask(dve, a, r):
            dve.wait_ge(p_ready, a * G4 + r)
            for g in range(KT):
                n = f"G{r}{g}"
                dve.wait_ge(*ra.on_act(n, a))
                src = ra.bank(n)[:, :].rearrange("p (u s) -> p u s", s=2 * C)[:, :, C:2 * C]
                V.tensor_tensor(ptmp[:, g, :, :], src, causal[:, :].unsqueeze(1).to_broadcast([P, BG * HH, C]),
                                ALU.mult).then_inc(ra.dve_read(n), 1)

        def dve_p_low(dve, a, k, r):
            dve.wait_ge(phi_ready, a * G4 + r + 1)
            V.tensor_tensor(p_part(1, k, r), ptmp[:, :, :, :], p_part(0, k, r), ALU.subtract).then_inc(p_ready, 1)

        def dve_state(dve, c):
            dve.wait_ge(sh_ready, c + 1)
            V.tensor_tensor(st[:, 1, :], state[:, :], st[:, 0, :], ALU.subtract).then_inc(dve_step, own.one())
            dve.wait_ge(dve_step, own.n)

        def dve_s_blocks(dve, c, r):
            dve.wait_ge(ksqs_done, c * G4 + r)
            for z in range(2):
                src = st[:, z, r * P:(r + 1) * P].rearrange("p (u d) -> p u d", d=E)
                ins = V.tensor_tensor(sblk[:, z, :, :].rearrange("p u (h d) -> p u h d", d=E),
                                      src.unsqueeze(2).to_broadcast([P, BG * KT, 2 * Q4, E]),
                                      head_mask[:, :, :].unsqueeze(1).to_broadcast([P, BG * KT, 2 * Q4, E]),
                                      ALU.mult)
            ins.then_inc(sblk_ready, 1)

        def dve_t(dve, c):
            for i8 in range(4):
                n = f"TF{i8}"
                dve.wait_ge(*rd.on_act(n, c))
                i8s = slice(i8 * 8, i8 * 8 + 8)
                V.tensor_tensor(tt[:, 1, :, i8s].rearrange("p l i -> p i l"),
                                rd.bank(n)[:, :].rearrange("p (i l) -> p i l", i=8),
                                tt[:, 0, :, i8s].rearrange("p l i -> p i l"), ALU.subtract).then_inc(rd.dve_read(n), 1)
            dve.wait_ge(*rd.on_dve("TF2", c))
            dve.wait_ge(*rd.on_dve("TF3", c))

        def dve_t_blocks(dve, c, r):
            dve.wait_ge(u_filled, c * G4 + r)
            for q in range(Q4):
                ins = V.tensor_scalar(tblk[:, 1, :, q, :], tt[:, 1, r * UN:(r + 1) * UN, :], quad_col[:, q:q + 1],
                                      None, ALU.mult)
            ins.then_inc(tlo_ready, 1)

        def dve_r(dve, c, k, r):
            dve.wait_ge(ksqs_done, c * G4 + r + 1)
            src = xbank[r % 2][:, :].rearrange("p (b g s) -> p b g s", b=BG, g=KT)[:, :, :, 0:C]
            val = vf[:, k, :, r * P:(r + 1) * P].rearrange("p g (b t) -> p b g t", b=BG)
            V.tensor_tensor(rf[:, :, :].rearrange("p (b g) t -> p b g t", b=BG), val, src,
                            ALU.subtract).then_inc(dve_step, own.one())
            dve.wait_ge(dve_step, own.n)
            V.transpose(rj[:, :, :].rearrange("p u t -> p (u t)"),
                        rf[:, :, :].rearrange("p u t -> p (u t)")).then_inc(rj_ready, 1)

        def dve_r_low(dve, c, r):
            dve.wait_ge(rh_ready, c * G4 + r + 1)
            V.tensor_tensor(rr16[:, 1, r % 2, :, :], rj[:, :, :], rr16[:, 0, r % 2, :, :],
                            ALU.subtract).then_inc(r_ready, 1)

        def dve_kj(dve, c, k, r):
            dve.wait_ge(ds_done, c * G4 + r)
            for z in range(2):
                V.transpose(kj[:, z, :, :].rearrange("p (g b) t -> p g (b t)", g=KT),
                            kq[:, z, k, 0, :, r * P:(r + 1) * P]).then_inc(dve_step, own.one())
            dve.wait_ge(dve_step, own.n)
            for q in range(Q4):
                V.tensor_scalar(kjb_diag[:, :, :, q * C:q * C + E],
                                kj[:, :, :, :].rearrange("p z u (h e) -> p h (z u) e", h=HH),
                                quad_col[:, q:q + 1], None, ALU.mult)

        def dve_u(dve, c, r):
            dve.wait_ge(uh_ready, c * G4 + r + 1)
            V.tensor_tensor(uc[:, r % 2, 1, :], ubank[:, 0:UN * E], uc[:, r % 2, 0, :],
                            ALU.subtract).then_inc(dve_step, own.one())
            dve.wait_ge(o_filled, c * G4 + r)
            dve.wait_ge(dve_step, own.n)
            src = uc[:, r % 2, :, :].rearrange("p z (u h d) -> p h (z u) d", h=HH, d=E)
            for q in range(Q4):
                ins = V.tensor_scalar(ub_diag[:, :, :, q * C:q * C + E], src, quad_col[:, q:q + 1], None, ALU.mult)
            ins.then_inc(ublk_ready, 1)

        def dve_o(dve, c, r):
            dve.wait_ge(oh_ready, c * G4 + r + 1)
            src = xbank[r % 2][:, :].rearrange("p (b g s) -> p g b s", b=BG, g=KT)[:, :, :, C:2 * C]
            dst = of[:, :, r, :, :].rearrange("p z g (b t) -> p z g b t", b=BG)
            V.tensor_tensor(dst[:, 1], src, dst[:, 0], ALU.subtract).then_inc(o_ready, 1)

        def dve_x1(dve, d, h):
            dve.wait_ge(lnx_ready, d + 1)
            n = f"x1{h}"
            dve.wait_ge(*rd.on_filled(n, d))
            rs = slice(h * RH, (h + 1) * RH)
            V.tensor_tensor(x1[:, rs, :], rd.bank(n)[:, :].rearrange("p (r d) -> p r d", r=RH), x1[:, rs, :],
                            ALU.add).then_inc(rd.dve_read(n), 1)

        def dve_residual(dve, d, k):
            dve.wait_ge(*rd.on_dve("x10", d))
            dve.wait_ge(*rd.on_dve("x11", d))
            V.tensor_tensor(xd[:, k, :, :], xd[:, k, :, :], x1[:, :, :], ALU.add).then_inc(dve_step, own.one())

        def dve_rms(dve, d):
            dve.wait_ge(sdr_ready, d + 1)
            V.reciprocal(rdr[:, :], sdr[:, :]).then_inc(dve_step, own.one())
            dve.wait_ge(dve_step, own.n)
            for r in range(G4):
                V.tensor_scalar(x1[:, r, :], x1[:, r, :], rdr[:, r:r + 1], None, ALU.mult).then_inc(hs1_ready, 1)

        def dve_turned_d(dve, d, tag):
            for h in range(2):
                n = f"{tag}{h}"
                dve.wait_ge(*rd.on_act(n, d))
                V.tensor_tensor(col_halves(hd, 1, h), row_halves(rd.bank(n)), col_halves(hd, 0, h),
                                ALU.subtract).then_inc(rd.dve_read(n), 1)

        def dve_gelu(dve, d, h, fills):
            for m2 in fills:
                dve.wait_ge(*rd.on_act(f"w1{h}{m2}", d))
                ms2 = slice(m2 * 2, m2 * 2 + 2)
                V.tensor_tensor(gg[:, 1, ms2, :], ge[:, m2 % 2, :, :], gg[:, 0, ms2, :],
                                ALU.subtract).then_inc(gl_ready, 1)

        def dve_y(dve, d, k, h):
            n = f"w2{h}"
            dve.wait_ge(*rd.on_filled(n, d))
            rs = slice(h * RH, (h + 1) * RH)
            V.tensor_tensor(xd[:, k, rs, :], rd.bank(n)[:, :].rearrange("p (r d) -> p r d", r=RH), xd[:, k, rs, :],
                            ALU.add).then_inc(rd.dve_read(n), 1)
            dve.wait_ge(*rd.on_dve(n, d))
            for r in range(h * RH, (h + 1) * RH):
                V.bn_stats(bn6d[:, r, :], xd[:, k, r, :]).then_inc(dve_step, own.one())

        def dve_y_stats(dve, d):
            dve.wait_ge(dve_step, own.n)
            for r in range(G4):
                ins = V.bn_aggr(mv2[:, r, :], bn6d[:, r, :])
            ins.then_inc(y_stats, 1)

        def dve_y_norm(dve, d, k):
            dve.wait_ge(sdy_ready, d + 1)
            V.reciprocal(rdy[:, :], sdy[:, :]).then_inc(dve_step, own.one())
            dve.wait_ge(dve_step, own.n)
            for r in range(G4):
                V.tensor_scalar(x1[:, r, :], xd[:, k, r, :], mv2[:, r, 0:1], rdy[:, r:r + 1],
                                ALU.subtract, ALU.mult).then_inc(hs2_ready, 1)

        def dve_out(dve, d, k):
            for h in range(2):
                n = f"ff{h}"
                dve.wait_ge(*rd.on_filled(n, d))
                rs = slice(h * RH, (h + 1) * RH)
                V.tensor_tensor(xd[:, k, rs, :], rd.bank(n)[:, :].rearrange("p (r d) -> p r d", r=RH), xd[:, k, rs, :],
                                ALU.add).then_inc(rd.dve_read(n), 1)

        def dve_a(dve, a, k, first=False):
            dve_norm1(dve, a)
            dve_norm2(dve, a)
            dve_norm3(dve, a)
            dve_keep_norm(dve, a, k, False)
            dve_turned(dve, a)
            dve_queries(dve, a, k)
            dve_norms(dve, a)
            dve_keys(dve, a)
            dve_beta(dve, a)
            dve_keys_low(dve, a, k)
            for r in range(G4):
                dve_key_blocks(dve, a, k, r, first)
                dve_p_mask(dve, a, r)
                dve_p_low(dve, a, k, r)

        def dve_chunk(dve, c, k, t=True, a=True, d=True):
            n, l = c + 1, c - 1
            dve_state(dve, c)
            dve_s_blocks(dve, c, 0)
            if a:
                dve_queries(dve, n, 1 - k)
                dve_norms(dve, n)
            if d:
                dve_x1(dve, l, 0)
            if a:
                dve_keys(dve, n)
            if d:
                dve_x1(dve, l, 1)
            if a:
                dve_keys_low(dve, n, 1 - k)
                dve_key_blocks(dve, n, 1 - k, 0)
            if d:
                dve_residual(dve, l, 1 - k)
                dve_rms(dve, l)
            if a:
                dve_key_blocks(dve, n, 1 - k, 1)
                dve_p_mask(dve, n, 0)
            if d:
                dve_turned_d(dve, l, "h1")
            if a:
                dve_p_low(dve, n, 1 - k, 0)
                dve_key_blocks(dve, n, 1 - k, 2)
                dve_p_mask(dve, n, 1)
            if d:
                dve_gelu(dve, l, 0, [0])
            if a:
                dve_p_low(dve, n, 1 - k, 1)
                dve_key_blocks(dve, n, 1 - k, 3)
                dve_p_mask(dve, n, 2)
            if d:
                dve_gelu(dve, l, 0, [1])
            if a:
                dve_p_low(dve, n, 1 - k, 2)
                dve_keep_norm(dve, n, 1 - k, d)
                dve_beta(dve, n)
                dve_p_mask(dve, n, 3)
            if d:
                dve_gelu(dve, l, 0, [2])
            if a:
                dve_p_low(dve, n, 1 - k, 3)
            dve_r(dve, c, k, 0)
            dve_r_low(dve, c, 0)
            dve_s_blocks(dve, c, 1)
            if d:
                dve_gelu(dve, l, 0, [3])
            dve_kj(dve, c, k, 0)
            dve_r(dve, c, k, 1)
            dve_r_low(dve, c, 1)
            dve_t(dve, c)
            dve_t_blocks(dve, c, 0)
            dve_s_blocks(dve, c, 2)
            dve_u(dve, c, 0)
            dve_t_blocks(dve, c, 1)
            if d:
                dve_y(dve, l, 1 - k, 0)
            dve_kj(dve, c, k, 1)
            dve_o(dve, c, 0)
            dve_u(dve, c, 1)
            dve_t_blocks(dve, c, 2)
            if d:
                dve_gelu(dve, l, 1, [0, 1])
            dve_r(dve, c, k, 2)
            dve_r_low(dve, c, 2)
            dve_s_blocks(dve, c, 3)
            if d:
                dve_gelu(dve, l, 1, [2, 3])
            if t:
                dve_norm1(dve, c + 2)
            dve_kj(dve, c, k, 2)
            dve_o(dve, c, 1)
            dve_u(dve, c, 2)
            dve_t_blocks(dve, c, 3)
            if t:
                dve_norm2(dve, c + 2)
            dve_r(dve, c, k, 3)
            dve_r_low(dve, c, 3)
            if t:
                dve_norm3(dve, c + 2)
            dve_kj(dve, c, k, 3)
            dve_o(dve, c, 2)
            dve_u(dve, c, 3)
            if d:
                dve_y(dve, l, 1 - k, 1)
                dve_y_stats(dve, l)
                dve_y_norm(dve, l, 1 - k)
            dve_o(dve, c, 3)
            if t:
                dve_turned(dve, c + 2)
            if d:
                dve_turned_d(dve, l, "h2")
                dve_out(dve, l, 1 - k)

        def pool_inverse(pool, a, first=False):
            g = nc.gpsimd
            if not first:
                pool.wait_ge(*rd.on_filled("TF2", a - 1))
                pool.wait_ge(*rd.on_filled("TF3", a - 1))
            pool.wait_ge(*ra.on_act("LA3", a))
            pool.wait_ge(*ra.on_act("LA2", a))
            pool.wait_ge(*ra.on_act("LB", a))
            beta_i = bl[:, :, :].rearrange("p q i -> p i q")
            g.tensor_tensor(al[:, :, :, :], al[:, :, :, :], beta_i.unsqueeze(3).to_broadcast([P, C, Q2, C]),
                            ALU.mult).then_inc(pool_step, pown.one())
            g.memset(tl[:, :, :, :].rearrange("p i q m -> p (i q m)"), 0.0).then_inc(pool_step, pown.one())
            pool.wait_ge(pool_step, pown.n)
            tflat = tl[:, :, :, :].rearrange("p i q m -> p (i q m)")
            for q in range(Q2):
                diag = tflat[:, q * C:q * C + (C - 1) * (Q2 * C + 1) + 1:Q2 * C + 1]
                ins = g.tensor_copy(diag, bl[:, q, :])
            ins.then_inc(pool_step, pown.one())
            pool.wait_ge(pool_step, pown.n)
            for j in range(C - 1):
                rows, cols = C - 1 - j, j + 1
                tmp = prod[:, 0:rows * Q2 * cols].rearrange("p (i q m) -> p i q m", i=rows, q=Q2)
                shape = [P, rows, Q2, cols]
                g.tensor_tensor(tmp, al[:, j + 1:C, :, j:j + 1].to_broadcast(shape),
                                tl[:, j:j + 1, :, 0:cols].to_broadcast(shape), ALU.mult).then_inc(pool_step, pown.one())
                pool.wait_ge(pool_step, pown.n)
                dst = tl[:, j + 1:C, :, 0:cols]
                last = g.tensor_tensor(dst, dst, tmp, ALU.subtract)
                if j == C - 2:
                    last.then_inc(inv_ready, 1)
                else:
                    last.then_inc(pool_step, pown.one())
                    pool.wait_ge(pool_step, pown.n)

        stage_a, stage_t = regI[:, 0:2 * part], regI[:, 2 * part:4 * part]
        w1_in = stage_a[:, 0:KT * FF].rearrange("p (t n) -> p t n", t=KT)
        w2_in = stage_a[:, KT * FF:KT * FF + MT * D].rearrange("p (t n) -> p t n", t=MT)
        sq_in = stage_t[:, 0:6 * KT * D].rearrange("p (w t n) -> p w t n", w=6, t=KT)
        dish = stage_t[:, 3072:3072 + D]
        wb_in = stage_t[:, 3328:3328 + KT * H].rearrange("p (t h) -> p t h", t=KT)
        wb_pad = stage_t[:, 3584:3584 + KT * P].rearrange("p (t h) -> p t h", t=KT)

        def rows(ap):
            return ap.rearrange("(t p) n -> p t n", p=P)

        loads = [(w1_in, rows(A["L0_attn_w1"])), (w2_in, rows(A["L0_attn_w2"])),
                 (sq_in[:, 0], rows(A["L0_attn_wk"])), (sq_in[:, 1], rows(A["L0_attn_wq"])),
                 (sq_in[:, 2], rows(A["L0_attn_wv"])), (sq_in[:, 3], rows(A["L0_attn_wo"])),
                 (sq_in[:, 4], rows(A["L0_ffn_weight"])), (wb_in, rows(A["L0_attn_wbeta"])),
                 (dish[0:R64, :], A["L0_ffn_disha"]), (dish[R64:P, :], A["L0_ffn_disha"]),
                 (ln_cols[:, 0, :], A["L0_attn_ln1_scale"].rearrange("(t p) -> p t", p=P)),
                 (ln_cols[:, 1, :], A["L0_attn_ln2_scale"].rearrange("(t p) -> p t", p=P)),
                 (b1_cols[:, :], A["L0_attn_b1"].rearrange("(t p) -> p t", p=P)),
                 (bias_in[:, 0, :], A["L0_attn_bo"].rearrange("(a n) -> a n", a=1)),
                 (bias_in[:, 1, :], A["L0_attn_b2"].rearrange("(a n) -> a n", a=1))]
        for i, w in enumerate(("bk", "bq", "bv")):
            loads.append((qkv_bias[:, i, :], A[f"L0_attn_{w}"].rearrange("(t p) -> p t", p=P)))
        bb = A["L0_attn_bbeta"].rearrange("(g q h a) -> g q h a", g=KT, q=Q4, a=1)
        late = [(beta_bias[q * C + g * HH:q * C + (g + 1) * HH, :], bb[g, q]) for g in range(KT) for q in range(Q4)]

        block = ctx.enter_context(nc.Block())

        @block.sync
        def _(sp):
            for dst, src in loads:
                sp.dma_start(dst, src, allow_slow_non_contiguous=True).then_inc(w_loaded, 16)
            sp.wait_ge(setup_pool, 1)
            for dst, src in late:
                sp.dma_start(dst, src).then_inc(w_loaded, 16)
            sp_load_a(sp, 0, True)
            sp_load_a(sp, 1)
            sp_load_d(sp, 0, 0)
            sp_load_a(sp, 2)
            with sp.Fori(1, CHUNKS // 2 - 1) as p:
                for c, k in ((p * 2 - 1, 1), (p * 2, 0)):
                    sp_load_d(sp, c, k)
                    sp_load_a(sp, c + 2)
                    sp_store(sp, c - 1, 1 - k)
            for c in range(CHUNKS - 3, CHUNKS + 1):
                if c < CHUNKS:
                    sp_load_d(sp, c, c % 2)
                if c + 2 < CHUNKS:
                    sp_load_a(sp, c + 2)
                sp_store(sp, c - 1, 1 - c % 2)

        @block.gpsimd
        def _(pool):
            g = nc.gpsimd
            g.memset(beta_bias[:, :], 0.0).then_inc(setup_pool, 1)
            for t in (ident, quad_col, head_col, causal):
                t2 = t[:, :] if len(t.shape) == 2 else t[:, :, :]
                ins = g.memset(t2, 0.0 if t is ident else 1.0)
            for t, v in ((eps_ln, EPS_LN), (eps_rms, EPS_RMS), (ones_row, 1.0)):
                ins = g.memset(t[:, :], v)
            for t in (kjb_flat, ub_flat):
                ins = g.memset(t[:, :], 0.0)
            ins.then_inc(pool_step, pown.one())
            pool.wait_ge(pool_step, pown.n)
            g.affine_select(out=ident[:, :], in_=ident[:, :], compare_op=ALU.not_equal, fill=1.0, base=0,
                                 pattern=[[-1, P]], channel_multiplier=1).then_inc(pool_step, pown.one())
            pool.wait_ge(pool_step, pown.n)
            hc = head_col[:, :, :].rearrange("p q h -> p (q h)")
            g.affine_select(out=hc, in_=hc, compare_op=ALU.is_ge, fill=0.0, base=0,
                                 pattern=[[-E, 8]], channel_multiplier=1).then_inc(pool_step, pown.one())
            pool.wait_ge(pool_step, pown.n)
            g.affine_select(out=hc, in_=hc, compare_op=ALU.is_ge, fill=0.0, base=E - 1,
                                 pattern=[[E, 8]], channel_multiplier=-1).then_inc(pool_step, pown.one())
            pool.wait_ge(pool_step, pown.n)
            g.affine_select(out=quad_col[:, :], in_=quad_col[:, :], compare_op=ALU.is_ge, fill=0.0, base=0,
                                 pattern=[[-C, Q4]], channel_multiplier=1).then_inc(pool_step, pown.one())
            pool.wait_ge(pool_step, pown.n)
            g.affine_select(out=quad_col[:, :], in_=quad_col[:, :], compare_op=ALU.is_ge, fill=0.0,
                                 base=C - 1, pattern=[[C, Q4]], channel_multiplier=-1).then_inc(pool_step, pown.one())
            pool.wait_ge(pool_step, pown.n)
            for q in range(Q4):
                c = causal[q * C:(q + 1) * C, :]
                g.affine_select(out=c, in_=c, compare_op=ALU.is_ge, fill=0.0, base=0,
                                     pattern=[[1, C]], channel_multiplier=-1).then_inc(pool_step, pown.one())
                pool.wait_ge(pool_step, pown.n)
            g.tensor_tensor(par_col[:, :], head_col[:, 0, :], head_col[:, 1, :], ALU.add).then_inc(pool_step, pown.one())
            for q in range(2, Q4):
                pool.wait_ge(pool_step, pown.n)
                g.tensor_tensor(par_col[:, :], par_col[:, :], head_col[:, q, :],
                                ALU.add).then_inc(pool_step, pown.one())
            hb = hc.unsqueeze(2).to_broadcast([P, 8, E])
            g.tensor_copy(head_mask[:, :, :], hb)
            g.tensor_copy(quad_mask[:, :, :], quad_col[:, :].unsqueeze(2).to_broadcast([P, Q4, E])
                          ).then_inc(setup_pool, 1)
            pool.wait_ge(setup_act, 1)
            pool.wait_ge(setup_dve, 3)
            pool.wait_ge(pool_step, pown.n)
            pool.sem_clear(pool_step)
            pown.n = 0
            pool_inverse(pool, 0, True)
            pool_inverse(pool, 1)
            pool.wait_ge(pool_step, pown.n)
            pool.sem_clear(pool_step)
            pown.n = 0
            with pool.Fori(1, CHUNKS // 2) as p:
                pool_inverse(pool, p * 2)
                pool_inverse(pool, p * 2 + 1)
                pool.wait_ge(pool_step, pown.n)
                pool.sem_clear(pool_step)
                pown.n = 0

        @block.scalar
        def _(act):
            act.wait_ge(setup_dve, 2)
            for w in range(3):
                nc.scalar.activation(wqkv[:, 0, w, :, :], sq_in[:, w], ACT.Copy)
            nc.scalar.activation(wo[:, 0, :, :], sq_in[:, 3], ACT.Copy)
            nc.scalar.activation(wffn[:, 0, :, :], sq_in[:, 5], ACT.Copy)
            nc.scalar.activation(bias_rows[:, 0, :, :], bias_in[:, :, :], ACT.Copy)
            nc.scalar.activation(wbeta[:, 0, :, :], wb_pad, ACT.Copy)
            nc.scalar.activation(w1[:, 0, :, :], w1_in, ACT.Copy)
            nc.scalar.activation(w2[:, 0, :, :], w2_in, ACT.Copy).then_inc(setup_act, 1)
            act_norm1(act, 0)
            act_norm2(act, 0)
            act_turned(act, 0)
            act_keys(act, 0)
            act_queries(act, 0, 0)
            act_norms(act, 0)
            act_values(act, 0, 0)
            act_beta(act, 0)
            act_keys_high(act, 0, 0)
            for r in range(G4):
                act_gram(act, 0, r)
                act_p_high(act, 0, 0, r)
            act_lanes(act, 0)
            act_norm1(act, 1)
            act_norm2(act, 1)
            act_turned(act, 1)
            act_chunk(act, 0, 0, d=False)
            with act.Fori(1, CHUNKS // 2 - 1) as p:
                act_chunk(act, p * 2 - 1, 1)
                act_chunk(act, p * 2, 0)
            act_chunk(act, CHUNKS - 3, 1)
            act_chunk(act, CHUNKS - 2, 0, t=False)
            act_chunk(act, CHUNKS - 1, 1, t=False, a=False)
            last = CHUNKS - 1
            act_layer_norm(act, last, 1)
            act_squares(act, last)
            act_turned_d(act, last, "h1")
            act_gelu(act, last, 0, range(4))
            act_gelu(act, last, 1, range(4))
            act_norm_y(act, last)
            act_turned_d(act, last, "h2")

        @block.tensor
        def _(pe):
            pe.wait_ge(setup_pool, 2)
            pe.wait_ge(w_loaded, 16 * (len(loads) + len(late)))
            nc.tensor.matmul(state[:, :], kjb[:, 0, 0, 0, :], kjb[:, 0, 0, 0:4, :].rearrange("p u n -> p (u n)"),
                             start=True, stop=True)
            for t in range(KT):
                for o in range(KT):
                    ins = nc.tensor.transpose(ps[4][:, (t * KT + o) * P:(t * KT + o + 1) * P],
                                              sq_in[:, 4, o, t * P:(t + 1) * P], ident[:, :])
            ins.then_inc(setup_pe, 1)
            pe.wait_ge(setup_dve, 3)
            pe_turn(pe, 0)
            pe_project(pe, 0, "k")
            pe_project(pe, 0, "q")
            pe_norms(pe, 0)
            pe_norms_back(pe, 0)
            pe_project(pe, 0, "v")
            pe_beta(pe, 0)
            for r in range(G4):
                pe_gram(pe, 0, r)
            pe_lanes(pe, 0)
            pe_turn(pe, 1)
            pe_chunk(pe, 0, 0, d=False)
            with pe.Fori(1, CHUNKS // 2 - 1) as p:
                pe_chunk(pe, p * 2 - 1, 1)
                pe_chunk(pe, p * 2, 0)
            pe_chunk(pe, CHUNKS - 3, 1)
            pe_chunk(pe, CHUNKS - 2, 0, t=False)
            pe_chunk(pe, CHUNKS - 1, 1, t=False, a=False)
            last = CHUNKS - 1
            pe_out_proj(pe, last, 0)
            pe_out_proj(pe, last, 1)
            pe_turn_d(pe, last, "h1", hs1_ready)
            for h in range(2):
                pe_w1(pe, last, h, range(4))
                pe_w2(pe, last, h, 0)
                pe_w2(pe, last, h, 1)
            pe_turn_d(pe, last, "h2", hs2_ready)
            pe_ffn(pe, last)

        @block.vector
        def _(dve):
            dve.wait_ge(w_loaded, 16 * (len(loads) + len(late)))
            dve.wait_ge(setup_pool, 2)
            V.tensor_scalar(beta_bias[:, :], beta_bias[:, :], 0.5, None, ALU.mult)
            V.memset(wb_pad.rearrange("p t h -> p (t h)"), 0.0).then_inc(dve_step, own.one())
            n = own.n
            dve.wait_ge(dve_step, n)
            for t in range(KT):
                for w in range(3):
                    V.tensor_scalar(sq_in[:, w, t, :], sq_in[:, w, t, :], ln_cols[:, 0, t:t + 1], None, ALU.mult)
                V.tensor_scalar(w1_in[:, t, :], w1_in[:, t, :], ln_cols[:, 1, t:t + 1], None, ALU.mult)
                src = wb_in[:, t, :].rearrange("p (g q h) -> p q g h", g=KT, q=Q4)
                dst = wb_pad[:, t, :].rearrange("p (q s) -> p q s", q=Q4)[:, :, 0:4].rearrange(
                    "p q (g h) -> p q g h", g=KT)
                ins = V.tensor_scalar(dst, src, ln_cols[:, 0, t:t + 1], None, ALU.mult)
            ins.then_inc(setup_dve, 1)
            dve.wait_ge(setup_pe, 1)
            for t in range(KT):
                ins = V.tensor_tensor(sq_in[:, 5, t, :], ps[4][:, t * D:(t + 1) * D], dish, ALU.add)
            ins.then_inc(setup_dve, 1)
            dve.wait_ge(setup_act, 1)
            for w in range(3):
                V.tensor_tensor(wqkv[:, 1, w, :, :], sq_in[:, w], wqkv[:, 0, w, :, :], ALU.subtract)
            V.tensor_tensor(wo[:, 1, :, :], sq_in[:, 3], wo[:, 0, :, :], ALU.subtract)
            V.tensor_tensor(wffn[:, 1, :, :], sq_in[:, 5], wffn[:, 0, :, :], ALU.subtract)
            V.tensor_tensor(bias_rows[:, 1, :, :], bias_in[:, :, :], bias_rows[:, 0, :, :], ALU.subtract)
            V.tensor_tensor(wbeta[:, 1, :, :], wb_pad, wbeta[:, 0, :, :], ALU.subtract)
            V.tensor_tensor(w1[:, 1, :, :], w1_in, w1[:, 0, :, :], ALU.subtract)
            V.tensor_tensor(w2[:, 1, :, :], w2_in, w2[:, 0, :, :], ALU.subtract).then_inc(setup_dve, 1)
            dve_a(dve, 0, 0, True)
            dve_norm1(dve, 1)
            dve_norm2(dve, 1)
            dve_norm3(dve, 1)
            dve_turned(dve, 1)
            dve_chunk(dve, 0, 0, d=False)
            dve.wait_ge(dve_step, own.n)
            dve.sem_clear(dve_step)
            own.n = 0
            with dve.Fori(1, CHUNKS // 2 - 1) as p:
                dve_chunk(dve, p * 2 - 1, 1)
                dve_chunk(dve, p * 2, 0)
                dve.wait_ge(dve_step, own.n)
                dve.sem_clear(dve_step)
                own.n = 0
            dve_chunk(dve, CHUNKS - 3, 1)
            dve_chunk(dve, CHUNKS - 2, 0, t=False)
            dve_chunk(dve, CHUNKS - 1, 1, t=False, a=False)
            last = CHUNKS - 1
            dve_x1(dve, last, 0)
            dve_x1(dve, last, 1)
            dve_residual(dve, last, 1)
            dve_rms(dve, last)
            dve_turned_d(dve, last, "h1")
            dve_gelu(dve, last, 0, range(4))
            dve_y(dve, last, 1, 0)
            dve_gelu(dve, last, 1, range(4))
            dve_y(dve, last, 1, 1)
            dve_y_stats(dve, last)
            dve_y_norm(dve, last, 1)
            dve_turned_d(dve, last, "h2")
            dve_out(dve, last, 1)


_INS = ['L0_attn_x', 'L0_attn_wq', 'L0_attn_bq', 'L0_attn_wk', 'L0_attn_bk', 'L0_attn_wv', 'L0_attn_bv',
        'L0_attn_wbeta', 'L0_attn_bbeta', 'L0_attn_wo', 'L0_attn_bo', 'L0_attn_w1', 'L0_attn_b1', 'L0_attn_w2',
        'L0_attn_b2', 'L0_attn_ln1_scale', 'L0_attn_ln2_scale', 'L0_ffn_weight', 'L0_ffn_disha']


def kernel(**inputs):
    import numpy as _np
    import concourse.bacc as _bacc
    from concourse import mybir as _mybir
    from concourse.bass_utils import run_bass_kernel_spmd as _run

    nc = _bacc.Bacc("TRN2", target_bir_lowering=False, num_devices=1)
    arrays, args = {}, {}
    for name in _INS:
        a = _np.ascontiguousarray(inputs[name])
        arrays[f"in_{name}_dram"] = a
        args[name] = nc.dram_tensor(f"in_{name}_dram", a.shape, _mybir.dt.from_np(a.dtype), kind="ExternalInput").ap()
    args["out"] = nc.dram_tensor("out_0_dram", (16, 512, 256), _mybir.dt.float32, kind="ExternalOutput").ap()
    gated_delta_block(nc, args)
    r = _run(nc, [arrays], core_ids=[0])
    return r.results[0]["out_0_dram"]
```

```python
from contextlib import ExitStack

import concourse.bass as bass
from concourse import mybir

F32 = mybir.dt.float32
F16 = mybir.dt.float16
ALU = mybir.AluOpType
ACT = mybir.ActivationFunctionType

P = 128
B, S, D, H, FF = 16, 512, 256, 16, 1024
E = D // H
C = 32
CHUNKS = S // C
G4 = 4
BG = B // G4
KT = D // P
MT = FF // P
Q4 = 4
HH = 2
UN = BG * KT * HH
LN = B * KT * HH
SEL = P // LN
Q2 = Q4 // SEL
RH = G4 // 2
HN = RH * P
EPS_LN, EPS_RMS, EPS_K = 1e-5, 1e-6, 1e-6
R64 = 64

assert LN * SEL == P and BG * C == P and Q4 * C == P


class Rota:

    def __init__(self, banks, filled, act_read, dve_read, phases, done):
        self.banks, self.sems = banks, (filled, act_read, dve_read)
        self.done = done
        self.at, self.per = {}, {}
        kinds = [list(phases.values())[-1][-1][1]] * len(banks)
        for ph, fills in phases.items():
            counts = [[0, 0, 0] for _ in banks]
            for i, (name, kind) in enumerate(fills):
                b = i % len(banks)
                self.at[name] = (ph, b, tuple(counts[b]), kinds[b], kind)
                counts[b][0] += 1
                counts[b][1] += "A" in kind
                counts[b][2] += "V" in kind
                kinds[b] = kind
            self.per[ph] = counts

    def bank(self, name):
        return self.banks[self.at[name][1]]

    def count(self, name, which, p):
        ph, b, before, _, _ = self.at[name]
        total = before[which]
        for other, times in self.done(ph, p):
            total = total + times * self.per[other][b][which]
        return total

    def on_free(self, name, p):
        _, b, _, last, _ = self.at[name]
        which = 1 if last[-1] == "A" else 2
        return self.sems[which][b], self.count(name, which, p)

    def on_filled(self, name, p):
        return self.sems[0][self.at[name][1]], self.count(name, 0, p) + 1

    def on_act(self, name, p):
        return self.sems[1][self.at[name][1]], self.count(name, 1, p) + 1

    def on_dve(self, name, p):
        return self.sems[2][self.at[name][1]], self.count(name, 2, p) + 1

    def filled(self, name):
        return self.sems[0][self.at[name][1]]

    def act_read(self, name):
        return self.sems[1][self.at[name][1]]

    def dve_read(self, name):
        return self.sems[2][self.at[name][1]]


class Steps:

    def __init__(self):
        self.n = 0

    def one(self):
        self.n += 1
        return 1


def gated_delta_block(nc, A):
    x, out = A["L0_attn_x"], A["out"]
    ctx = ExitStack()
    with ctx:
        def sb(name, shape, dt=F32):
            return ctx.enter_context(nc.sbuf_tensor(name, shape, dt))

        def sem(name):
            return ctx.enter_context(nc.semaphore(name))

        ident = sb("ident", [P, P])
        quad_col = sb("quad_col", [P, Q4])
        head_col = sb("head_col", [P, Q4, HH])
        par_col = sb("par_col", [P, HH])
        quad_mask = sb("quad_mask", [P, Q4, E], F16)
        head_mask = sb("head_mask", [P, 2 * Q4, E], F16)
        causal = sb("causal", [P, C])
        eps_ln, eps_rms = sb("eps_ln", [P, 1]), sb("eps_rms", [P, 1])
        ln_cols = sb("ln_cols", [P, 2, KT])
        qkv_bias = sb("qkv_bias", [P, 3, KT])
        beta_bias = sb("beta_bias", [P, 1])
        b1_cols = sb("b1_cols", [P, MT])
        bias_in = sb("bias_in", [1, 2, D])
        bias_rows = sb("bias_rows", [1, 2, 2, D], F16)
        ones_row = sb("ones_row", [1, P], F16)
        wqkv = sb("wqkv", [P, 2, 3, KT, D], F16)
        wbeta = sb("wbeta", [P, 2, KT, P], F16)
        wo = sb("wo", [P, 2, KT, D], F16)
        w1 = sb("w1", [P, 2, KT, FF], F16)
        w2 = sb("w2", [P, 2, MT, D], F16)
        wffn = sb("wffn", [P, 2, KT, D], F16)

        xa = sb("xa", [P, G4, D])
        bn6 = sb("bn6", [P, G4, 6])
        mv = sb("mv", [P, G4, 2])
        rstd = sb("rstd", [P, G4])
        sd1, ms, sd2, rr = (sb(n, [P, G4]) for n in ("sd1", "ms", "sd2", "rr"))
        hf = sb("hf", [P, 2, KT, B * C], F16)
        kq = sb("kq", [P, 2, 2, 2, KT, B * C], F16)
        vf = sb("vf", [P, 2, KT, B * C])
        kraw = sb("kraw", [P, KT, B * C])
        ksq = sb("ksq", [P, KT, B * C])
        sdk, rnk = sb("sdk", [P, KT, G4 * 2 * Q4]), sb("rnk", [P, KT, G4 * 2 * Q4])
        kblk = sb("kblk", [P, 2, KT * BG, Q4, C], F16)
        kqm = sb("kqm", [P, 2, 2, KT * BG, HH, 2, C], F16)
        beta_f = ksq[:, 0, :]
        beta_t = ksq[:, 1, :].rearrange("p (b t) -> p b t", b=B)
        beta_j = sb("beta_j", [P, LN])
        ptmp = sb("ptmp", [P, KT, BG * HH, C])
        pt = sb("pt", [P, 2, 2, KT, B, HH, C], F16)
        part = C * Q2 * C
        regI = sb("regI", [P, 4 * part])
        al = regI[:, 0:part].rearrange("p (i q j) -> p i q j", i=C, q=Q2)
        tl = regI[:, part:2 * part].rearrange("p (i q m) -> p i q m", i=C, q=Q2)
        gram = regI[:, 2 * part:3 * part].rearrange("p (l i) -> p l i", i=C)
        tt = regI[:, 3 * part:4 * part].bitcast(F16).rearrange("p (z l i) -> p z l i", z=2, i=C)
        bl = sb("bl", [P, Q2, C])
        prod = sb("prod", [P, Q2 * (C // 2) ** 2])
        st = sb("st", [P, 2, LN * E // HH], F16)
        sblk = sb("sblk", [P, 2, BG * KT, P], F16)
        rf, rj = sb("rf", [P, BG * KT, C]), sb("rj", [P, BG * KT, C])
        rr16 = sb("rr16", [P, 2, 2, BG * KT, C], F16)
        uc = sb("uc", [P, 2, 2, UN * E], F16)
        kj = sb("kj", [P, 2, BG * KT, C], F16)
        tblk = sb("tblk", [P, 2, UN, Q4, C], F16)
        bw = 2 * BG * KT * P

        def head_blocks(name):
            flat = sb(name, [P, HH * (bw + E)], F16)
            blocks = flat[:, 0:HH * bw].rearrange("p (h z u n) -> p h z u n", h=HH, z=2, n=P)
            diag = flat[:, :].rearrange("p (h w) -> p h w", h=HH)[:, :, 0:bw].rearrange("p h (v n) -> p h v n", n=P)
            return flat, blocks, diag

        kjb_flat, kjb, kjb_diag = head_blocks("kjb")
        ub_flat, ub, ub_diag = head_blocks("ub")
        of = sb("of", [P, 2, G4, KT, P], F16)
        xd = sb("xd", [P, 2, G4, D])
        rsd, nmr = sb("rsd", [P, 2, G4]), sb("nmr", [P, 2, G4])
        x1 = sb("x1", [P, G4, D])
        ssq, sdr, rdr = sb("ssq", [P, G4]), sb("sdr", [P, G4]), sb("rdr", [P, G4])
        hd = sb("hd", [P, 2, KT, B * C], F16)
        ge = sb("ge", [P, 2, 2, HN])
        gg = sb("gg", [P, 2, MT, HN], F16)
        mv2, sdy, rdy = sb("mv2", [P, G4, 2]), sb("sdy", [P, G4]), sb("rdy", [P, G4])
        bn6d = sb("bn6d", [P, G4, 6])

        ps = [ctx.enter_context(nc.psum_tensor(f"ps{i}", [P, 512], F32)) for i in range(8)]
        state, ubank, xbank = ps[0], ps[1], [ps[2], ps[3]]

        wa_loaded, wb_loaded = sem("wa_loaded"), sem("wb_loaded")
        setup_pool, setup_act = sem("setup_pool"), sem("setup_act")
        setup_dve, setup_pe, blocks_clear = sem("setup_dve"), sem("setup_pe"), sem("blocks_clear")
        setup_low = sem("setup_low")
        x_loaded, stats_ready, sd1_ready = sem("x_loaded"), sem("stats_ready"), sem("sd1_ready")
        ms_ready, sd2_ready, hs_ready = sem("ms_ready"), sem("sd2_ready"), sem("hs_ready")
        rn_ready, knhi_ready = sem("rn_ready"), sem("knhi_ready")
        kn_split, kblk_ready, beta_ready = sem("kn_split"), sem("kblk_ready"), sem("beta_ready")
        phi_ready, p_ready = sem("phi_ready"), sem("p_ready")
        tanh_ready, inv_ready = sem("tanh_ready"), sem("inv_ready")
        sh_ready, sblk_ready, ksqs_done = sem("sh_ready"), sem("sblk_ready"), sem("ksqs_done")
        rj_ready, rh_ready, r_ready = sem("rj_ready"), sem("rh_ready"), sem("r_ready")
        thi_ready, tlo_ready = sem("thi_ready"), sem("tlo_ready")
        u_filled, uh_ready, ublk_ready = sem("u_filled"), sem("uh_ready"), sem("ublk_ready")
        ds_done, o_filled, oh_ready, o_ready = sem("ds_done"), sem("o_filled"), sem("oh_ready"), sem("o_ready")
        xd_loaded, lnx_ready, ssq_ready = sem("xd_loaded"), sem("lnx_ready"), sem("ssq_ready")
        sdr_ready, hs1_ready = sem("sdr_ready"), sem("hs1_ready")
        gl_ready = [sem("gl_ready0"), sem("gl_ready1")]
        y_stats, sdy_ready = sem("y_stats"), sem("sdy_ready")
        hs2_ready, out_stored, xd_free = sem("hs2_ready"), sem("out_stored"), sem("xd_free")
        dve_step, pool_step = sem("dve_step"), sem("pool_step")
        pe_passed = sem("pe_passed")
        own, pown = Steps(), Steps()

        a_fills = [("hT0", "AV"), ("hT1", "AV"), ("k0", "A"), ("k1", "A"), ("q0", "AV"), ("q1", "AV"),
                   ("ks0", "A"), ("ks1", "A"), ("v0", "A"), ("v1", "A"), ("kr0", "V"), ("kr1", "V"), ("beta", "A")]
        a_fills += [(f"G{r}{g}", "AV") for r in range(G4) for g in range(KT)]
        a_fills += [(f"LA{i}", "A") for i in range(4)] + [("LB", "A")]
        d1_fills = [("x10", "V"), ("x11", "V"), ("h10", "AV"), ("h11", "AV")] + [(f"w10{m}", "A") for m in range(4)]
        t_fills = [(f"TF{i}", "AV") for i in range(4)]
        d2_fills = [("w20", "V")] + [(f"w11{m}", "A") for m in range(4)] + [("w21", "V")]
        d3_fills = [("h20", "AV"), ("h21", "AV"), ("ff0", "V"), ("ff1", "V")]

        def rota(tag, banks, phases, done):
            return Rota(banks, *[[sem(f"{tag}{w}{i}") for i in range(len(banks))]
                                 for w in ("_filled", "_act_read", "_dve_read")], phases, done)

        def floor0(v):
            return max(v, 0) if type(v) is int else v

        def capped(v, top):
            return min(v, top) if type(v) is int else v

        def before_cd(ph, c):
            if ph == "D3":
                return [("D3", c), ("D1", capped(c + 1, CHUNKS)), ("T", capped(c + 2, CHUNKS)),
                        ("D2", capped(c + 1, CHUNKS))]
            if ph == "D1":
                return [("D3", c), ("D1", c), ("T", capped(c + 1, CHUNKS)), ("D2", c)]
            if ph == "T":
                return [("D3", floor0(c - 1)), ("D1", c), ("T", c), ("D2", floor0(c - 1))]
            return [("D3", c), ("D1", c + 1), ("T", capped(c + 2, CHUNKS)), ("D2", c)]

        ra = rota("a", [ps[4], ps[5]], {"A": a_fills}, lambda ph, c: [("A", c)])
        rd = rota("d", [ps[6], ps[7]], {"D3": d3_fills, "D1": d1_fills, "T": t_fills, "D2": d2_fills}, before_cd)

        def tokens(ap, c, b):
            return ap.rearrange("(r b) t d -> b t r d", b=BG)[b, bass.ds(c * C, C), :, :]

        def mm3(out_, lh, rh, first, last=True, skip=False):
            passes = ((0, 0), (0, 1), (1, 0))
            for n, (a, b) in enumerate(passes):
                ins = nc.tensor.matmul(out_, lh(a), rh(b), start=first and n == 0,
                                       stop=last and n == 2, skip_group_check=skip)
            return ins

        def turn64(out_, in_, hp):
            if hp.start == 0:
                return nc.tensor.transpose(out_[hp], in_, ident[hp, hp])
            return nc.tensor.matmul(out_[hp], in_, ident[hp, hp], start=True, stop=True)

        def sp_load_a(sp, c, first=False):
            if not first:
                sp.wait_ge(*ra.on_filled("hT1", c - 1))
            for b in range(BG):
                sp.dma_start(xa[b * C:(b + 1) * C, :, :], tokens(x, c, b)).then_inc(x_loaded, 16)

        def sp_load_d(sp, d, k):
            for b in range(BG):
                sp.dma_start(xd[b * C:(b + 1) * C, k, :, :], tokens(x, d, b)).then_inc(xd_loaded, 16)

        def sp_store(sp, d, k):
            sp.wait_ge(*rd.on_dve("ff0", d))
            sp.wait_ge(*rd.on_dve("ff1", d))
            for b in range(BG):
                sp.dma_start(tokens(out, d, b), xd[b * C:(b + 1) * C, k, :, :]).then_inc(out_stored, 16)
            sp.wait_ge(out_stored, d * (16 * BG) + 16 * BG)
            sp.sem_inc(xd_free, 1)

        def pe_turn(pe, a):
            for h in range(2):
                n = f"hT{h}"
                pe.wait_ge(hs_ready, a * G4 + (h + 1) * RH)
                pe.wait_ge(*ra.on_free(n, a))
                for r in range(RH):
                    for t in range(KT):
                        s = (r * KT + t) * P
                        ins = nc.tensor.transpose(ra.bank(n)[:, s:s + P],
                                                  xa[:, h * RH + r, t * P:(t + 1) * P], ident[:, :])
                ins.then_inc(ra.filled(n), 1)

        def pe_project(pe, a, w):
            wi = "kqv".index(w)
            if w == "k":
                pe.wait_ge(*ra.on_dve("hT0", a))
                pe.wait_ge(*ra.on_dve("hT1", a))
            for g in range(KT):
                n = f"{w}{g}"
                pe.wait_ge(*ra.on_free(n, a))
                for t in range(KT):
                    ins = mm3(ra.bank(n)[:, :], lambda z: wqkv[:, z, wi, t, g * P:(g + 1) * P],
                              lambda z: hf[:, z, t, :], t == 0, t == KT - 1)
                ins.then_inc(ra.filled(n), 1)

        def pe_beta(pe, a):
            pe.wait_ge(*ra.on_free("beta", a))
            for t in range(KT):
                ins = mm3(ra.bank("beta")[:, :], lambda z: wbeta[:, z, t, :], lambda z: hf[:, z, t, :],
                          t == 0, t == KT - 1)
            ins.then_inc(ra.filled("beta"), 1)

        def pe_norms(pe, a):
            for g in range(KT):
                n = f"ks{g}"
                pe.wait_ge(*ra.on_act(f"k{g}", a))
                pe.wait_ge(*ra.on_free(n, a))
                for r in range(G4):
                    ins = nc.tensor.matmul(ra.bank(n)[:, r * 8:(r + 1) * 8], ksq[:, g, r * P:(r + 1) * P],
                                           head_col[:, :, :].rearrange("p q h -> p (q h)"), start=True, stop=True)
                ins.then_inc(ra.filled(n), 1)

        def pe_norms_back(pe, a):
            for g in range(KT):
                n = f"kr{g}"
                pe.wait_ge(rn_ready, a * KT + g + 1)
                pe.wait_ge(*ra.on_free(n, a))
                for r in range(G4):
                    ins = nc.tensor.transpose(ra.bank(n)[:, r * P:(r + 1) * P], ksq[:, g, r * P:(r + 1) * P],
                                              ident[:, :])
                ins.then_inc(ra.filled(n), 1)

        def pe_gram(pe, a, r):
            pe.wait_ge(kblk_ready, a * G4 + r + 1)
            for g in range(KT):
                n = f"G{r}{g}"
                pe.wait_ge(*ra.on_free(n, a))
                for b in range(BG):
                    u = g * BG + b
                    ins = mm3(ra.bank(n)[:, b * P:(b + 1) * P],
                              lambda z: kblk[:, z, u, :, :].rearrange("p q t -> p (q t)"),
                              lambda z: kqm[:, r % 2, z, u, :, :, :].rearrange("p h a t -> p (h a t)"), True)
                ins.then_inc(ra.filled(n), 1)

        def pe_lanes(pe, a, fills):
            pe.wait_ge(*ra.on_act(f"G{G4 - 1}{KT - 1}", a))
            pe.wait_ge(*ra.on_act(f"G{G4 - 1}{KT - 2}", a))
            for i8 in fills:
                n = f"LA{i8}"
                pe.wait_ge(*ra.on_free(n, a))
                pe.sem_inc(pe_passed, 1)
                for i in range(8):
                    for s in reversed(range(SEL)):
                        hp = slice(s * LN, (s + 1) * LN)
                        ins = turn64(ra.bank(n)[:, i * R64:(i + 1) * R64], gram[hp, :, i8 * 8 + i], hp)
                ins.then_inc(ra.filled(n), 1)

        def pe_lanes_beta(pe, a):
            pe.wait_ge(beta_ready, a + 1)
            pe.wait_ge(*ra.on_free("LB", a))
            pe.sem_inc(pe_passed, 1)
            for s in reversed(range(SEL)):
                hp = slice(s * LN, (s + 1) * LN)
                ins = turn64(ra.bank("LB")[:, 0:R64], beta_j[hp, :], hp)
            ins.then_inc(ra.filled("LB"), 1)

        def pe_t(pe, c):
            pe.wait_ge(inv_ready, c + 1)
            for i8 in range(4):
                n = f"TF{i8}"
                pe.wait_ge(*rd.on_free(n, c))
                pe.sem_inc(pe_passed, 1)
                for i in range(8):
                    for s in reversed(range(SEL)):
                        hp = slice(s * LN, (s + 1) * LN)
                        ins = turn64(rd.bank(n)[:, i * LN:(i + 1) * LN],
                                     tl[hp, i8 * 8 + i, :, :].rearrange("p q m -> p (q m)"), hp)
                ins.then_inc(rd.filled(n), 1)

        def pe_ksqs(pe, c, k, r):
            pe.wait_ge(sblk_ready, c * G4 + r + 1)
            pe.wait_ge(o_ready, floor0(c * G4 + r - 1))
            for b in range(BG):
                for g in range(KT):
                    u = b * KT + g
                    t0 = (r * BG + b) * C
                    ins = mm3(xbank[r % 2][:, u * 2 * C:(u + 1) * 2 * C], lambda z: sblk[:, z, u, :],
                              lambda z: kq[:, z, k, :, g, t0:t0 + C], u == 0, u == BG * KT - 1, True)
            ins.then_inc(ksqs_done, 1)

        def pe_u(pe, c, r):
            pe.wait_ge(thi_ready, c * G4 + r + 1)
            pe.wait_ge(tlo_ready, c * G4 + r + 1)
            pe.wait_ge(r_ready, c * G4 + r + 1)
            pe.wait_ge(ublk_ready, c * G4 + r)
            for b in range(BG):
                for g in range(KT):
                    for hh in range(HH):
                        u = (b * KT + g) * HH + hh
                        ins = mm3(ubank[:, u * E:(u + 1) * E],
                                  lambda z: tblk[:, z, u, :, :].rearrange("p q i -> p (q i)"),
                                  lambda z: rr16[:, z, r % 2, b * KT + g, hh * E:(hh + 1) * E], True)
            ins.then_inc(u_filled, 1)

        def pe_s_and_o(pe, c, k, r):
            pe.wait_ge(ublk_ready, c * G4 + r + 1)
            pe.wait_ge(p_ready, c * G4 + r + 1)
            for b in range(BG):
                for g in range(KT):
                    for hh in range(HH):
                        u = (b * KT + g) * HH + hh
                        s = ((r * BG + b) * KT + g) * E
                        ins = mm3(state[:, s:s + E], lambda z: kjb[:, hh, z, g * BG + b, :],
                                  lambda z: uc[:, r % 2, z, u * E:(u + 1) * E], False, True, True)
            ins.then_inc(ds_done, 1)
            for b in range(BG):
                for g in range(KT):
                    for hh in range(HH):
                        s = (b * KT + g) * 2 * C + C
                        ins = mm3(xbank[r % 2][:, s:s + C], lambda z: ub[:, hh, z, b * KT + g, :],
                                  lambda z: pt[:, z, k, g, r * BG + b, hh, :], False, True, True)
            ins.then_inc(o_filled, 1)

        def add_row(out_, which):
            nc.tensor.matmul(out_, ones_row[:, :], bias_rows[:, 0, which, :], start=True, stop=False)
            nc.tensor.matmul(out_, ones_row[:, :], bias_rows[:, 1, which, :], start=False, stop=False)

        def pe_out_proj(pe, d, h):
            n = f"x1{h}"
            pe.wait_ge(o_ready, d * G4 + (h + 1) * RH)
            pe.wait_ge(*rd.on_free(n, d))
            for r in range(RH):
                add_row(rd.bank(n)[:, r * D:(r + 1) * D], 0)
                for t in range(KT):
                    ins = mm3(rd.bank(n)[:, r * D:(r + 1) * D], lambda z: of[:, z, h * RH + r, t, :],
                              lambda z: wo[:, z, t, :], False, t == KT - 1)
            ins.then_inc(rd.filled(n), 1)

        def pe_turn_d(pe, d, tag, ready):
            for h in range(2):
                n = f"{tag}{h}"
                pe.wait_ge(ready, d * G4 + (h + 1) * RH)
                pe.wait_ge(*rd.on_free(n, d))
                for r in range(RH):
                    for t in range(KT):
                        s = (r * KT + t) * P
                        ins = nc.tensor.transpose(rd.bank(n)[:, s:s + P], x1[:, h * RH + r, t * P:(t + 1) * P],
                                                  ident[:, :])
                ins.then_inc(rd.filled(n), 1)

        def pe_w1(pe, d, h, fills):
            pe.wait_ge(*rd.on_dve(f"h1{h}", d))
            for m2 in fills:
                n = f"w1{h}{m2}"
                pe.wait_ge(*rd.on_free(n, d))
                for j in range(2):
                    m = m2 * 2 + j
                    for t in range(KT):
                        ins = mm3(rd.bank(n)[:, j * HN:(j + 1) * HN], lambda z: w1[:, z, t, m * P:(m + 1) * P],
                                  lambda z: hd[:, z, t, h * HN:(h + 1) * HN], t == 0, t == KT - 1)
                ins.then_inc(rd.filled(n), 1)

        def pe_w2(pe, d, h, r, half):
            n = f"w2{h}"
            if r == 0 and half == 0:
                pe.wait_ge(*rd.on_free(n, d))
                pe.wait_ge(gl_ready[h], d * 4 + 4)
            if half == 0:
                add_row(rd.bank(n)[:, r * D:(r + 1) * D], 1)
            for m in range(half * MT // 2, (half + 1) * MT // 2):
                ins = mm3(rd.bank(n)[:, r * D:(r + 1) * D], lambda z: gg[:, z, m, r * P:(r + 1) * P],
                          lambda z: w2[:, z, m, :], False, m == MT - 1)
            if r == RH - 1 and half == 1:
                ins.then_inc(rd.filled(n), 1)

        def pe_ffn(pe, d):
            for h in range(2):
                n = f"ff{h}"
                pe.wait_ge(*rd.on_dve(f"h2{h}", d))
                pe.wait_ge(*rd.on_free(n, d))
                for r in range(RH):
                    s = (h * RH + r) * P
                    for t in range(KT):
                        ins = mm3(rd.bank(n)[:, r * D:(r + 1) * D], lambda z: hd[:, z, t, s:s + P],
                                  lambda z: wffn[:, z, t, :], t == 0, t == KT - 1)
                ins.then_inc(rd.filled(n), 1)

        def pe_chunk(pe, c, k, t=True, a=True, d=True, o=True):
            if a:
                pe_project(pe, c + 1, "k")
                pe_project(pe, c + 1, "q")
            if o:
                pe_turn_d(pe, c - 2, "h2", hs2_ready)
            if a:
                pe_norms(pe, c + 1)
                pe_project(pe, c + 1, "v")
                pe_norms_back(pe, c + 1)
            if o:
                pe_ffn(pe, c - 2)
            if a:
                pe_beta(pe, c + 1)
            if d:
                pe_out_proj(pe, c - 1, 0)
                pe_out_proj(pe, c - 1, 1)
            if a:
                pe_gram(pe, c + 1, 0)
            if d:
                pe_turn_d(pe, c - 1, "h1", hs1_ready)
            if a:
                pe_gram(pe, c + 1, 1)
            if d:
                pe_w1(pe, c - 1, 0, [0])
            if a:
                pe_gram(pe, c + 1, 2)
            if d:
                pe_w1(pe, c - 1, 0, [1])
            if a:
                pe_gram(pe, c + 1, 3)
            if d:
                pe_w1(pe, c - 1, 0, [2])
            pe_ksqs(pe, c, k, 0)
            if d:
                pe_w1(pe, c - 1, 0, [3])
            if a:
                pe_lanes(pe, c + 1, [0, 1])
            pe_ksqs(pe, c, k, 1)
            if a:
                pe_lanes(pe, c + 1, [2, 3])
                pe_lanes_beta(pe, c + 1)
            pe_t(pe, c)
            if d:
                pe_w2(pe, c - 1, 0, 0, 0)
            pe_u(pe, c, 0)
            if d:
                pe_w2(pe, c - 1, 0, 0, 1)
            pe_s_and_o(pe, c, k, 0)
            pe_u(pe, c, 1)
            if d:
                pe_w2(pe, c - 1, 0, 1, 0)
            pe_ksqs(pe, c, k, 2)
            if d:
                pe_w2(pe, c - 1, 0, 1, 1)
            pe_s_and_o(pe, c, k, 1)
            pe_u(pe, c, 2)
            if d:
                pe_w1(pe, c - 1, 1, [0, 1])
            pe_ksqs(pe, c, k, 3)
            if d:
                pe_w1(pe, c - 1, 1, [2, 3])
            pe_s_and_o(pe, c, k, 2)
            pe_u(pe, c, 3)
            if d:
                pe_w2(pe, c - 1, 1, 0, 0)
                pe_w2(pe, c - 1, 1, 0, 1)
            pe_s_and_o(pe, c, k, 3)
            if t:
                pe_turn(pe, c + 2)
            if d:
                pe_w2(pe, c - 1, 1, 1, 0)
                pe_w2(pe, c - 1, 1, 1, 1)

        def row_halves(bank):
            return bank[:, :].rearrange("p (r t n) -> p t r n", r=RH, t=KT)

        def col_halves(tile, z, h):
            return tile[:, z, :, h * HN:(h + 1) * HN].rearrange("p t (r n) -> p t r n", r=RH)

        def act_norm1(act, a):
            act.wait_ge(stats_ready, a + 1)
            nc.scalar.activation(sd1[:, :], mv[:, :, 1], ACT.Sqrt, bias=eps_ln[:, 0:1]).then_inc(sd1_ready, 1)

        def act_norm2(act, a):
            act.wait_ge(ms_ready, a + 1)
            nc.scalar.activation(sd2[:, :], ms[:, :], ACT.Sqrt).then_inc(sd2_ready, 1)

        def act_turned(act, a):
            for h in range(2):
                n = f"hT{h}"
                act.wait_ge(*ra.on_filled(n, a))
                nc.scalar.activation(col_halves(hf, 0, h), row_halves(ra.bank(n)),
                                     ACT.Copy).then_inc(ra.act_read(n), 1)

        def act_keys(act, a):
            act.wait_ge(kn_split, a)
            for g in range(KT):
                n = f"k{g}"
                bias = qkv_bias[:, 0, g:g + 1]
                act.wait_ge(*ra.on_filled(n, a))
                nc.scalar.activation(kraw[:, g, :], ra.bank(n)[:, :], ACT.Identity, bias=bias)
                nc.scalar.activation(ksq[:, g, :], ra.bank(n)[:, :], ACT.Square,
                                     bias=bias).then_inc(ra.act_read(n), 1)

        def act_queries(act, a, k):
            for g in range(KT):
                n = f"q{g}"
                act.wait_ge(*ra.on_filled(n, a))
                nc.scalar.activation(kq[:, 0, k, 1, g, :], ra.bank(n)[:, :], ACT.Identity,
                                     bias=qkv_bias[:, 1, g:g + 1]).then_inc(ra.act_read(n), 1)

        def act_norms(act, a):
            for g in range(KT):
                n = f"ks{g}"
                act.wait_ge(*ra.on_filled(n, a))
                nc.scalar.activation(sdk[:, g, :], ra.bank(n)[:, 0:G4 * 8], ACT.Sqrt).then_inc(ra.act_read(n), 1)

        def act_values(act, a, k):
            for g in range(KT):
                n = f"v{g}"
                act.wait_ge(*ra.on_filled(n, a))
                nc.scalar.activation(vf[:, k, g, :], ra.bank(n)[:, :], ACT.Identity,
                                     bias=qkv_bias[:, 2, g:g + 1]).then_inc(ra.act_read(n), 1)

        def act_beta(act, a):
            act.wait_ge(*ra.on_filled("beta", a))
            act.wait_ge(beta_ready, a)
            nc.scalar.activation(beta_f[:, :], ra.bank("beta")[:, :], ACT.Identity, bias=beta_bias[:, 0:1],
                                 scale=0.5).then_inc(ra.act_read("beta"), 1)

        def act_tanh(act, a):
            act.wait_ge(*ra.on_act("beta", a))
            nc.scalar.activation(beta_f[:, :], beta_f[:, :], ACT.Tanh).then_inc(tanh_ready, 1)

        def act_keys_high(act, a, k):
            for g in range(KT):
                act.wait_ge(*ra.on_dve(f"kr{g}", a))
                nc.scalar.activation(kq[:, 0, k, 0, g, :], kraw[:, g, :], ACT.Copy).then_inc(knhi_ready, 1)

        def act_gram(act, a, r):
            for g in range(KT):
                n = f"G{r}{g}"
                act.wait_ge(*ra.on_filled(n, a))
                src = ra.bank(n)[:, :].rearrange("p (b h s) -> p b h s", b=BG, h=HH)[:, :, :, 0:C]
                dst = gram.rearrange("p (b g h) i -> p b g h i", b=B, g=KT)
                nc.scalar.activation(dst[:, r * BG:(r + 1) * BG, g, :, :], src,
                                     ACT.Copy).then_inc(ra.act_read(n), 1)

        def act_p_high(act, a, k, r):
            act.wait_ge(*ra.on_dve(f"G{r}0", a))
            act.wait_ge(*ra.on_dve(f"G{r}1", a))
            nc.scalar.activation(p_part(0, k, r), ptmp[:, :, :, :], ACT.Copy).then_inc(phi_ready, 1)

        def p_part(z, k, r):
            return pt[:, z, k, :, r * BG:(r + 1) * BG, :, :].rearrange("p g b h i -> p g (b h) i")

        def act_lanes(act, a):
            act.wait_ge(inv_ready, a)
            for i8 in range(4):
                n = f"LA{i8}"
                act.wait_ge(*ra.on_filled(n, a))
                nc.scalar.activation(al[:, i8 * 8:i8 * 8 + 8, :, :].rearrange("p i q j -> p (i q j)"),
                                     ra.bank(n)[:, :], ACT.Copy).then_inc(ra.act_read(n), 1)
            act.wait_ge(*ra.on_filled("LB", a))
            nc.scalar.activation(bl[:, :, :].rearrange("p q j -> p (q j)"), ra.bank("LB")[:, 0:R64],
                                 ACT.Copy).then_inc(ra.act_read("LB"), 1)

        def act_state(act, c):
            act.wait_ge(ds_done, c * G4)
            nc.scalar.activation(st[:, 0, :], state[:, :], ACT.Copy).then_inc(sh_ready, 1)

        def act_t(act, c):
            for i8 in range(4):
                n = f"TF{i8}"
                act.wait_ge(*rd.on_filled(n, c))
                nc.scalar.activation(tt[:, 0, :, i8 * 8:i8 * 8 + 8].rearrange("p l i -> p i l"),
                                     rd.bank(n)[:, :].rearrange("p (i l) -> p i l", i=8),
                                     ACT.Copy).then_inc(rd.act_read(n), 1)

        def act_t_blocks(act, c, r):
            act.wait_ge(u_filled, c * G4 + r)
            if r == 0:
                act.wait_ge(*rd.on_act("TF3", c))
            for q in range(Q4):
                ins = nc.scalar.activation(tblk[:, 0, :, q, :], tt[:, 0, r * UN:(r + 1) * UN, :], ACT.Copy,
                                           scale=quad_col[:, q:q + 1])
            ins.then_inc(thi_ready, 1)

        def act_r(act, c, r):
            act.wait_ge(rj_ready, c * G4 + r + 1)
            nc.scalar.activation(rr16[:, 0, r % 2, :, :], rj[:, :, :], ACT.Copy).then_inc(rh_ready, 1)

        def act_u(act, c, r):
            act.wait_ge(u_filled, c * G4 + r + 1)
            nc.scalar.activation(uc[:, r % 2, 0, :], ubank[:, 0:UN * E], ACT.Copy).then_inc(uh_ready, 1)

        def act_o(act, c, r, d):
            act.wait_ge(o_filled, c * G4 + r + 1)
            if d:
                act.wait_ge(*rd.on_filled(f"x1{r // RH}", c - 1))
            src = xbank[r % 2][:, :].rearrange("p (b g s) -> p g b s", b=BG, g=KT)[:, :, :, C:2 * C]
            dst = of[:, 0, r, :, :].rearrange("p g (b t) -> p g b t", b=BG)
            nc.scalar.activation(dst, src, ACT.Copy).then_inc(oh_ready, 1)

        def act_layer_norm(act, d, k):
            act.wait_ge(xd_loaded, d * (16 * BG) + 16 * BG)
            for r in range(G4):
                ins = nc.scalar.activation(x1[:, r, :], xd[:, k, r, :], ACT.Identity, bias=nmr[:, k, r:r + 1],
                                           scale=rsd[:, k, r:r + 1])
            ins.then_inc(lnx_ready, 1)

        def act_squares(act, d):
            for r in range(G4):
                act.wait_ge(*rd.on_dve(f"x1{r // RH}", d))
                nc.scalar.activation(ge[:, r // 2, r % 2, :], x1[:, r, :], ACT.Square,
                                     accum_out=ssq[:, r:r + 1]).then_inc(ssq_ready, 1)
            act.wait_ge(ssq_ready, (d + 1) * G4)
            nc.scalar.activation(sdr[:, :], ssq[:, :], ACT.Sqrt, bias=eps_rms[:, 0:1],
                                 scale=1.0 / D).then_inc(sdr_ready, 1)

        def act_turned_d(act, d, tag):
            for h in range(2):
                n = f"{tag}{h}"
                act.wait_ge(*rd.on_filled(n, d))
                nc.scalar.activation(col_halves(hd, 0, h), row_halves(rd.bank(n)),
                                     ACT.Copy).then_inc(rd.act_read(n), 1)

        def act_gelu(act, d, h, fills):
            for m2 in fills:
                n = f"w1{h}{m2}"
                act.wait_ge(*rd.on_filled(n, d))
                if m2 >= 2:
                    act.wait_ge(gl_ready[h], d * 4 + m2 - 1)
                elif h:
                    act.wait_ge(gl_ready[0], d * 4 + m2 + 3)
                for j in range(2):
                    m = m2 * 2 + j
                    nc.scalar.activation(ge[:, m2 % 2, j, :], rd.bank(n)[:, j * HN:(j + 1) * HN],
                                         ACT.Gelu_apprx_tanh, bias=b1_cols[:, m:m + 1])
                    ins = nc.scalar.activation(gg[:, 0, m, :], rd.bank(n)[:, j * HN:(j + 1) * HN],
                                               ACT.Gelu_apprx_tanh, bias=b1_cols[:, m:m + 1])
                ins.then_inc(rd.act_read(n), 1)

        def act_norm_y(act, d):
            act.wait_ge(y_stats, d + 1)
            nc.scalar.activation(sdy[:, :], mv2[:, :, 1], ACT.Sqrt, bias=eps_ln[:, 0:1]).then_inc(sdy_ready, 1)

        def act_chunk(act, c, k, t=True, a=True, d=True, o=True):
            act_state(act, c)
            if a:
                act_keys(act, c + 1)
            if o:
                act_norm_y(act, c - 2)
            if a:
                act_queries(act, c + 1, 1 - k)
            if o:
                act_turned_d(act, c - 2, "h2")
            if a:
                act_norms(act, c + 1)
                act_values(act, c + 1, 1 - k)
            if d:
                act_layer_norm(act, c - 1, 1 - k)
            if a:
                act_keys_high(act, c + 1, 1 - k)
                act_beta(act, c + 1)
            if d:
                act_squares(act, c - 1)
            if a:
                act_tanh(act, c + 1)
                act_gram(act, c + 1, 0)
            if d:
                act_turned_d(act, c - 1, "h1")
            if a:
                act_p_high(act, c + 1, 1 - k, 0)
                act_gram(act, c + 1, 1)
            if d:
                act_gelu(act, c - 1, 0, [0])
            if a:
                act_p_high(act, c + 1, 1 - k, 1)
                act_gram(act, c + 1, 2)
            if d:
                act_gelu(act, c - 1, 0, [1])
            if a:
                act_p_high(act, c + 1, 1 - k, 2)
                act_gram(act, c + 1, 3)
            if d:
                act_gelu(act, c - 1, 0, [2])
            if a:
                act_p_high(act, c + 1, 1 - k, 3)
            act_r(act, c, 0)
            if d:
                act_gelu(act, c - 1, 0, [3])
            if a:
                act_lanes(act, c + 1)
            act_r(act, c, 1)
            act_t(act, c)
            act_t_blocks(act, c, 0)
            act_u(act, c, 0)
            act_t_blocks(act, c, 1)
            act_o(act, c, 0, d)
            act_u(act, c, 1)
            act_t_blocks(act, c, 2)
            act_r(act, c, 2)
            act_o(act, c, 1, d)
            act_u(act, c, 2)
            if d:
                act_gelu(act, c - 1, 1, [0, 1])
            act_t_blocks(act, c, 3)
            act_r(act, c, 3)
            if d:
                act_gelu(act, c - 1, 1, [2, 3])
            if t:
                act_norm1(act, c + 2)
            act_o(act, c, 2, d)
            act_u(act, c, 3)
            if t:
                act_norm2(act, c + 2)
            act_o(act, c, 3, d)
            if t:
                act_turned(act, c + 2)

        V = nc.vector

        def dve_keep_norm(dve, n, k, d):
            if d:
                dve.wait_ge(lnx_ready, n - 1)
            V.tensor_copy(rsd[:, k, :], rstd[:, :])
            V.scalar_tensor_tensor(out=nmr[:, k, :], in0=mv[:, :, 0], scalar=-1.0, in1=rstd[:, :],
                                   op0=ALU.mult, op1=ALU.mult).then_inc(dve_step, own.one())
            dve.wait_ge(dve_step, own.n)

        def dve_norm1(dve, a):
            dve.wait_ge(x_loaded, a * (16 * BG) + 16 * BG)
            for r in range(G4):
                V.bn_stats(bn6[:, r, :], xa[:, r, :]).then_inc(dve_step, own.one())
            dve.wait_ge(dve_step, own.n)
            for r in range(G4):
                ins = V.bn_aggr(mv[:, r, :], bn6[:, r, :])
            ins.then_inc(stats_ready, 1)

        def dve_norm2(dve, a):
            dve.wait_ge(sd1_ready, a + 1)
            V.reciprocal(rstd[:, :], sd1[:, :]).then_inc(dve_step, own.one())
            dve.wait_ge(dve_step, own.n)
            V.tensor_tensor(ms[:, :], mv[:, :, 1], rstd[:, :], ALU.mult).then_inc(dve_step, own.one())
            dve.wait_ge(dve_step, own.n)
            V.tensor_tensor(ms[:, :], ms[:, :], rstd[:, :], ALU.mult).then_inc(dve_step, own.one())
            dve.wait_ge(dve_step, own.n)
            V.tensor_scalar(ms[:, :], ms[:, :], EPS_RMS, None, ALU.add).then_inc(ms_ready, 1)

        def dve_norm3(dve, a):
            dve.wait_ge(sd2_ready, a + 1)
            V.reciprocal(rr[:, :], sd2[:, :]).then_inc(dve_step, own.one())
            dve.wait_ge(dve_step, own.n)
            V.tensor_tensor(rr[:, :], rr[:, :], rstd[:, :], ALU.mult).then_inc(dve_step, own.one())
            dve.wait_ge(dve_step, own.n)
            for r in range(G4):
                V.tensor_scalar(xa[:, r, :], xa[:, r, :], mv[:, r, 0:1], rr[:, r:r + 1],
                                ALU.subtract, ALU.mult).then_inc(hs_ready, 1)

        def dve_turned(dve, a):
            for h in range(2):
                n = f"hT{h}"
                dve.wait_ge(*ra.on_act(n, a))
                V.tensor_tensor(col_halves(hf, 1, h), row_halves(ra.bank(n)), col_halves(hf, 0, h),
                                ALU.subtract).then_inc(ra.dve_read(n), 1)

        def dve_queries(dve, a, k):
            for g in range(KT):
                n = f"q{g}"
                dve.wait_ge(*ra.on_act(n, a))
                V.scalar_tensor_tensor(out=kq[:, 1, k, 1, g, :], in0=ra.bank(n)[:, :],
                                       scalar=qkv_bias[:, 1, g:g + 1], in1=kq[:, 0, k, 1, g, :],
                                       op0=ALU.add, op1=ALU.subtract).then_inc(ra.dve_read(n), 1)

        def dve_norms(dve, a):
            for g in range(KT):
                dve.wait_ge(*ra.on_act(f"ks{g}", a))
            V.tensor_scalar(sdk[:, :, :], sdk[:, :, :], EPS_K, None, ALU.add).then_inc(dve_step, own.one())
            dve.wait_ge(dve_step, own.n)
            V.reciprocal(rnk[:, :, :], sdk[:, :, :]).then_inc(dve_step, own.one())
            dve.wait_ge(dve_step, own.n)
            for g in range(KT):
                dst = ksq[:, g, :].rearrange("p (h e) -> p h e", e=E)
                V.tensor_copy(dst, rnk[:, g, :].unsqueeze(2).to_broadcast([P, G4 * 8, E])).then_inc(rn_ready, 1)

        def dve_beta(dve, a):
            dve.wait_ge(tanh_ready, a + 1)
            V.tensor_scalar(beta_f[:, :], beta_f[:, :], 0.5, 0.5, ALU.mult, ALU.add).then_inc(dve_step, own.one())
            dve.wait_ge(dve_step, own.n)
            V.transpose(beta_t[:, :, :].rearrange("p b t -> p (b t)"), beta_f[:, :]).then_inc(dve_step, own.one())
            dve.wait_ge(dve_step, own.n)
            V.tensor_copy(beta_j[:, :].rearrange("p (b g) -> p b g", g=KT * HH),
                          beta_t[:, :, 0:KT * HH]).then_inc(beta_ready, 1)

        def dve_keys(dve, a):
            for g in range(KT):
                n = f"kr{g}"
                dve.wait_ge(*ra.on_filled(n, a))
                V.tensor_tensor(kraw[:, g, :], kraw[:, g, :], ra.bank(n)[:, :], ALU.mult).then_inc(ra.dve_read(n), 1)

        def dve_keys_low(dve, a, k):
            dve.wait_ge(knhi_ready, a * KT + KT)
            V.tensor_tensor(kq[:, 1, k, 0, :, :], kraw[:, :, :], kq[:, 0, k, 0, :, :],
                            ALU.subtract).then_inc(kn_split, 1)
            dve.wait_ge(kn_split, a + 1)

        def dve_key_blocks(dve, a, k, r, first=False):
            if not (first and r < 2):
                dve.wait_ge(*ra.on_filled(f"G{(r - 2) % G4}1", a if r >= 2 else a - 1))
            for z in range(2):
                src = kq[:, z, k, :, :, r * P:(r + 1) * P].rearrange("p w g (b t) -> p w g b t", b=BG)
                for hh in range(HH):
                    V.tensor_scalar(kqm[:, r % 2, z, :, hh, :, :].rearrange("p (g b) w t -> p w g b t", g=KT), src,
                                    par_col[:, hh:hh + 1], None, ALU.mult)
            if not (first and r == 0):
                dve.wait_ge(*ra.on_filled(f"G{(r - 1) % G4}1", a if r else a - 1))
            src = kq[:, :, k, 0, :, r * P:(r + 1) * P].rearrange("p z g (b t) -> p z g b t", b=BG)
            for q in range(Q4):
                ins = V.tensor_scalar(kblk[:, :, :, q, :].rearrange("p z (g b) t -> p z g b t", g=KT), src,
                                      quad_col[:, q:q + 1], None, ALU.mult)
            ins.then_inc(kblk_ready, 1)

        def dve_p_mask(dve, a, r):
            dve.wait_ge(p_ready, a * G4 + r)
            for g in range(KT):
                n = f"G{r}{g}"
                dve.wait_ge(*ra.on_act(n, a))
                src = ra.bank(n)[:, :].rearrange("p (u s) -> p u s", s=2 * C)[:, :, C:2 * C]
                V.tensor_tensor(ptmp[:, g, :, :], src, causal[:, :].unsqueeze(1).to_broadcast([P, BG * HH, C]),
                                ALU.mult).then_inc(ra.dve_read(n), 1)

        def dve_p_low(dve, a, k, r):
            dve.wait_ge(phi_ready, a * G4 + r + 1)
            V.tensor_tensor(p_part(1, k, r), ptmp[:, :, :, :], p_part(0, k, r), ALU.subtract).then_inc(p_ready, 1)

        def dve_state(dve, c):
            dve.wait_ge(sh_ready, c + 1)
            V.tensor_tensor(st[:, 1, :], state[:, :], st[:, 0, :], ALU.subtract).then_inc(dve_step, own.one())
            dve.wait_ge(dve_step, own.n)

        def dve_s_blocks(dve, c, r):
            dve.wait_ge(ksqs_done, c * G4 + r)
            for z in range(2):
                src = st[:, z, r * P:(r + 1) * P].rearrange("p (u d) -> p u d", d=E)
                ins = V.tensor_tensor(sblk[:, z, :, :].rearrange("p u (h d) -> p u h d", d=E),
                                      src.unsqueeze(2).to_broadcast([P, BG * KT, 2 * Q4, E]),
                                      head_mask[:, :, :].unsqueeze(1).to_broadcast([P, BG * KT, 2 * Q4, E]),
                                      ALU.mult)
            ins.then_inc(sblk_ready, 1)

        def dve_t(dve, c):
            for i8 in range(4):
                n = f"TF{i8}"
                dve.wait_ge(*rd.on_act(n, c))
                i8s = slice(i8 * 8, i8 * 8 + 8)
                V.tensor_tensor(tt[:, 1, :, i8s].rearrange("p l i -> p i l"),
                                rd.bank(n)[:, :].rearrange("p (i l) -> p i l", i=8),
                                tt[:, 0, :, i8s].rearrange("p l i -> p i l"), ALU.subtract).then_inc(rd.dve_read(n), 1)
            dve.wait_ge(*rd.on_dve("TF2", c))
            dve.wait_ge(*rd.on_dve("TF3", c))

        def dve_t_blocks(dve, c, r):
            dve.wait_ge(u_filled, c * G4 + r)
            for q in range(Q4):
                ins = V.tensor_scalar(tblk[:, 1, :, q, :], tt[:, 1, r * UN:(r + 1) * UN, :], quad_col[:, q:q + 1],
                                      None, ALU.mult)
            ins.then_inc(tlo_ready, 1)

        def dve_r(dve, c, k, r):
            dve.wait_ge(ksqs_done, c * G4 + r + 1)
            src = xbank[r % 2][:, :].rearrange("p (b g s) -> p b g s", b=BG, g=KT)[:, :, :, 0:C]
            val = vf[:, k, :, r * P:(r + 1) * P].rearrange("p g (b t) -> p b g t", b=BG)
            V.tensor_tensor(rf[:, :, :].rearrange("p (b g) t -> p b g t", b=BG), val, src,
                            ALU.subtract).then_inc(dve_step, own.one())
            dve.wait_ge(dve_step, own.n)
            V.transpose(rj[:, :, :].rearrange("p u t -> p (u t)"),
                        rf[:, :, :].rearrange("p u t -> p (u t)")).then_inc(rj_ready, 1)

        def dve_r_low(dve, c, r):
            dve.wait_ge(rh_ready, c * G4 + r + 1)
            V.tensor_tensor(rr16[:, 1, r % 2, :, :], rj[:, :, :], rr16[:, 0, r % 2, :, :],
                            ALU.subtract).then_inc(r_ready, 1)

        def dve_kj(dve, c, k, r):
            dve.wait_ge(ds_done, c * G4 + r)
            for z in range(2):
                V.transpose(kj[:, z, :, :].rearrange("p (g b) t -> p g (b t)", g=KT),
                            kq[:, z, k, 0, :, r * P:(r + 1) * P]).then_inc(dve_step, own.one())
            dve.wait_ge(dve_step, own.n)
            for q in range(Q4):
                V.tensor_scalar(kjb_diag[:, :, :, q * C:q * C + E],
                                kj[:, :, :, :].rearrange("p z u (h e) -> p h (z u) e", h=HH),
                                quad_col[:, q:q + 1], None, ALU.mult)

        def dve_u(dve, c, r):
            dve.wait_ge(uh_ready, c * G4 + r + 1)
            V.tensor_tensor(uc[:, r % 2, 1, :], ubank[:, 0:UN * E], uc[:, r % 2, 0, :],
                            ALU.subtract).then_inc(dve_step, own.one())
            dve.wait_ge(o_filled, c * G4 + r)
            dve.wait_ge(dve_step, own.n)
            src = uc[:, r % 2, :, :].rearrange("p z (u h d) -> p h (z u) d", h=HH, d=E)
            for q in range(Q4):
                ins = V.tensor_scalar(ub_diag[:, :, :, q * C:q * C + E], src, quad_col[:, q:q + 1], None, ALU.mult)
            ins.then_inc(ublk_ready, 1)

        def dve_o(dve, c, r):
            dve.wait_ge(oh_ready, c * G4 + r + 1)
            src = xbank[r % 2][:, :].rearrange("p (b g s) -> p g b s", b=BG, g=KT)[:, :, :, C:2 * C]
            dst = of[:, :, r, :, :].rearrange("p z g (b t) -> p z g b t", b=BG)
            V.tensor_tensor(dst[:, 1], src, dst[:, 0], ALU.subtract).then_inc(o_ready, 1)

        def dve_x1(dve, d, h):
            dve.wait_ge(lnx_ready, d + 1)
            n = f"x1{h}"
            dve.wait_ge(*rd.on_filled(n, d))
            rs = slice(h * RH, (h + 1) * RH)
            V.tensor_tensor(x1[:, rs, :], rd.bank(n)[:, :].rearrange("p (r d) -> p r d", r=RH), x1[:, rs, :],
                            ALU.add).then_inc(rd.dve_read(n), 1)

        def dve_residual(dve, d, k):
            dve.wait_ge(*rd.on_dve("x10", d))
            dve.wait_ge(*rd.on_dve("x11", d))
            V.tensor_tensor(xd[:, k, :, :], xd[:, k, :, :], x1[:, :, :], ALU.add).then_inc(dve_step, own.one())

        def dve_rms(dve, d):
            dve.wait_ge(sdr_ready, d + 1)
            V.reciprocal(rdr[:, :], sdr[:, :]).then_inc(dve_step, own.one())
            dve.wait_ge(dve_step, own.n)
            for r in range(G4):
                V.tensor_scalar(x1[:, r, :], x1[:, r, :], rdr[:, r:r + 1], None, ALU.mult).then_inc(hs1_ready, 1)

        def dve_turned_d(dve, d, tag):
            for h in range(2):
                n = f"{tag}{h}"
                dve.wait_ge(*rd.on_act(n, d))
                V.tensor_tensor(col_halves(hd, 1, h), row_halves(rd.bank(n)), col_halves(hd, 0, h),
                                ALU.subtract).then_inc(rd.dve_read(n), 1)

        def dve_gelu(dve, d, fills):
            for m2 in fills:
                dve.wait_ge(*rd.on_act(f"w11{m2}", d))
                ms2 = slice(m2 * 2, m2 * 2 + 2)
                V.tensor_tensor(gg[:, 1, ms2, :], ge[:, m2 % 2, :, :], gg[:, 0, ms2, :],
                                ALU.subtract).then_inc(gl_ready[1], 1)

        def dve_y(dve, d, k, h):
            n = f"w2{h}"
            dve.wait_ge(*rd.on_filled(n, d))
            rs = slice(h * RH, (h + 1) * RH)
            V.tensor_tensor(xd[:, k, rs, :], rd.bank(n)[:, :].rearrange("p (r d) -> p r d", r=RH), xd[:, k, rs, :],
                            ALU.add).then_inc(rd.dve_read(n), 1)
            dve.wait_ge(*rd.on_dve(n, d))
            for r in range(h * RH, (h + 1) * RH):
                V.bn_stats(bn6d[:, r, :], xd[:, k, r, :]).then_inc(dve_step, own.one())

        def dve_y_stats(dve, d):
            dve.wait_ge(dve_step, own.n)
            for r in range(G4):
                ins = V.bn_aggr(mv2[:, r, :], bn6d[:, r, :])
            ins.then_inc(y_stats, 1)

        def dve_y_norm(dve, d, k):
            dve.wait_ge(sdy_ready, d + 1)
            V.reciprocal(rdy[:, :], sdy[:, :]).then_inc(dve_step, own.one())
            dve.wait_ge(dve_step, own.n)
            for r in range(G4):
                V.tensor_scalar(x1[:, r, :], xd[:, k, r, :], mv2[:, r, 0:1], rdy[:, r:r + 1],
                                ALU.subtract, ALU.mult).then_inc(hs2_ready, 1)

        def dve_out(dve, d, k):
            for h in range(2):
                n = f"ff{h}"
                dve.wait_ge(*rd.on_filled(n, d))
                rs = slice(h * RH, (h + 1) * RH)
                V.tensor_tensor(xd[:, k, rs, :], rd.bank(n)[:, :].rearrange("p (r d) -> p r d", r=RH), xd[:, k, rs, :],
                                ALU.add).then_inc(rd.dve_read(n), 1)

        def dve_chunk(dve, c, k, t=True, a=True, d=True, o=True):
            n, l = c + 1, c - 1
            dve_state(dve, c)
            dve_s_blocks(dve, c, 0)
            if o:
                dve_y_norm(dve, c - 2, k)
            if a:
                dve_queries(dve, n, 1 - k)
            if o:
                dve_turned_d(dve, c - 2, "h2")
            if a:
                dve_norms(dve, n)
                dve_keys(dve, n)
            if o:
                dve_out(dve, c - 2, k)
            if a:
                dve_keys_low(dve, n, 1 - k)
                dve_key_blocks(dve, n, 1 - k, 0)
            if d:
                dve_x1(dve, l, 0)
                dve_x1(dve, l, 1)
                dve_residual(dve, l, 1 - k)
                dve_rms(dve, l)
            if a:
                dve_key_blocks(dve, n, 1 - k, 1)
                dve_p_mask(dve, n, 0)
            if d:
                dve_turned_d(dve, l, "h1")
            if not d:
                dve_p_low(dve, n, 1 - k, 0)
            if a:
                dve_key_blocks(dve, n, 1 - k, 2)
                dve_p_mask(dve, n, 1)
            if not d:
                dve_p_low(dve, n, 1 - k, 1)
            if a:
                dve_key_blocks(dve, n, 1 - k, 3)
                dve_p_mask(dve, n, 2)
                dve_keep_norm(dve, n, 1 - k, d)
                dve_beta(dve, n)
            if not d:
                dve_p_low(dve, n, 1 - k, 2)
            if a:
                dve_p_mask(dve, n, 3)
            if not d:
                dve_p_low(dve, n, 1 - k, 3)
            dve_r(dve, c, k, 0)
            dve_s_blocks(dve, c, 1)
            dve_r_low(dve, c, 0)
            dve_kj(dve, c, k, 0)
            dve_r(dve, c, k, 1)
            dve_r_low(dve, c, 1)
            dve_t(dve, c)
            dve_t_blocks(dve, c, 0)
            dve_s_blocks(dve, c, 2)
            dve_u(dve, c, 0)
            dve_t_blocks(dve, c, 1)
            dve_kj(dve, c, k, 1)
            dve_o(dve, c, 0)
            dve_u(dve, c, 1)
            dve_t_blocks(dve, c, 2)
            dve_r(dve, c, k, 2)
            dve_r_low(dve, c, 2)
            dve_s_blocks(dve, c, 3)
            if d:
                dve_y(dve, l, 1 - k, 0)
            dve_kj(dve, c, k, 2)
            dve_o(dve, c, 1)
            dve_u(dve, c, 2)
            dve_t_blocks(dve, c, 3)
            if d:
                dve_gelu(dve, l, [0, 1])
            if t:
                dve_norm1(dve, c + 2)
            dve_r(dve, c, k, 3)
            dve_r_low(dve, c, 3)
            if d:
                dve_gelu(dve, l, [2, 3])
            if t:
                dve_norm2(dve, c + 2)
            dve_kj(dve, c, k, 3)
            dve_o(dve, c, 2)
            dve_u(dve, c, 3)
            if t:
                dve_norm3(dve, c + 2)
            dve_o(dve, c, 3)
            if t:
                dve_turned(dve, c + 2)
            if d:
                dve_y(dve, l, 1 - k, 1)
                dve_y_stats(dve, l)

        def pool_p_low(pool, a, k, r):
            pool.wait_ge(phi_ready, a * G4 + r + 1)
            nc.gpsimd.tensor_tensor(p_part(1, k, r), ptmp[:, :, :, :], p_part(0, k, r),
                                    ALU.subtract).then_inc(p_ready, 1)

        def pool_gelu(pool, d, m2):
            pool.wait_ge(*rd.on_act(f"w10{m2}", d))
            ms2 = slice(m2 * 2, m2 * 2 + 2)
            nc.gpsimd.tensor_tensor(gg[:, 1, ms2, :], ge[:, m2 % 2, :, :], gg[:, 0, ms2, :],
                                    ALU.subtract).then_inc(gl_ready[0], 1)

        def pool_chunk(pool, c, k, a=True, d=True):
            for r in range(G4):
                if a and d:
                    pool_p_low(pool, c + 1, 1 - k, r)
                if d:
                    pool_gelu(pool, c - 1, r)
            if a:
                pool_inverse(pool, c + 1)

        def pool_inverse(pool, a, first=False):
            g = nc.gpsimd
            if not first:
                pool.wait_ge(*rd.on_filled("TF2", a - 1))
                pool.wait_ge(*rd.on_filled("TF3", a - 1))
            pool.wait_ge(*ra.on_act("LA3", a))
            pool.wait_ge(*ra.on_act("LA2", a))
            pool.wait_ge(*ra.on_act("LB", a))
            beta_i = bl[:, :, :].rearrange("p q i -> p i q")
            g.tensor_tensor(al[:, :, :, :], al[:, :, :, :], beta_i.unsqueeze(3).to_broadcast([P, C, Q2, C]),
                            ALU.mult).then_inc(pool_step, pown.one())
            g.memset(tl[:, :, :, :].rearrange("p i q m -> p (i q m)"), 0.0).then_inc(pool_step, pown.one())
            pool.wait_ge(pool_step, pown.n)
            tflat = tl[:, :, :, :].rearrange("p i q m -> p (i q m)")
            for q in range(Q2):
                diag = tflat[:, q * C:q * C + (C - 1) * (Q2 * C + 1) + 1:Q2 * C + 1]
                ins = g.tensor_copy(diag, bl[:, q, :])
            ins.then_inc(pool_step, pown.one())
            pool.wait_ge(pool_step, pown.n)
            for j in range(C - 1):
                rows, cols = C - 1 - j, j + 1
                tmp = prod[:, 0:rows * Q2 * cols].rearrange("p (i q m) -> p i q m", i=rows, q=Q2)
                shape = [P, rows, Q2, cols]
                g.tensor_tensor(tmp, al[:, j + 1:C, :, j:j + 1].to_broadcast(shape),
                                tl[:, j:j + 1, :, 0:cols].to_broadcast(shape), ALU.mult).then_inc(pool_step, pown.one())
                pool.wait_ge(pool_step, pown.n)
                dst = tl[:, j + 1:C, :, 0:cols]
                last = g.tensor_tensor(dst, dst, tmp, ALU.subtract)
                if j == C - 2:
                    last.then_inc(inv_ready, 1)
                else:
                    last.then_inc(pool_step, pown.one())
                    pool.wait_ge(pool_step, pown.n)

        stage_a, stage_t = regI[:, 0:2 * part], regI[:, 2 * part:4 * part]
        w1_in = stage_a[:, 0:KT * FF].rearrange("p (t n) -> p t n", t=KT)
        w2_in = stage_a[:, KT * FF:KT * FF + MT * D].rearrange("p (t n) -> p t n", t=MT)
        sq_in = stage_t[:, 0:6 * KT * D].rearrange("p (w t n) -> p w t n", w=6, t=KT)
        dish = stage_t[:, 3072:3072 + D]
        wb_in = stage_t[:, 3328:3328 + KT * H].rearrange("p (t h) -> p t h", t=KT)
        wb_pad = stage_t[:, 3584:3584 + KT * P].rearrange("p (t h) -> p t h", t=KT)

        def rows(ap):
            return ap.rearrange("(t p) n -> p t n", p=P)

        loads_a = [(sq_in[:, 0], rows(A["L0_attn_wk"])), (sq_in[:, 1], rows(A["L0_attn_wq"])),
                   (sq_in[:, 2], rows(A["L0_attn_wv"])), (wb_in, rows(A["L0_attn_wbeta"])),
                   (ln_cols[:, 0, :], A["L0_attn_ln1_scale"].rearrange("(t p) -> p t", p=P))]
        for i, w in enumerate(("bk", "bq", "bv")):
            loads_a.append((qkv_bias[:, i, :], A[f"L0_attn_{w}"].rearrange("(t p) -> p t", p=P)))
        loads_b = [(sq_in[:, 4], rows(A["L0_ffn_weight"])), (w1_in, rows(A["L0_attn_w1"])),
                   (w2_in, rows(A["L0_attn_w2"])), (sq_in[:, 3], rows(A["L0_attn_wo"])),
                   (dish[0:R64, :], A["L0_ffn_disha"]), (dish[R64:P, :], A["L0_ffn_disha"]),
                   (ln_cols[:, 1, :], A["L0_attn_ln2_scale"].rearrange("(t p) -> p t", p=P)),
                   (b1_cols[:, :], A["L0_attn_b1"].rearrange("(t p) -> p t", p=P)),
                   (bias_in[:, 0, :], A["L0_attn_bo"].rearrange("(a n) -> a n", a=1)),
                   (bias_in[:, 1, :], A["L0_attn_b2"].rearrange("(a n) -> a n", a=1))]
        bb = A["L0_attn_bbeta"].rearrange("(g q h a) -> g q h a", g=KT, q=Q4, a=1)
        late = [(beta_bias[q * C + g * HH:q * C + (g + 1) * HH, :], bb[g, q]) for g in range(KT) for q in range(Q4)]

        block = ctx.enter_context(nc.Block())

        @block.sync
        def _(sp):
            sp_load_a(sp, 0, True)
            for dst, src in loads_a:
                sp.dma_start(dst, src, allow_slow_non_contiguous=True).then_inc(wa_loaded, 16)
            sp.wait_ge(setup_pool, 1)
            for dst, src in late:
                sp.dma_start(dst, src).then_inc(wa_loaded, 16)
            for dst, src in loads_b:
                sp.dma_start(dst, src, allow_slow_non_contiguous=True).then_inc(wb_loaded, 16)
            sp_load_a(sp, 1)
            sp_load_d(sp, 0, 0)
            sp_load_d(sp, 1, 1)
            sp_load_a(sp, 2)
            sp_load_a(sp, 3)
            with sp.Fori(1, CHUNKS // 2 - 1) as p:
                for c, k in ((p * 2, 0), (p * 2 + 1, 1)):
                    sp_store(sp, c - 2, k)
                    sp_load_d(sp, c, k)
                    sp_load_a(sp, c + 2)
            for c in range(CHUNKS - 2, CHUNKS + 2):
                sp_store(sp, c - 2, c % 2)
                if c < CHUNKS:
                    sp_load_d(sp, c, c % 2)

        @block.gpsimd
        def _(pool):
            g = nc.gpsimd
            g.memset(beta_bias[:, :], 0.0).then_inc(setup_pool, 1)
            for t in (ident, quad_col, head_col, causal):
                t2 = t[:, :] if len(t.shape) == 2 else t[:, :, :]
                ins = g.memset(t2, 0.0 if t is ident else 1.0)
            for t, v in ((eps_ln, EPS_LN), (eps_rms, EPS_RMS), (ones_row, 1.0)):
                ins = g.memset(t[:, :], v)
            ins.then_inc(pool_step, pown.one())
            pool.wait_ge(pool_step, pown.n)
            g.affine_select(out=ident[:, :], in_=ident[:, :], compare_op=ALU.not_equal, fill=1.0, base=0,
                                 pattern=[[-1, P]], channel_multiplier=1).then_inc(pool_step, pown.one())
            pool.wait_ge(pool_step, pown.n)
            hc = head_col[:, :, :].rearrange("p q h -> p (q h)")
            g.affine_select(out=hc, in_=hc, compare_op=ALU.is_ge, fill=0.0, base=0,
                                 pattern=[[-E, 8]], channel_multiplier=1).then_inc(pool_step, pown.one())
            pool.wait_ge(pool_step, pown.n)
            g.affine_select(out=hc, in_=hc, compare_op=ALU.is_ge, fill=0.0, base=E - 1,
                                 pattern=[[E, 8]], channel_multiplier=-1).then_inc(pool_step, pown.one())
            pool.wait_ge(pool_step, pown.n)
            g.affine_select(out=quad_col[:, :], in_=quad_col[:, :], compare_op=ALU.is_ge, fill=0.0, base=0,
                                 pattern=[[-C, Q4]], channel_multiplier=1).then_inc(pool_step, pown.one())
            pool.wait_ge(pool_step, pown.n)
            g.affine_select(out=quad_col[:, :], in_=quad_col[:, :], compare_op=ALU.is_ge, fill=0.0,
                                 base=C - 1, pattern=[[C, Q4]], channel_multiplier=-1).then_inc(pool_step, pown.one())
            pool.wait_ge(pool_step, pown.n)
            for q in range(Q4):
                c = causal[q * C:(q + 1) * C, :]
                g.affine_select(out=c, in_=c, compare_op=ALU.is_ge, fill=0.0, base=0,
                                     pattern=[[1, C]], channel_multiplier=-1).then_inc(pool_step, pown.one())
                pool.wait_ge(pool_step, pown.n)
            g.tensor_tensor(par_col[:, :], head_col[:, 0, :], head_col[:, 1, :], ALU.add).then_inc(pool_step, pown.one())
            for q in range(2, Q4):
                pool.wait_ge(pool_step, pown.n)
                g.tensor_tensor(par_col[:, :], par_col[:, :], head_col[:, q, :],
                                ALU.add).then_inc(pool_step, pown.one())
            hb = hc.unsqueeze(2).to_broadcast([P, 8, E])
            g.tensor_copy(head_mask[:, :, :], hb)
            g.tensor_copy(quad_mask[:, :, :], quad_col[:, :].unsqueeze(2).to_broadcast([P, Q4, E])
                          ).then_inc(setup_pool, 1)
            pool.wait_ge(setup_act, 2)
            pool.wait_ge(setup_dve, 3)
            g.tensor_tensor(wo[:, 1, :, :], sq_in[:, 3], wo[:, 0, :, :], ALU.subtract)
            g.tensor_tensor(wffn[:, 1, :, :], sq_in[:, 5], wffn[:, 0, :, :], ALU.subtract)
            g.tensor_tensor(bias_rows[:, 1, :, :], bias_in[:, :, :], bias_rows[:, 0, :, :], ALU.subtract)
            pool.wait_ge(setup_act, 3)
            g.tensor_tensor(w1[:, 1, :, :], w1_in, w1[:, 0, :, :], ALU.subtract)
            pool.wait_ge(setup_act, 4)
            g.tensor_tensor(w2[:, 1, :, :], w2_in, w2[:, 0, :, :], ALU.subtract).then_inc(setup_low, 1)
            pool.wait_ge(setup_low, 1)
            pool.wait_ge(pool_step, pown.n)
            pool.sem_clear(pool_step)
            pown.n = 0
            for r in range(G4):
                pool_p_low(pool, 0, 0, r)
            pool_inverse(pool, 0, True)
            pool_chunk(pool, 0, 0, d=False)
            pool_chunk(pool, 1, 1)
            pool.wait_ge(pool_step, pown.n)
            pool.sem_clear(pool_step)
            pown.n = 0
            with pool.Fori(1, CHUNKS // 2 - 1) as p:
                pool_chunk(pool, p * 2, 0)
                pool_chunk(pool, p * 2 + 1, 1)
                pool.wait_ge(pool_step, pown.n)
                pool.sem_clear(pool_step)
                pown.n = 0
            pool_chunk(pool, CHUNKS - 2, 0)
            pool_chunk(pool, CHUNKS - 1, 1, a=False)
            for m2 in range(4):
                pool_gelu(pool, CHUNKS - 1, m2)

        @block.scalar
        def _(act):
            act_norm1(act, 0)
            act_norm2(act, 0)
            act.wait_ge(setup_dve, 1)
            for w in range(3):
                nc.scalar.activation(wqkv[:, 0, w, :, :], sq_in[:, w], ACT.Copy)
            nc.scalar.activation(wbeta[:, 0, :, :], wb_pad, ACT.Copy).then_inc(setup_act, 1)
            act_turned(act, 0)
            act_keys(act, 0)
            act_queries(act, 0, 0)
            act_norms(act, 0)
            act.wait_ge(setup_dve, 3)
            nc.scalar.activation(wo[:, 0, :, :], sq_in[:, 3], ACT.Copy)
            nc.scalar.activation(wffn[:, 0, :, :], sq_in[:, 5], ACT.Copy)
            nc.scalar.activation(bias_rows[:, 0, :, :], bias_in[:, :, :], ACT.Copy).then_inc(setup_act, 1)
            act_values(act, 0, 0)
            nc.scalar.activation(w1[:, 0, :, :], w1_in, ACT.Copy).then_inc(setup_act, 1)
            nc.scalar.activation(w2[:, 0, :, :], w2_in, ACT.Copy).then_inc(setup_act, 1)
            act_beta(act, 0)
            act_tanh(act, 0)
            act_keys_high(act, 0, 0)
            for r in range(G4):
                act_gram(act, 0, r)
                act_p_high(act, 0, 0, r)
            act_lanes(act, 0)
            act_norm1(act, 1)
            act_norm2(act, 1)
            act_turned(act, 1)
            act_chunk(act, 0, 0, d=False, o=False)
            act_chunk(act, 1, 1, o=False)
            with act.Fori(1, CHUNKS // 2 - 1) as p:
                act_chunk(act, p * 2, 0)
                act_chunk(act, p * 2 + 1, 1)
            act_chunk(act, CHUNKS - 2, 0, t=False)
            act_chunk(act, CHUNKS - 1, 1, t=False, a=False)
            last = CHUNKS - 1
            act_norm_y(act, last - 1)
            act_turned_d(act, last - 1, "h2")
            act_layer_norm(act, last, 1)
            act_squares(act, last)
            act_turned_d(act, last, "h1")
            act_gelu(act, last, 0, range(4))
            act_gelu(act, last, 1, range(4))
            act_norm_y(act, last)
            act_turned_d(act, last, "h2")

        @block.tensor
        def _(pe):
            pe.wait_ge(setup_pool, 2)
            pe.wait_ge(blocks_clear, 1)
            nc.tensor.matmul(state[:, :], kjb[:, 0, 0, 0, :], kjb[:, 0, 0, 0:4, :].rearrange("p u n -> p (u n)"),
                             start=True, stop=True)
            pe_turn(pe, 0)
            pe.wait_ge(setup_dve, 2)
            pe_project(pe, 0, "k")
            pe_project(pe, 0, "q")
            pe.wait_ge(wb_loaded, 16 * len(loads_b))
            for t in range(KT):
                for o in range(KT):
                    ins = nc.tensor.transpose(ps[6][:, (t * KT + o) * P:(t * KT + o + 1) * P],
                                              sq_in[:, 4, o, t * P:(t + 1) * P], ident[:, :])
            ins.then_inc(setup_pe, 1)
            pe_norms(pe, 0)
            pe_project(pe, 0, "v")
            pe_norms_back(pe, 0)
            pe_beta(pe, 0)
            for r in range(G4):
                pe_gram(pe, 0, r)
            pe_lanes(pe, 0, range(4))
            pe_lanes_beta(pe, 0)
            pe_turn(pe, 1)
            pe_chunk(pe, 0, 0, d=False, o=False)
            pe_chunk(pe, 1, 1, o=False)
            with pe.Fori(1, CHUNKS // 2 - 1) as p:
                pe_chunk(pe, p * 2, 0)
                pe_chunk(pe, p * 2 + 1, 1)
            pe_chunk(pe, CHUNKS - 2, 0, t=False)
            pe_chunk(pe, CHUNKS - 1, 1, t=False, a=False)
            last = CHUNKS - 1
            pe_turn_d(pe, last - 1, "h2", hs2_ready)
            pe_ffn(pe, last - 1)
            pe_out_proj(pe, last, 0)
            pe_out_proj(pe, last, 1)
            pe_turn_d(pe, last, "h1", hs1_ready)
            for h in range(2):
                pe_w1(pe, last, h, range(4))
                for r in range(RH):
                    pe_w2(pe, last, h, r, 0)
                    pe_w2(pe, last, h, r, 1)
            pe_turn_d(pe, last, "h2", hs2_ready)
            pe_ffn(pe, last)

        @block.vector
        def _(dve):
            V.memset(wb_pad.rearrange("p t h -> p (t h)"), 0.0).then_inc(dve_step, own.one())
            V.memset(kjb_flat[:, :], 0.0)
            V.memset(ub_flat[:, :], 0.0).then_inc(blocks_clear, 1)
            dve.wait_ge(blocks_clear, 1)
            dve.wait_ge(setup_pool, 2)
            dve_norm1(dve, 0)
            dve.wait_ge(wa_loaded, 16 * (len(loads_a) + len(late)))
            V.tensor_scalar(beta_bias[:, :], beta_bias[:, :], 0.5, None, ALU.mult)
            for t in range(KT):
                for w in range(3):
                    V.tensor_scalar(sq_in[:, w, t, :], sq_in[:, w, t, :], ln_cols[:, 0, t:t + 1], None, ALU.mult)
                src = wb_in[:, t, :].rearrange("p (g q h) -> p q g h", g=KT, q=Q4)
                dst = wb_pad[:, t, :].rearrange("p (q s) -> p q s", q=Q4)[:, :, 0:4].rearrange(
                    "p q (g h) -> p q g h", g=KT)
                ins = V.tensor_scalar(dst, src, ln_cols[:, 0, t:t + 1], None, ALU.mult)
            ins.then_inc(setup_dve, 1)
            dve_norm2(dve, 0)
            dve_norm3(dve, 0)
            dve_keep_norm(dve, 0, 0, False)
            dve.wait_ge(setup_act, 1)
            for w in range(3):
                V.tensor_tensor(wqkv[:, 1, w, :, :], sq_in[:, w], wqkv[:, 0, w, :, :], ALU.subtract)
            V.tensor_tensor(wbeta[:, 1, :, :], wb_pad, wbeta[:, 0, :, :], ALU.subtract).then_inc(setup_dve, 1)
            dve_turned(dve, 0)
            dve_queries(dve, 0, 0)
            dve.wait_ge(wb_loaded, 16 * len(loads_b))
            for t in range(KT):
                V.tensor_scalar(w1_in[:, t, :], w1_in[:, t, :], ln_cols[:, 1, t:t + 1], None, ALU.mult)
            dve.wait_ge(setup_pe, 1)
            for t in range(KT):
                ins = V.tensor_tensor(sq_in[:, 5, t, :], ps[6][:, t * D:(t + 1) * D], dish, ALU.add)
            ins.then_inc(setup_dve, 1)
            dve_norms(dve, 0)
            dve_keys(dve, 0)
            dve_beta(dve, 0)
            dve_keys_low(dve, 0, 0)
            for r in range(G4):
                dve_key_blocks(dve, 0, 0, r, True)
                dve_p_mask(dve, 0, r)
            dve_norm1(dve, 1)
            dve_norm2(dve, 1)
            dve_norm3(dve, 1)
            dve_turned(dve, 1)
            dve_chunk(dve, 0, 0, d=False, o=False)
            dve_chunk(dve, 1, 1, o=False)
            dve.wait_ge(dve_step, own.n)
            dve.sem_clear(dve_step)
            own.n = 0
            with dve.Fori(1, CHUNKS // 2 - 1) as p:
                dve_chunk(dve, p * 2, 0)
                dve_chunk(dve, p * 2 + 1, 1)
                dve.wait_ge(dve_step, own.n)
                dve.sem_clear(dve_step)
                own.n = 0
            dve_chunk(dve, CHUNKS - 2, 0, t=False)
            dve_chunk(dve, CHUNKS - 1, 1, t=False, a=False)
            last = CHUNKS - 1
            dve_y_norm(dve, last - 1, 0)
            dve_turned_d(dve, last - 1, "h2")
            dve_out(dve, last - 1, 0)
            dve_x1(dve, last, 0)
            dve_x1(dve, last, 1)
            dve_residual(dve, last, 1)
            dve_rms(dve, last)
            dve_turned_d(dve, last, "h1")
            dve_y(dve, last, 1, 0)
            dve_gelu(dve, last, range(4))
            dve_y(dve, last, 1, 1)
            dve_y_stats(dve, last)
            dve_y_norm(dve, last, 1)
            dve_turned_d(dve, last, "h2")
            dve_out(dve, last, 1)


_INS = ['L0_attn_x', 'L0_attn_wq', 'L0_attn_bq', 'L0_attn_wk', 'L0_attn_bk', 'L0_attn_wv', 'L0_attn_bv',
        'L0_attn_wbeta', 'L0_attn_bbeta', 'L0_attn_wo', 'L0_attn_bo', 'L0_attn_w1', 'L0_attn_b1', 'L0_attn_w2',
        'L0_attn_b2', 'L0_attn_ln1_scale', 'L0_attn_ln2_scale', 'L0_ffn_weight', 'L0_ffn_disha']


def kernel(**inputs):
    import numpy as _np
    import concourse.bacc as _bacc
    from concourse import mybir as _mybir
    from concourse.bass_utils import run_bass_kernel_spmd as _run

    nc = _bacc.Bacc("TRN2", target_bir_lowering=False, num_devices=1)
    arrays, args = {}, {}
    for name in _INS:
        a = _np.ascontiguousarray(inputs[name])
        arrays[f"in_{name}_dram"] = a
        args[name] = nc.dram_tensor(f"in_{name}_dram", a.shape, _mybir.dt.from_np(a.dtype), kind="ExternalInput").ap()
    args["out"] = nc.dram_tensor("out_0_dram", (16, 512, 256), _mybir.dt.float32, kind="ExternalOutput").ap()
    gated_delta_block(nc, args)
    r = _run(nc, [arrays], core_ids=[0])
    return r.results[0]["out_0_dram"]
```
